# Optimizing a Trainium2 kernel written in Bass

```python
import numpy as np
import jax
import jax.numpy as jnp

def _softmax(x, axis=-1):
    return jax.nn.softmax(x, axis=axis)

def _gelu(x):
    return jax.nn.gelu(x, approximate=True)

def _silu(x):
    return jax.nn.silu(x)

def _sigmoid(x):
    return jax.nn.sigmoid(x)

def _layernorm(x, axis=-1, eps=1e-05):
    m = jnp.mean(x, axis=axis, keepdims=True)
    v = jnp.var(x, axis=axis, keepdims=True)
    return (x - m) / jnp.sqrt(v + eps)

def _scatter_add(tgt, idx, src, axis=0):
    return tgt.at[idx].add(src)

def _segment_sum(src, seg, n):
    return jax.ops.segment_sum(src, seg, n)
kernel_name = 'mk_seq_postln_d1_jaxref_r8_444841'

def setup_inputs(seed: int=0):
    np.random.seed(seed)
    _w = jnp.asarray

    def _L0_attn_setup():
        import jax, jax.numpy as jnp
        import numpy as np
        D_MODEL = 128
        D_STATE = 16
        BATCH = 2
        SEQ = 256
        key = jax.random.key(seed)
        k1, k2, k3, k4, k5 = jax.random.split(key, 5)
        x = jax.random.normal(k1, (BATCH, SEQ, D_MODEL), dtype=jnp.float32)
        log_A_diag = jax.random.normal(k2, (D_MODEL, D_STATE), dtype=jnp.float32)
        B_w = jax.random.normal(k3, (D_STATE, D_MODEL), dtype=jnp.float32) / np.sqrt(D_MODEL)
        C_w = jax.random.normal(k4, (D_MODEL, D_STATE), dtype=jnp.float32) / np.sqrt(D_STATE)
        D_vec = jax.random.normal(k5, (D_MODEL,), dtype=jnp.float32)
        return {'x': x, 'log_A_diag': log_A_diag, 'B_w': B_w, 'C_w': C_w, 'D_vec': D_vec}
    _L0_attn_in = _L0_attn_setup()

    def _L0_ffn_setup():
        import jax, jax.numpy as jnp
        import numpy as np
        EPS = 1e-05

        def _layernorm(x, w, b):
            mu = jnp.mean(x, axis=-1, keepdims=True)
            var = jnp.mean((x - mu) ** 2, axis=-1, keepdims=True)
            return (x - mu) * jax.lax.rsqrt(var + EPS) * w + b

        def _rope_tables(T, D, base=10000.0):
            inv_freq = 1.0 / base ** (jnp.arange(0, D, 2, dtype=jnp.float32) / D)
            t = jnp.arange(T, dtype=jnp.float32)
            freqs = jnp.einsum('i,j->ij', t, inv_freq)
            emb = jnp.concatenate([freqs, freqs], axis=-1)
            return (jnp.cos(emb), jnp.sin(emb))

        def _rotate_half(x):
            x1, x2 = (x[..., :x.shape[-1] // 2], x[..., x.shape[-1] // 2:])
            return jnp.concatenate([-x2, x1], axis=-1)

        def _attn(x, ln_w, ln_b, conv_w, attn_w, proj_w, n_head):
            B, T, C = x.shape
            D = C // n_head
            h = _layernorm(x, ln_w, ln_b)
            hc = jnp.transpose(h, (0, 2, 1))
            hc = jnp.pad(hc, ((0, 0), (0, 0), (2, 0)))
            hc = jax.lax.conv_general_dilated(hc, conv_w, window_strides=(1,), padding='VALID', dimension_numbers=('NCH', 'OIH', 'NCH'), feature_group_count=C)
            h = jnp.transpose(hc, (0, 2, 1))
            qkv = h @ attn_w
            q, k, v = jnp.split(qkv, 3, axis=-1)
            q = q.reshape(B, T, n_head, D)
            k = k.reshape(B, T, n_head, D)
            v = v.reshape(B, T, n_head, D)
            cos, sin = _rope_tables(T, D)
            cos = cos[None, :, None, :]
            sin = sin[None, :, None, :]
            q = q * cos + _rotate_half(q) * sin
            k = k * cos + _rotate_half(k) * sin
            scores = jnp.einsum('bqhd,bkhd->bhqk', q, k) / jnp.sqrt(jnp.float32(D))
            causal = jnp.tril(jnp.ones((T, T), dtype=bool))
            scores = jnp.where(causal, scores, jnp.float32(-1e+30))
            p = jax.nn.softmax(scores, axis=-1)
            y = jnp.einsum('bhqk,bkhd->bqhd', p, v).reshape(B, T, C)
            return y @ proj_w

        def _moe(x, ln_w, ln_b, router_w, expert_wv, expert_proj):
            h = _layernorm(x, ln_w, ln_b)
            logits = h @ router_w
            expert_idx = jnp.argmax(logits, axis=-1)
            E = router_w.shape[-1]
            out = jnp.zeros_like(x)
            for e in range(E):
                gv = h @ expert_wv[e]
                gate_raw, value = jnp.split(gv, 2, axis=-1)
                y = gate_raw * jax.nn.sigmoid(gate_raw) * value @ expert_proj[e]
                out = out + jnp.where((expert_idx == e)[..., None], y, 0.0)
            return out
        C, H, E, B, T = (128, 16, 4, 4, 128)
        Dff = 4 * C
        key = jax.random.key(seed)
        ks = jax.random.split(key, 8)
        s = 0.02
        return {'x': jax.random.normal(ks[0], (B, T, C), dtype=jnp.float32), 'ln1_w': jnp.ones((C,), jnp.float32), 'ln1_b': jnp.zeros((C,), jnp.float32), 'ln2_w': jnp.ones((C,), jnp.float32), 'ln2_b': jnp.zeros((C,), jnp.float32), 'conv_w': jax.random.normal(ks[1], (C, 1, 3), dtype=jnp.float32) * 0.1, 'attn_w': jax.random.normal(ks[2], (C, 3 * C), dtype=jnp.float32) * s, 'proj_w': jax.random.normal(ks[3], (C, C), dtype=jnp.float32) * s, 'router_w': jax.random.normal(ks[4], (C, E), dtype=jnp.float32) * s, 'expert_wv': jax.random.normal(ks[5], (E, C, 2 * Dff), dtype=jnp.float32) * s, 'expert_proj': jax.random.normal(ks[6], (E, Dff, C), dtype=jnp.float32) * s}
    _L0_ffn_in = _L0_ffn_setup()
    _d = {'L0_attn_x': _L0_attn_in['x'], 'L0_attn_log_A_diag': _L0_attn_in['log_A_diag'], 'L0_attn_B_w': _L0_attn_in['B_w'], 'L0_attn_C_w': _L0_attn_in['C_w'], 'L0_attn_D_vec': _L0_attn_in['D_vec'], 'L0_ffn_ln1_w': _L0_ffn_in['ln1_w'], 'L0_ffn_ln1_b': _L0_ffn_in['ln1_b'], 'L0_ffn_ln2_w': _L0_ffn_in['ln2_w'], 'L0_ffn_ln2_b': _L0_ffn_in['ln2_b'], 'L0_ffn_conv_w': _L0_ffn_in['conv_w'], 'L0_ffn_attn_w': _L0_ffn_in['attn_w'], 'L0_ffn_proj_w': _L0_ffn_in['proj_w'], 'L0_ffn_router_w': _L0_ffn_in['router_w'], 'L0_ffn_expert_wv': _L0_ffn_in['expert_wv'], 'L0_ffn_expert_proj': _L0_ffn_in['expert_proj']}
    _x0 = _d['L0_attn_x']
    _d['L0_attn_x'] = jax.random.normal(jax.random.fold_in(jax.random.key(seed), 1), (4, 1024, 128), dtype=_x0.dtype)
    del _x0
    return _d

def reference(L0_attn_x, L0_attn_log_A_diag, L0_attn_B_w, L0_attn_C_w, L0_attn_D_vec, L0_ffn_ln1_w, L0_ffn_ln1_b, L0_ffn_ln2_w, L0_ffn_ln2_b, L0_ffn_conv_w, L0_ffn_attn_w, L0_ffn_proj_w, L0_ffn_router_w, L0_ffn_expert_wv, L0_ffn_expert_proj):

    def _L0_attn_ref(x, log_A_diag, B_w, C_w, D_vec):
        import jax, jax.numpy as jnp
        import numpy as np
        D_MODEL = 128
        D_STATE = 16
        BATCH = 2
        SEQ = 256
        B, L, D = x.shape
        pad = 2 * L
        A_bar = jnp.exp(-jnp.exp(log_A_diag))
        B_t = jnp.einsum('bld,sd->bls', x, B_w)
        k_idx = jnp.arange(L, dtype=x.dtype)
        kernel = A_bar[..., None] ** k_idx
        kernel_fft = jnp.fft.rfft(kernel, n=pad, axis=-1)
        B_fft = jnp.fft.rfft(B_t.transpose(0, 2, 1), n=pad, axis=-1)
        conv_fft = kernel_fft[None] * B_fft[:, None]
        conv = jnp.fft.irfft(conv_fft, n=pad, axis=-1)[..., :L]
        y = jnp.einsum('bdsl,ds->bld', conv, C_w)
        y = y + D_vec[None, None, :] * x
        return y

    def _L0_ffn_ref(x, ln1_w, ln1_b, ln2_w, ln2_b, conv_w, attn_w, proj_w, router_w, expert_wv, expert_proj):
        import jax, jax.numpy as jnp
        import numpy as np
        EPS = 1e-05

        def _layernorm(x, w, b):
            mu = jnp.mean(x, axis=-1, keepdims=True)
            var = jnp.mean((x - mu) ** 2, axis=-1, keepdims=True)
            return (x - mu) * jax.lax.rsqrt(var + EPS) * w + b

        def _rope_tables(T, D, base=10000.0):
            inv_freq = 1.0 / base ** (jnp.arange(0, D, 2, dtype=jnp.float32) / D)
            t = jnp.arange(T, dtype=jnp.float32)
            freqs = jnp.einsum('i,j->ij', t, inv_freq)
            emb = jnp.concatenate([freqs, freqs], axis=-1)
            return (jnp.cos(emb), jnp.sin(emb))

        def _rotate_half(x):
            x1, x2 = (x[..., :x.shape[-1] // 2], x[..., x.shape[-1] // 2:])
            return jnp.concatenate([-x2, x1], axis=-1)

        def _attn(x, ln_w, ln_b, conv_w, attn_w, proj_w, n_head):
            B, T, C = x.shape
            D = C // n_head
            h = _layernorm(x, ln_w, ln_b)
            hc = jnp.transpose(h, (0, 2, 1))
            hc = jnp.pad(hc, ((0, 0), (0, 0), (2, 0)))
            hc = jax.lax.conv_general_dilated(hc, conv_w, window_strides=(1,), padding='VALID', dimension_numbers=('NCH', 'OIH', 'NCH'), feature_group_count=C)
            h = jnp.transpose(hc, (0, 2, 1))
            qkv = h @ attn_w
            q, k, v = jnp.split(qkv, 3, axis=-1)
            q = q.reshape(B, T, n_head, D)
            k = k.reshape(B, T, n_head, D)
            v = v.reshape(B, T, n_head, D)
            cos, sin = _rope_tables(T, D)
            cos = cos[None, :, None, :]
            sin = sin[None, :, None, :]
            q = q * cos + _rotate_half(q) * sin
            k = k * cos + _rotate_half(k) * sin
            scores = jnp.einsum('bqhd,bkhd->bhqk', q, k) / jnp.sqrt(jnp.float32(D))
            causal = jnp.tril(jnp.ones((T, T), dtype=bool))
            scores = jnp.where(causal, scores, jnp.float32(-1e+30))
            p = jax.nn.softmax(scores, axis=-1)
            y = jnp.einsum('bhqk,bkhd->bqhd', p, v).reshape(B, T, C)
            return y @ proj_w

        def _moe(x, ln_w, ln_b, router_w, expert_wv, expert_proj):
            h = _layernorm(x, ln_w, ln_b)
            logits = h @ router_w
            expert_idx = jnp.argmax(logits, axis=-1)
            E = router_w.shape[-1]
            out = jnp.zeros_like(x)
            for e in range(E):
                gv = h @ expert_wv[e]
                gate_raw, value = jnp.split(gv, 2, axis=-1)
                y = gate_raw * jax.nn.sigmoid(gate_raw) * value @ expert_proj[e]
                out = out + jnp.where((expert_idx == e)[..., None], y, 0.0)
            return out
        n_head = 16
        x = x + _attn(x, ln1_w, ln1_b, conv_w, attn_w, proj_w, n_head)
        x = x + _moe(x, ln2_w, ln2_b, router_w, expert_wv, expert_proj)
        return x
    x = L0_attn_x
    x = _layernorm(x + _L0_attn_ref(x, L0_attn_log_A_diag, L0_attn_B_w, L0_attn_C_w, L0_attn_D_vec), axis=-1)
    x = _layernorm(x + _L0_ffn_ref(x, L0_ffn_ln1_w, L0_ffn_ln1_b, L0_ffn_ln2_w, L0_ffn_ln2_b, L0_ffn_conv_w, L0_ffn_attn_w, L0_ffn_proj_w, L0_ffn_router_w, L0_ffn_expert_wv, L0_ffn_expert_proj), axis=-1)
    return x

_drawn_inputs = setup_inputs


def setup_inputs(seed=0):
    import zlib

    import numpy as np

    out = dict(_drawn_inputs(seed))
    spreads = {'L0_ffn_ln1_w': (1.0, 0.6),
     'L0_ffn_ln1_b': (0.0, 0.8),
     'L0_ffn_ln2_w': (1.0, 0.6),
     'L0_ffn_ln2_b': (0.0, 0.8)}
    factors = {'L0_ffn_conv_w': 8.0,
     'L0_ffn_attn_w': 8.0,
     'L0_ffn_proj_w': 8.0,
     'L0_ffn_router_w': 8.0,
     'L0_ffn_expert_wv': 8.0,
     'L0_ffn_expert_proj': 8.0}
    for name, (base, spread) in spreads.items():
        noise = np.random.default_rng([zlib.crc32(name.encode()), seed]).standard_normal(out[name].shape)
        drawn = base * np.exp(spread * noise) if base else spread * noise
        out[name] = jnp.asarray(drawn.astype(out[name].dtype))
    for name, factor in factors.items():
        out[name] = (out[name] * factor).astype(out[name].dtype)
    return out
```

```python
from contextlib import ExitStack

import numpy as np
import concourse.bass as bass
from concourse import mybir

F32 = mybir.dt.float32
BF16 = mybir.dt.bfloat16
ALU = mybir.AluOpType
ACT = mybir.ActivationFunctionType
AX_X = mybir.AxisListType.X

P = 128
NB = 4
T = 1024
D = 128
S = 16
CH = 8
G = D * S // P
NH = 16
HD = 8
HG = 4
KT = T // P
NE = 4
DFF = 512
FT = DFF // P
EPS = 1e-5
MASKED = -1e30
RATE_MAX = 1e4
SCALE = float(1.0 / np.sqrt(np.float32(HD)))
VC = 9
VW = 32

C_IDENT, C_MASKQ, C_MASKK = 0, P, 2 * P
C_COS, C_SIN = 3 * P, 3 * P + T
C_DS = C_SIN + T
C_DD = C_DS + S
C_PU = C_DD + 8
C_PI = C_PU + 1
C_CM = C_PI + CH
C_ALL = C_CM + CH


def constants():
    c = np.zeros((P, C_ALL), np.float32)
    n = np.arange(P)
    c[:, C_IDENT:C_IDENT + P] = np.eye(P)
    c[:, C_MASKQ:C_MASKQ + P] = np.where(n[None, :] > n[:, None], MASKED, 0.0)
    c[:, C_MASKK:C_MASKK + P] = np.where(n[:, None] > n[None, :], MASKED, 0.0)
    inv = (1.0 / 10000.0 ** (np.arange(0, HD, 2, dtype=np.float32) / HD)).astype(np.float32)
    freq = np.arange(T, dtype=np.float32)[None, :] * inv[:, None]
    d = n % HD
    c[:, C_COS:C_COS + T] = np.cos(freq)[d % (HD // 2)]
    c[:, C_SIN:C_SIN + T] = np.sin(freq)[d % (HD // 2)] * np.where(d < HD // 2, -1, 1)[:, None]
    c[:, C_DS:C_DS + S] = (n % S)[:, None] == np.arange(S)[None, :]
    c[:, C_DD:C_DD + 8] = (n // S)[:, None] == np.arange(8)[None, :]
    j = n // S
    r = np.arange(CH)
    c[:, C_PU] = -(CH - 1 - j)
    c[:, C_PI:C_PI + CH] = -np.maximum(r[None, :] - j[:, None], 0)
    c[:, C_CM:C_CM + CH] = r[None, :] >= j[:, None]
    return c


class Chain:

    def __init__(self, eng, sem):
        self.eng, self.sem, self.base, self.n = eng, sem, 0, 0

    def done(self, ins):
        ins.then_inc(self.sem, 1)
        self.n += 1

    def sync(self):
        self.eng.wait_ge(self.sem, self.base + self.n)

    def link(self, ins):
        self.done(ins)
        self.sync()


def max_units():
    out = []
    for t in range(KT):
        for chunk in range(2 if t >= 4 else 1):
            n = min(P * (t + 1) - 512 * chunk, 512)
            k = 4 if n == 128 else 2 if n == 256 else 1
            out += [(t, 512 * chunk, n, tuple(range(h, h + k)), chunk) for h in range(0, 4, k)]
    return out


def exp_units():
    out = []
    for half in range(2):
        for j in range(4 * (half + 1)):
            q0 = max(P * j, 512 * half)
            n = 512 * (half + 1) - q0
            k = 4 if n <= 256 else 2
            out += [(half, j, q0, n, tuple(range(h, h + k))) for h in range(0, 4, k)]
    return out


MAXU = max_units()
EXPU = exp_units()


def place(n, heads, i):
    at = heads.index(i)
    per = 4 if n == 128 else 2 if n == 256 else 1
    return at // per, (at % per) * n


def layer_kernel(nc, const, x, log_a, b_w, c_w, d_vec, ln1_w, ln1_b, ln2_w, ln2_b, conv_w,
                 attn_w, proj_w, router_w, expert_wv, expert_proj, out):
    ctx = ExitStack()
    with ctx:
        def sb(name, shape, dt=F32):
            return ctx.enter_context(nc.sbuf_tensor(name, shape, dt))

        def sem(name):
            return ctx.enter_context(nc.semaphore(name))

        cst = sb("cst", [P, C_COS])
        small = sb("small", [P, C_ALL - C_DS])
        ident = cst[:, C_IDENT:C_IDENT + P]
        ident_b = sb("ident_b", [P, P], BF16)
        mask_q = sb("mask_q", [P, P], BF16)
        mask_k = sb("mask_k", [P, P], BF16)
        w_qkv = sb("w_qkv", [P, 3 * D])
        w_rot = sb("w_rot", [P, 2 * D])
        w_proj = sb("w_proj", [P, D])
        w_router = sb("w_router", [P, NE])
        vecs = sb("vecs", [P, 8])
        x1 = sb("x1", [P, NB, CH, D])
        v_all = sb("v_all", [P, NB, KT, NH, VC])
        o_all = sb("o_all", [P, NB, KT, D])
        eps_t = sb("eps_t", [P, 1])
        ones = sb("ones", [32, P])
        zero3 = sb("zero3", [3, T], BF16)
        region = nc.sbuf_base + 64 - nc.sbuf_base % 64

        class Region:

            def __init__(self):
                self.at = region

            def __call__(self, name, shape, dt=F32):
                size = int(np.prod(shape[1:])) * (4 if dt == F32 else 2)
                t = nc.alloc_sbuf_tensor_at(name, shape, dt, offset=self.at)
                self.at += -(-size // 64) * 64
                assert self.at <= nc.sbuf_usable_end, (name, self.at)
                return t

        ra = Region()
        cos = ra("cos", [P, T])
        sin = ra("sin", [P, T])
        w_state = ra("w_state", [P, D, S])
        w_carry = ra("w_carry", [P, G, CH, 8])
        w_chunk = ra("w_chunk", [P, CH, D])
        decay = ra("decay", [P, G, P])
        b_pad = ra("b_pad", [P, 240])
        diag_d = ra("diag_d", [P, P])
        xt = [ra(f"xt{u}", [P, CH, D]) for u in range(2)]
        xT = [ra(f"xT{u}", [P, CH, P]) for u in range(2)]
        bt = [ra(f"bt{u}", [P, P]) for u in range(2)]
        hs = [ra(f"hs{u}", [P, G * P + 16]) for u in range(2)]
        hz = [ra(f"hz{u}", [P, CH, D]) for u in range(2)]
        hT = [ra(f"hT{u}", [P, T + 2]) for u in range(2)]
        hc = [ra(f"hc{u}", [P, T]) for u in range(2)]
        tq = [ra(f"tq{k}", [P, T]) for k in range(2)]
        tr = [ra(f"tr{k}", [P, T]) for k in range(2)]
        part = [[ra(f"part{k}_{j}", [P, T], BF16) for j in range(3)] for k in range(2)]
        st = [ra(f"st{u}", [P, CH, 6]) for u in range(2)]
        mv = [ra(f"mv{u}", [P, CH, 2]) for u in range(2)]
        hv = [ra(f"hv{u}", [P, 4, CH]) for u in range(2)]
        sc = [ra(f"sc{u}", [P, 8, CH]) for u in range(2)]
        lg_d = ra("lg_d", [P, S])
        cw_d = ra("cw_d", [P, S])
        lg_g = ra("lg_g", [G, P])
        cw_g = ra("cw_g", [G, P])
        bw_s = ra("bw_s", [S, P])
        dv = ra("dv", [P, 1])
        a_rep = ra("a_rep", [P, CH, S])
        c_rep = ra("c_rep", [P, CH, S])
        aT = ra("aT", [P, P])
        cT = ra("cT", [P, P])
        aG = ra("aG", [P, G])
        cG = ra("cG", [P, G])
        pu = ra("pu", [P, P])
        pi = ra("pi", [P, CH, D])
        ph = ra("ph", [P, CH, G])
        phc = ra("phc", [P, CH, G])

        rb = Region()
        qs = [rb(f"qs{g}", [P, 4, T], BF16) for g in range(HG)]
        ks = [rb(f"ks{g}", [P, 4, T], BF16) for g in range(HG)]
        vs = [rb(f"vs{g}", [P, KT, 4, VW]) for g in range(2)]
        pT = [rb(f"pT{n}", [P, T]) for n in range(4)]
        oT = [rb(f"oT{n}", [P, 512]) for n in range(2)]
        mx = [rb(f"mx{n}", [P, 4, KT]) for n in range(2)]
        mxb = [rb(f"mxb{n}", [P, 4, 4]) for n in range(2)]
        m_neg = rb("m_neg", [32, P])
        m_res = rb("m_res", [32, P])
        m_part = [rb(f"m_part{j}", [32, P], BF16) for j in range(3)]
        rden = [rb(f"rden{n}", [P, 4, 4]) for n in range(2)]

        w_val = rb("w_val", [P, NE, 2 * DFF])
        w_out = rb("w_out", [P, NE, FT, D])

        rc = Region()
        o_in = [rc(f"o_in{u}", [P, KT, D]) for u in range(2)]
        ocT = [rc(f"ocT{u}", [P, P, CH]) for u in range(2)]
        x2 = [rc(f"x2{u}", [P, CH, D]) for u in range(2)]
        acc = [rc(f"acc{u}", [P, CH, D]) for u in range(2)]
        zz = [rc(f"zz{u}", [P, CH, D]) for u in range(2)]
        h2T = [rc(f"h2T{u}", [P, CH, P]) for u in range(2)]
        gate = [rc(f"gate{n}", [P, 512]) for n in range(3)]
        act_v = [rc(f"act_v{n}", [P, FT, 512]) for n in range(2)]
        stc = [rc(f"stc{u}", [P, CH, 6]) for u in range(2)]
        mvc = [rc(f"mvc{u}", [P, CH, 2]) for u in range(2)]
        hvc = [rc(f"hvc{u}", [P, 4, CH]) for u in range(2)]
        scc = [rc(f"scc{u}", [P, 4, CH]) for u in range(2)]
        lmax = [rc(f"lmax{u}", [P, CH]) for u in range(2)]
        pick = [rc(f"pick{u}", [P, CH, NE]) for u in range(2)]
        left = [rc(f"left{u}", [P, CH]) for u in range(2)]

        ps = ctx.enter_context(nc.psum_tensor("ps", [P, 8, 512], F32))

        def banks(a, n):
            return ps[:, a:a + n, :].rearrange("p a c -> p (a c)")

        q_parts = nc.dram_tensor("q_parts", (NB, NH, 3, HD, T), BF16, kind="Internal").ap()
        k_parts = nc.dram_tensor("k_parts", (NB, NH, 3, HD, T), BF16, kind="Internal").ap()

        x_v = x.rearrange("b (p r) d -> b p r d", r=CH)
        out_v = out.rearrange("b (p r) d -> b p r d", r=CH)

        s_params = sem("params_loaded")
        s_weights = sem("weights_loaded")
        s_experts = sem("experts_loaded")
        s_set_act = sem("setup_act")
        s_set_dve = sem("setup_dve")
        s_set_pool = sem("setup_pool")
        s_set_pe = sem("setup_pe")
        s_x = [sem(f"x_loaded{u}") for u in range(2)]
        s_xtr = [sem(f"x_transposed{u}") for u in range(2)]
        s_xTa = [sem(f"xT_copied_act{u}") for u in range(2)]
        s_xTd = [sem(f"xT_copied_dve{u}") for u in range(2)]
        s_bt = [sem(f"inputs_projected{u}") for u in range(2)]
        s_btc = [sem(f"inputs_copied{u}") for u in range(2)]
        s_u = [sem(f"chunk_states_ready{u}") for u in range(2)]
        s_scan = [sem(f"states_scanned{u}") for u in range(2)]
        s_y = [sem(f"mixer_ready{u}") for u in range(2)]
        s_var = [sem(f"variance_ready{u}") for u in range(2)]
        s_sd = [sem(f"deviation_ready{u}") for u in range(2)]
        s_x1 = [sem(f"x1_ready{u}") for u in range(2)]
        s_hz = [sem(f"hz_ready{u}") for u in range(2)]
        s_hzt = [sem(f"hz_transposed{u}") for u in range(2)]
        s_hT = [sem(f"hT_ready{u}") for u in range(2)]
        s_hc = [sem(f"conv_ready{u}") for u in range(2)]
        s_qk = [sem(f"qk_projected{u}") for u in range(2)]
        s_rope = [sem(f"qk_turned{u}") for u in range(2)]
        s_v = [sem(f"v_projected{u}") for u in range(2)]
        s_vc = [sem(f"v_copied{u}") for u in range(2)]
        s_sum = [sem(f"qk_summed{k}") for k in range(2)]
        s_cast1 = [sem(f"part1_ready{k}") for k in range(2)]
        s_rest1 = [sem(f"rest1_ready{k}") for k in range(2)]
        s_cast2 = [sem(f"part2_ready{k}") for k in range(2)]
        s_cast3 = [sem(f"part3_ready{k}") for k in range(2)]
        s_stored = [sem(f"parts_stored{k}") for k in range(2)]
        s_dve = sem("dve_step")
        s_pool = sem("pool_step")
        s_clear = sem("slots_cleared")
        s_stage = [sem(f"slot_staged{g}") for g in range(HG)]
        s_mrow = sem("max_rows_written")
        s_vst = sem("values_staged")
        s_ms = sem("max_scores_ready")
        s_mr = sem("max_reduced")
        s_mg = sem("group_maxima_ready")
        s_mt = sem("maxima_transposed")
        s_mn = sem("maxima_negated")
        s_mpc = sem("max_part_steps")
        s_mp = sem("max_parts_ready")
        s_es = sem("exp_scores_ready")
        s_ex = sem("exp_done")
        s_pv = sem("unit_weighted")
        s_oc = sem("half_copied")
        s_ot = sem("half_transposed")
        s_on = sem("half_normalised")
        s_oin = [sem(f"o_staged{u}") for u in range(2)]
        s_otr = [sem(f"o_transposed{u}") for u in range(2)]
        s_oca = [sem(f"ocT_copied{u}") for u in range(2)]
        s_pj = [sem(f"projected{u}") for u in range(2)]
        s_x2 = [sem(f"x2_ready{u}") for u in range(2)]
        s_acc = [sem(f"acc_started{u}") for u in range(2)]
        s_varc = [sem(f"variance2_ready{u}") for u in range(2)]
        s_sdc = [sem(f"deviation2_ready{u}") for u in range(2)]
        s_zz = [sem(f"zz_ready{u}") for u in range(2)]
        s_zt = [sem(f"zz_transposed{u}") for u in range(2)]
        s_h2 = [sem(f"h2T_ready{u}") for u in range(2)]
        s_lg = [sem(f"logits_ready{u}") for u in range(2)]
        s_pk = [sem(f"experts_picked{u}") for u in range(2)]
        s_gv = sem("gate_value_ready")
        s_sg = sem("gate_silu_ready")
        s_av = sem("activations_ready")
        s_yy = sem("expert_out_ready")
        s_ya = sem("expert_out_added")
        s_res = [sem(f"result_ready{u}") for u in range(2)]
        s_out = [sem(f"result_stored{u}") for u in range(2)]

        block = ctx.enter_context(nc.Block())

        VC_CREDIT = ROPE_CREDIT = CAST3_CREDIT = 1
        STORED_CREDIT = 16
        MR_CREDIT, EX_CREDIT, PV_CREDIT, OC_CREDIT, OT_CREDIT = 2, 2, 4, 1, 2
        OTR_CREDIT, OUT_CREDIT, AV_CREDIT, YA_CREDIT = 1, 16, 1, 1
        NMU, NEU = len(MAXU), len(EXPU)
        STAGE = 16 * 13
        MROW = 16 * 3
        HALF0 = sum(1 for e in EXPU if e[0] == 0)
        UNITS = 2 * NE * 2 * FT
        CHUNKS = 2 * NE * 2

        @block.sync
        def _(sp):
            for dst, src in (
                (cst[:, :], const[:, 0:C_COS]), (small[:, :], const[:, C_DS:C_ALL]),
                (lg_d[:, :], log_a), (cw_d[:, :], c_w),
                (lg_g[:, :], log_a.rearrange("(g e) s -> g (e s)", e=8)),
                (cw_g[:, :], c_w.rearrange("(g e) s -> g (e s)", e=8)),
                (bw_s[:, :], b_w), (dv[:, :], d_vec.rearrange("(d o) -> d o", o=1)),
            ):
                sp.dma_start(dst, src).then_inc(s_params, 16)
            for u in range(2):
                sp.dma_start(xt[u][:, :, :], x_v[u]).then_inc(s_x[u], 16)
            for dst, src in (
                (w_qkv[:, :], attn_w), (cos[:, :], const[:, C_COS:C_COS + T]),
                (sin[:, :], const[:, C_SIN:C_SIN + T]),
                (w_proj[:, :], proj_w), (w_router[:, :], router_w),
                (vecs[:, 0:1], ln1_w.rearrange("(d o) -> d o", o=1)),
                (vecs[:, 1:2], ln1_b.rearrange("(d o) -> d o", o=1)),
                (vecs[:, 2:3], ln2_w.rearrange("(d o) -> d o", o=1)),
                (vecs[:, 3:4], ln2_b.rearrange("(d o) -> d o", o=1)),
                (vecs[:, 4:7], conv_w.rearrange("c o k -> c (o k)")),
            ):
                sp.dma_start(dst, src).then_inc(s_weights, 16)
            for u in range(2):
                sp.wait_ge(s_xtr[u], 1)
                sp.dma_start(xt[u][:, :, :], x_v[2 + u]).then_inc(s_x[u], 16)

            with sp.Fori(0, 2) as i:
                for k, dram in ((0, q_parts), (1, k_parts)):
                    for u in range(2):
                        for j, s, credit in ((0, s_cast1, 0), (1, s_cast2, 0), (2, s_cast3, CAST3_CREDIT)):
                            sp.wait_ge(s[k], 2 * i + u + 1 + credit)
                            dst = dram[2 * i + u].rearrange("h j d t -> j h d t")[j]
                            sp.dma_start(dst, part[k][j][:, :]
                                         ).then_inc(s_stored[k], 16)

            for k in range(2):
                sp.wait_ge(s_stored[k], 16 * 3 * NB + STORED_CREDIT)
            sp.wait_ge(s_clear, 2)

            def stage(b, g):
                q_g = q_parts[b].rearrange("h j d t -> (j d) h t")[:, 4 * g:4 * g + 4, :]
                k_g = k_parts[b].rearrange("h j d t -> (j d) h t")[:, 4 * g:4 * g + 4, :]
                for i in range(3):
                    sp.dma_start(qs[g][24 * i:24 * i + 24, :, :], q_g).then_inc(s_stage[g], 16)
                    for j in range(3):
                        at = 24 * i + 8 * j
                        sp.dma_start(ks[g][at:at + 8, :, :], k_g[8 * i:8 * i + 8]).then_inc(s_stage[g], 16)
                sp.dma_start(qs[g][96:99, :, :], zero3[:, :].unsqueeze(1).broadcast_to([3, 4, T])
                             ).then_inc(s_stage[g], 16)

            def max_rows(n, g):
                sp.wait_ge(s_mp, n + 1)
                for j in range(3):
                    sp.dma_start(qs[g][96 + j:97 + j, :, :], m_part[j][:, :]).then_inc(s_mrow, 16)

            for g in range(HG):
                stage(0, g)
                if g == 1:
                    for e in range(NE):
                        sp.dma_start(w_val[:, e, :], expert_wv[e]).then_inc(s_experts, 16)
                        sp.dma_start(w_out[:, e, :, :], expert_proj[e].rearrange("(f p) d -> p f d", p=P)
                                     ).then_inc(s_experts, 16)

            for g in range(HG):
                if g >= 1:
                    max_rows(g - 1, g - 1)
                if g >= 2:
                    sp.wait_ge(s_es, NEU * (g - 1))
                    stage(1, g - 2)
            with sp.Fori(1, NB - 1) as b:
                for g in range(HG):
                    max_rows(4 * b + g - 1, (g + 3) % 4)
                    sp.wait_ge(s_es, NEU * (4 * b + g - 1))
                    stage(b + 1 if g >= 2 else b, (g + 2) % 4)
            for g in range(HG):
                n = 4 * (NB - 1) + g
                max_rows(n - 1, (g + 3) % 4)
                if g < 2:
                    sp.wait_ge(s_es, NEU * (n - 1))
                    stage(NB - 1, g + 2)
            max_rows(4 * NB - 1, 3)

            with sp.Fori(0, 2) as i:
                for u in range(2):
                    sp.wait_ge(s_res[u], i + 1)
                    sp.dma_start(out_v[2 * i + u], zz[u][:, :, :]).then_inc(s_out[u], 16)
            for u in range(2):
                sp.wait_ge(s_out[u], 32 + OUT_CREDIT)

        @block.tensor
        def _(pe):
            mm = nc.tensor.matmul

            def tp(out_, in_, k=P):
                return nc.tensor.transpose(out_, in_, ident[0:k, 0:k])

            pe.sem_inc(s_mr, MR_CREDIT)
            pe.sem_inc(s_ex, EX_CREDIT)
            for u in range(2):
                pe.sem_inc(s_vc[u], VC_CREDIT)
                pe.sem_inc(s_rope[u], ROPE_CREDIT)
            pe.sem_inc(s_oc, OC_CREDIT)
            pe.sem_inc(s_av, AV_CREDIT)
            pe.sem_inc(s_ya, YA_CREDIT)

            pe.wait_ge(s_params, 16 * 8)
            tp(ps[:, 0, 0:S], bw_s[:, :], S).then_inc(s_set_pe, 1)
            pe.wait_ge(s_set_dve, 1)
            tp(ps[:, 1, 0:P], a_rep[:, :, :].rearrange("d j s -> d (j s)"))
            tp(ps[:, 1, P:2 * P], c_rep[:, :, :].rearrange("d j s -> d (j s)"))
            tp(ps[:, 2, 0:G], lg_g[:, :], G)
            tp(ps[:, 2, G:2 * G], cw_g[:, :], G).then_inc(s_set_pe, 1)
            pe.wait_ge(s_set_dve, 3)
            pe.wait_ge(s_set_pool, 1)
            pe.wait_ge(s_weights, 16 * 10)

            with pe.Fori(0, 2) as i:
                for u in range(2):
                    pe.wait_ge(s_x[u], 16 * i + 16)
                    pe.wait_ge(s_vc[u], i + VC_CREDIT)
                    for r in range(CH):
                        last = tp(ps[:, 4 * u + r // 4, (r % 4) * P:(r % 4 + 1) * P], xt[u][:, r, :])
                    last.then_inc(s_xtr[u], 1)
                for u in range(2):
                    pe.wait_ge(s_xTa[u], i + 1)
                    pe.wait_ge(s_xTd[u], i + 1)
                    pe.wait_ge(s_rope[u], 2 * i + ROPE_CREDIT)
                    for j in range(CH):
                        last = mm(ps[:, 4 * u + 2, 0:P], b_pad[:, 112 - S * j:240 - S * j], xT[u][:, j, :],
                                  start=(j == 0), stop=(j == CH - 1))
                    last.then_inc(s_bt[u], 1)
                for u in range(2):
                    pe.wait_ge(s_btc[u], i + 1)
                    for g in range(G):
                        last = mm(ps[:, 4 * u + g // 4, (g % 4) * P:(g % 4 + 1) * P],
                                  w_state[:, 8 * g:8 * g + 8, :].rearrange("p d s -> p (d s)"), bt[u][:, :],
                                  start=(g % 4 == 0), stop=True, skip_group_check=True)
                    last.then_inc(s_u[u], 1)
                for u in range(2):
                    pe.wait_ge(s_scan[u], i + 1)
                    for h in range(2):
                        y = ps[:, 4 * u + h, :].rearrange("p (r d) -> p r d", d=D)
                        mm(ps[:, 4 * u + h, :], bt[u][:, :],
                           w_chunk[:, 4 * h:4 * h + 4, :].rearrange("p r d -> p (r d)"),
                           start=True, stop=False, skip_group_check=True)
                        for r in range(4):
                            mm(y[:, r, :], xT[u][:, 4 * h + r, :], diag_d[:, :],
                               start=False, stop=False, skip_group_check=True)
                        for g in range(G):
                            last = mm(y[:, :, 8 * g:8 * g + 8], hs[u][:, g * P:(g + 1) * P],
                                      w_carry[:, g, 4 * h:4 * h + 4, :],
                                      start=False, stop=(g == G - 1), skip_group_check=True)
                    last.then_inc(s_y[u], 1)
                for u in range(2):
                    pe.wait_ge(s_hz[u], i + 1)
                    for r in range(CH):
                        last = tp(ps[:, 4 * u + 2 + r // 4, (r % 4) * P:(r % 4 + 1) * P], hz[u][:, r, :])
                    last.then_inc(s_hzt[u], 1)
                for k in range(2):
                    for u in range(2):
                        if k == 0:
                            pe.wait_ge(s_hc[u], i + 1)
                        else:
                            pe.wait_ge(s_rope[u], 2 * i + 1 + ROPE_CREDIT)
                        for w, at in ((w_qkv, 0), (w_rot, 2)):
                            for h in range(2):
                                last = mm(ps[:, 4 * u + at + h, :], w[:, k * D:(k + 1) * D],
                                          hc[u][:, 512 * h:512 * h + 512], start=True, stop=True)
                        last.then_inc(s_qk[u], 1)
                for u in range(2):
                    pe.wait_ge(s_rope[u], 2 * i + 2 + ROPE_CREDIT)
                    for t in range(KT):
                        last = mm(ps[:, 4 * u + t // 4, (t % 4) * P:(t % 4 + 1) * P],
                                  hc[u][:, t * P:(t + 1) * P], w_qkv[:, 2 * D:3 * D],
                                  start=(t % 4 == 0), stop=True, skip_group_check=True)
                    last.then_inc(s_v[u], 1)

            for u in range(2):
                pe.wait_ge(s_vc[u], 2 + VC_CREDIT)
            MISC, OBANK, MBANK = 5, 4, 6

            def max_unit(n, b, g, idx):
                t, k0, nk, heads, chunk = MAXU[idx]
                bank = MBANK + idx % 2
                if idx == 0:
                    pe.wait_ge(s_stage[g], STAGE * (b + 1))
                pe.wait_ge(s_mr, NMU * n + idx - 1 + MR_CREDIT)
                diag = k0 + nk == P * (t + 1)
                for a, h in enumerate(heads):
                    last = mm(ps[:, bank, a * nk:(a + 1) * nk], qs[g][:, h, t * P:(t + 1) * P],
                              ks[g][:, h, k0:k0 + nk], start=(a == 0),
                              stop=(not diag), skip_group_check=True)
                if diag:
                    m = len(heads)
                    o = ps[:, bank, 0:m * nk].rearrange("p (h k) -> p h k", h=m)[:, :, nk - P:nk]
                    last = mm(o, ident_b[:, :], mask_q[:, :].unsqueeze(1).broadcast_to([P, m, P]),
                              start=False, stop=True, skip_group_check=True)
                last.then_inc(s_ms, 1)

            def exp_unit(n, g, idx):
                half, j, q0, nq, heads = EXPU[idx]
                pair = 2 * (idx % 2)
                if idx == 0:
                    pe.wait_ge(s_mrow, MROW * (n + 1))
                pe.wait_ge(s_ex, NEU * n + idx - 1 + EX_CREDIT)
                diag = q0 == P * j
                for h in heads:
                    bank, col = place(nq, heads, h)
                    first = col == 0
                    last = mm(ps[:, pair + bank, col:col + nq], ks[g][:, h, j * P:(j + 1) * P],
                              qs[g][:, h, q0:q0 + nq], start=first, stop=(not diag), skip_group_check=True)
                if diag:
                    per = 4 if nq == 128 else 2 if nq == 256 else 1
                    for bank in range(len(heads) // per):
                        o = ps[:, pair + bank, 0:per * nq].rearrange("p (h q) -> p h q", h=per)[:, :, 0:P]
                        last = mm(o, ident_b[:, :], mask_k[:, :].unsqueeze(1).broadcast_to([P, per, P]),
                                  start=False, stop=True, skip_group_check=True)
                last.then_inc(s_es, 1)

            def weigh(n, par, idx):
                half, j, q0, nq, heads = EXPU[idx]
                if idx == 0:
                    pe.wait_ge(s_vst, n + 1)
                if j == 0 and heads[0] == 0:
                    pe.wait_ge(s_oc, 2 * n + half + OC_CREDIT)
                pe.wait_ge(s_ex, NEU * n + idx + 1 + EX_CREDIT)
                for a, h in enumerate(heads):
                    last = mm(ps[VW * h:VW * h + VW, OBANK, q0 - 512 * half:512],
                              vs[par][:, j, h, :], pT[idx % 4][:, a * nq:(a + 1) * nq],
                              start=(j == 0), stop=(j == 4 * half + 3), skip_group_check=True)
                last.then_inc(s_pv, 1)

            def turn_max(n, par):
                pe.wait_ge(s_mg, n + 1)
                tp(ps[0:32, MISC, 0:P], mx[par][:, :, :].rearrange("p h t -> p (h t)")).then_inc(s_mt, 1)

            def turn_out(n, half):
                pe.wait_ge(s_oc, 2 * n + half + 1 + OC_CREDIT)
                for t in range(4):
                    last = tp(ps[:, MISC, t * P:(t + 1) * P], oT[half][:, t * P:(t + 1) * P])
                last.then_inc(s_ot, 1)

            def step(mn, mb, mg, en, eg, first_exp=False, last_exp=False):
                done_m = 0

                def maxima(upto):
                    nonlocal done_m
                    while mn is not None and done_m < min(upto, NMU):
                        max_unit(mn, mb, mg, done_m)
                        done_m += 1

                weighed = 0
                for k in range(NEU):
                    if en is None:
                        break
                    exp_unit(en, eg, k)
                    maxima((k + 1) * NMU // NEU)
                    if k == 2 and not first_exp:
                        pe.wait_ge(s_on, 2 * en - 1)
                        turn_out(en - 1, 1)
                    if k == 5:
                        if not first_exp:
                            pe.wait_ge(s_on, 2 * en)
                        if not last_exp:
                            turn_max(en + 1, (eg + 1) % 2)
                    if k == 14:
                        if not last_exp:
                            pe.wait_ge(s_mn, en + 2)
                        turn_out(en, 0)
                    while k - weighed >= 2:
                        weigh(en, eg % 2, weighed)
                        weighed += 1
                if en is None:
                    maxima(4)
                    if mn > 0:
                        turn_max(mn - 1, (mg + 1) % 2)
                    maxima(NMU)
                else:
                    while weighed < NEU:
                        weigh(en, eg % 2, weighed)
                        weighed += 1

            step(0, 0, 0, None, None)
            step(1, 0, 1, None, None)
            step(2, 0, 2, 0, 0, first_exp=True)
            step(3, 0, 3, 1, 1)
            with pe.Fori(1, NB) as b:
                for g in range(HG):
                    step(4 * b + g, b, g, 4 * b + g - 2, (g + 2) % 4)
            step(None, None, None, 4 * NB - 2, 2)
            step(None, None, None, 4 * NB - 1, 3, last_exp=True)
            pe.wait_ge(s_on, 2 * 4 * NB - 1)
            turn_out(4 * NB - 1, 1)

            pe.wait_ge(s_on, 2 * 4 * NB)
            pe.wait_ge(s_experts, 16 * 2 * NE)
            with pe.Fori(0, 2) as i:
                pe.wait_ge(s_av, UNITS * i + AV_CREDIT)
                pe.wait_ge(s_ya, CHUNKS * i + YA_CREDIT)
                for u in range(2):
                    pe.wait_ge(s_oin[u], i + 1)
                    for t in range(KT):
                        last = tp(ps[:, 4 * u + t // 4, (t % 4) * P:(t % 4 + 1) * P], o_in[u][:, t, :])
                    last.then_inc(s_otr[u], 1)
                for u in range(2):
                    pe.wait_ge(s_oca[u], i + 1)
                    for r in range(CH):
                        last = mm(ps[:, 4 * u + 2 + r // 4, (r % 4) * P:(r % 4 + 1) * P],
                                  ocT[u][:, :, r], w_proj[:, :], start=(r % 4 == 0), stop=True,
                                  skip_group_check=True)
                    last.then_inc(s_pj[u], 1)
                for u in range(2):
                    pe.wait_ge(s_zz[u], i + 1)
                    for r in range(CH):
                        last = tp(ps[:, 4 * u + r // 4, (r % 4) * P:(r % 4 + 1) * P], zz[u][:, r, :])
                    last.then_inc(s_zt[u], 1)
                for u in range(2):
                    pe.wait_ge(s_h2[u], i + 1)
                    for r in range(CH):
                        last = mm(ps[:, 4 * u + 2, r * NE:(r + 1) * NE], h2T[u][:, r, :], w_router[:, :],
                                  start=(r == 0), stop=True, skip_group_check=True)
                    last.then_inc(s_lg[u], 1)
                for u in range(2):
                    pe.wait_ge(s_pk[u], i + 1)

                def down(c):
                    e = c // 2 % NE
                    pe.wait_ge(s_av, UNITS * i + FT * (c + 1) + AV_CREDIT)
                    if c >= 2:
                        pe.wait_ge(s_ya, CHUNKS * i + c - 1 + YA_CREDIT)
                    for r in range(4):
                        for f in range(FT):
                            last = mm(ps[:, 6 + c % 2, r * P:(r + 1) * P], act_v[c % 2][:, f, r * P:(r + 1) * P],
                                      w_out[:, e, f, :], start=(r == 0 and f == 0), stop=(f == FT - 1),
                                      skip_group_check=True)
                    last.then_inc(s_yy, 1)

                for c in range(CHUNKS):
                    u, e, ch = c // (2 * NE), c // 2 % NE, c % 2
                    for f in range(FT):
                        idx = FT * c + f
                        if idx >= 3:
                            pe.wait_ge(s_av, UNITS * i + idx - 2 + AV_CREDIT)
                        for v in range(2):
                            col = v * DFF + f * P
                            last = mm(ps[:, 2 * (idx % 3) + v, :], w_val[:, e, col:col + P],
                                      h2T[u][:, 4 * ch:4 * ch + 4, :].rearrange("p r t -> p (r t)"),
                                      start=True, stop=True)
                        last.then_inc(s_gv, 1)
                    if c:
                        down(c - 1)
                down(CHUNKS - 1)

        @block.scalar
        def _(act):
            A = nc.scalar.activation
            for k in range(2):
                act.sem_inc(s_stored[k], STORED_CREDIT)
            act.sem_inc(s_pv, PV_CREDIT)
            act.sem_inc(s_ot, OT_CREDIT)

            act.wait_ge(s_params, 16 * 8)
            A(lg_d[:, :], lg_d[:, :], ACT.Exp)
            A(lg_g[:, :], lg_g[:, :], ACT.Exp).then_inc(s_set_act, 1)
            act.wait_ge(s_set_dve, 2)
            A(pu[:, :], aT[:, :], ACT.Exp, scale=small[:, C_PU - C_DS:C_PU - C_DS + 1])
            for r in range(CH):
                at = C_PI - C_DS + r
                A(pi[:, r, :], aT[:, :], ACT.Exp, scale=small[:, at:at + 1])
                last = A(ph[:, r, :], aG[:, :], ACT.Exp, scale=-float(r + 1))
            last.then_inc(s_set_act, 1)

            act.wait_ge(s_weights, 16 * 10)
            act.wait_ge(s_set_dve, 3)
            with act.Fori(0, 2) as i:
                for u in range(2):
                    act.wait_ge(s_xtr[u], i + 1)
                    A(xT[u][:, 0:4, :], ps[:, 4 * u, :].rearrange("p (r c) -> p r c", c=P),
                      ACT.Copy).then_inc(s_xTa[u], 1)
                for m in range(2):
                    for u in range(2):
                        act.wait_ge(s_var[u], 2 * i + m + 1)
                        src = mv[u][:, :, 1] if m == 0 else sc[u][:, 3, :]
                        A(sc[u][:, 4 * m, :], src, ACT.Sqrt, bias=eps_t[:, 0:1]).then_inc(s_sd[u], 1)
                for u in range(2):
                    act.wait_ge(s_hzt[u], i + 1)
                    slots = hT[u][:, 2:T + 2].rearrange("c (p r) -> c r p", r=CH)
                    for h in range(2):
                        last = A(slots[:, 4 * h:4 * h + 4, :],
                                 ps[:, 4 * u + 2 + h, :].rearrange("c (r p) -> c r p", p=P),
                                 ACT.Identity, scale=vecs[:, 0:1], bias=vecs[:, 1:2])
                    last.then_inc(s_hT[u], 1)
                for k in range(2):
                    for u in range(2):
                        m = 2 * i + u
                        act.wait_ge(s_sum[k], m + 1)
                        act.wait_ge(s_stored[k], 48 * m + STORED_CREDIT)
                        A(part[k][0][:, :], tq[k][:, :], ACT.Copy).then_inc(s_cast1[k], 1)
                        act.wait_ge(s_rest1[k], m + 1)
                        A(part[k][1][:, :], tr[k][:, :], ACT.Copy).then_inc(s_cast2[k], 1)
                for u in range(2):
                    act.wait_ge(s_v[u], i + 1)
                    for h in range(2):
                        last = A(v_all[:, 2 * i + u, 4 * h:4 * h + 4, :, 0:HD],
                                 ps[:, 4 * u + h, :].rearrange("p (t h d) -> p t h d", t=4, d=HD), ACT.Copy)
                    last.then_inc(s_vc[u], 1)

            def negate_max(n, first=False):
                act.wait_ge(s_mt, n + 1)
                if not first:
                    act.wait_ge(s_mp, n)
                A(m_neg[:, :], ps[0:32, 5, 0:P], ACT.Copy, scale=-1.0).then_inc(s_mn, 1)

            def copy_out(n, half):
                units = HALF0 if half == 0 else NEU
                act.wait_ge(s_pv, NEU * n + units + PV_CREDIT)
                act.wait_ge(s_ot, 2 * n + half - 1 + OT_CREDIT)
                A(oT[half][:, :], ps[:, 4, :], ACT.Copy).then_inc(s_oc, 1)

            def exps(n, max_n):
                for k, (half, j, q0, nq, heads) in enumerate(EXPU):
                    act.wait_ge(s_es, NEU * n + k + 1)
                    act.wait_ge(s_pv, NEU * n + k - 3 + PV_CREDIT)
                    pair = 2 * (k % 2)
                    w = nq * len(heads)
                    if nq == 384:
                        src = ps[:, pair:pair + 2, 0:nq]
                        dst = pT[k % 4][:, 0:w].rearrange("p (h q) -> p h q", h=2)
                    else:
                        src = banks(pair, 2)[:, 0:w]
                        dst = pT[k % 4][:, 0:w]
                    A(dst, src, ACT.Exp, scale=SCALE).then_inc(s_ex, 1)
                    if k == HALF0 + 1:
                        copy_out(n, 0)
                    if k == 8 and max_n is not None:
                        negate_max(max_n)
                copy_out(n, 1)

            negate_max(0, first=True)
            exps(0, 1)
            exps(1, 2)
            with act.Fori(1, NB) as b:
                for g in range(HG):
                    exps(4 * b + g - 2, 4 * b + g - 1)
            exps(4 * NB - 2, 4 * NB - 1)
            exps(4 * NB - 1, None)

            with act.Fori(0, 2) as i:
                for u in range(2):
                    act.wait_ge(s_otr[u], i + 1 + OTR_CREDIT)
                    A(ocT[u][:, :, :].rearrange("c p r -> c (p r)"), banks(4 * u, 2), ACT.Copy
                      ).then_inc(s_oca[u], 1)
                for u in range(2):
                    act.wait_ge(s_varc[u], 2 * i + 1)
                    A(scc[u][:, 0, :], mvc[u][:, :, 1], ACT.Sqrt, bias=eps_t[:, 0:1]).then_inc(s_sdc[u], 1)
                for u in range(2):
                    act.wait_ge(s_zt[u], i + 1)
                    A(h2T[u][:, :, :].rearrange("c r p -> c (r p)"), banks(4 * u, 2), ACT.Identity,
                      scale=vecs[:, 2:3], bias=vecs[:, 3:4]).then_inc(s_h2[u], 1)
                for idx in range(UNITS):
                    act.wait_ge(s_gv, UNITS * i + idx + 1)
                    if idx >= 3:
                        act.wait_ge(s_av, UNITS * i + idx - 2 + AV_CREDIT)
                    A(gate[idx % 3][:, :], ps[:, 2 * (idx % 3), :], ACT.Silu).then_inc(s_sg, 1)
                for u in range(2):
                    act.wait_ge(s_varc[u], 2 * i + 2)
                    A(scc[u][:, 0, :], mvc[u][:, :, 1], ACT.Sqrt, bias=eps_t[:, 0:1]).then_inc(s_sdc[u], 1)

        @block.vector
        def _(dve):
            V = nc.vector
            chain = Chain(dve, s_dve)
            for k in range(2):
                dve.sem_inc(s_cast3[k], CAST3_CREDIT)

            def merge_halves(to, stats, tmp):
                m0, m1, v0, v1 = (stats[:, :, c] for c in (1, 4, 2, 5))
                V.tensor_tensor(tmp[:, 0, :], m0, m1, ALU.add)
                V.tensor_tensor(tmp[:, 1, :], m0, m1, ALU.subtract)
                chain.link(V.tensor_tensor(tmp[:, 2, :], v0, v1, ALU.add))
                V.tensor_scalar(to[:, :, 0], tmp[:, 0, :], 0.5, None, ALU.mult)
                chain.link(V.scalar_tensor_tensor(out=tmp[:, 3, :], in0=tmp[:, 1, :], scalar=0.25,
                                                  in1=tmp[:, 1, :], op0=ALU.mult, op1=ALU.mult))
                return V.scalar_tensor_tensor(out=to[:, :, 1], in0=tmp[:, 2, :], scalar=1.0 / D,
                                              in1=tmp[:, 3, :], op0=ALU.mult, op1=ALU.add)

            V.memset(eps_t[:, :], EPS)
            V.memset(b_pad[:, :], 0.0)
            for u in range(2):
                V.memset(hT[u][:, 0:2], 0.0)
            V.memset(zero3[:, :], 0.0)
            dve.wait_ge(s_params, 16 * 8)
            V.tensor_copy(ident_b[:, :], ident)
            V.tensor_copy(mask_q[:, :], cst[:, C_MASKQ:C_MASKQ + P])
            V.tensor_copy(mask_k[:, :], cst[:, C_MASKK:C_MASKK + P])
            V.tensor_scalar(diag_d[:, :], ident, dv[:, 0:1], None, ALU.mult)
            V.tensor_copy(c_rep[:, :, :], cw_d[:, :].unsqueeze(1).broadcast_to([P, CH, S]))
            dve.wait_ge(s_set_act, 1)
            V.tensor_scalar(a_rep[:, :, :], lg_d[:, :].unsqueeze(1).broadcast_to([P, CH, S]),
                            RATE_MAX, None, ALU.min)
            chain.link(V.tensor_scalar(lg_g[:, :], lg_g[:, :], RATE_MAX, None, ALU.min))
            V.tensor_tensor(diag_d[:, :], diag_d[:, :], ident, ALU.add).then_inc(s_set_dve, 1)
            dve.wait_ge(s_set_pe, 2)
            V.tensor_copy(b_pad[:, 112:128], ps[:, 0, 0:S])
            V.tensor_copy(aT[:, :], ps[:, 1, 0:P])
            V.tensor_copy(cT[:, :], ps[:, 1, P:2 * P])
            V.tensor_copy(aG[:, :], ps[:, 2, 0:G])
            V.tensor_copy(cG[:, :], ps[:, 2, G:2 * G]).then_inc(s_set_dve, 1)
            dve.wait_ge(s_set_dve, 2)
            dve.wait_ge(s_set_act, 2)
            V.tensor_tensor(w_state[:, :, :], pu[:, :].unsqueeze(2).broadcast_to([P, D, S]),
                            small[:, 0:S].unsqueeze(1).broadcast_to([P, D, S]), ALU.mult)
            chain.link(V.tensor_tensor(phc[:, :, :], ph[:, :, :],
                                       cG[:, :].unsqueeze(1).broadcast_to([P, CH, G]), ALU.mult))
            for g in range(G):
                V.tensor_tensor(w_carry[:, g, :, :], phc[:, :, g].unsqueeze(2).broadcast_to([P, CH, 8]),
                                small[:, C_DD - C_DS:C_DD - C_DS + 8].unsqueeze(1).broadcast_to([P, CH, 8]),
                                ALU.mult)
            for r in range(CH):
                at = C_CM - C_DS + r
                last = V.scalar_tensor_tensor(out=w_chunk[:, r, :], in0=pi[:, r, :], scalar=small[:, at:at + 1],
                                              in1=cT[:, :], op0=ALU.mult, op1=ALU.mult)
            last.then_inc(s_set_dve, 1)
            dve.wait_ge(s_weights, 16 * 10)

            dve.wait_ge(s_set_pool, 1)
            A_CHAIN = 16
            base = chain.n
            with dve.Fori(0, 2) as i:
                chain.base, chain.n = base + A_CHAIN * i, 0
                for u in range(2):
                    dve.wait_ge(s_xtr[u], i + 1)
                    V.tensor_copy(xT[u][:, 4:8, :], ps[:, 4 * u + 1, :].rearrange("p (r c) -> p r c", c=P)
                                  ).then_inc(s_xTd[u], 1)
                for u in range(2):
                    dve.wait_ge(s_bt[u], i + 1)
                    V.tensor_copy(bt[u][:, :], ps[:, 4 * u + 2, 0:P]).then_inc(s_btc[u], 1)
                for u in range(2):
                    dve.wait_ge(s_u[u], i + 1)
                    chain.link(V.tensor_tensor_scan(hs[u][:, 1:G * P + 1], decay[:, :, :].rearrange("p g c -> p (g c)"),
                                                    banks(4 * u, 4), 0.0, ALU.mult, ALU.add))
                    V.memset(hs[u][:, 0:G * P].rearrange("p (g c) -> p g c", c=P)[:, :, 0:1], 0.0
                             ).then_inc(s_scan[u], 1)
                for u in range(2):
                    dve.wait_ge(s_y[u], i + 1)
                    for r in range(CH):
                        last = V.bn_stats(st[u][:, r, :], ps[:, 4 * u + r // 4, (r % 4) * P:(r % 4 + 1) * P])
                    chain.link(last)
                    merge_halves(mv[u], st[u], hv[u]).then_inc(s_var[u], 1)
                for u in range(2):
                    dve.wait_ge(s_sd[u], 2 * i + 1)
                    dve.wait_ge(s_var[u], 2 * i + 1)
                    chain.link(V.reciprocal(sc[u][:, 1, :], sc[u][:, 0, :]))
                    chain.link(V.tensor_tensor(sc[u][:, 2, :], mv[u][:, :, 1], sc[u][:, 1, :], ALU.mult))
                    V.tensor_tensor(sc[u][:, 3, :], sc[u][:, 2, :], sc[u][:, 1, :], ALU.mult
                                    ).then_inc(s_var[u], 1)
                    for r in range(CH):
                        V.tensor_scalar(x1[:, 2 * i + u, r, :], ps[:, 4 * u + r // 4, (r % 4) * P:(r % 4 + 1) * P],
                                        mv[u][:, r, 0:1], sc[u][:, 1, r:r + 1], ALU.subtract, ALU.mult)
                    dve.wait_ge(s_sd[u], 2 * i + 2)
                    V.reciprocal(sc[u][:, 5, :], sc[u][:, 4, :]).then_inc(s_x1[u], 1)
                for u in range(2):
                    dve.wait_ge(s_hT[u], i + 1)
                    for k in range(3):
                        if k == 0:
                            ins = V.tensor_scalar(hc[u][:, :], hT[u][:, 0:T], vecs[:, 4:5], None, ALU.mult)
                        else:
                            ins = V.scalar_tensor_tensor(out=hc[u][:, :], in0=hT[u][:, k:T + k],
                                                         scalar=vecs[:, 4 + k:5 + k], in1=hc[u][:, :],
                                                         op0=ALU.mult, op1=ALU.add)
                        if k < 2:
                            chain.link(ins)
                        else:
                            ins.then_inc(s_hc[u], 1)
                for k in range(2):
                    for u in range(2):
                        dve.wait_ge(s_qk[u], 2 * i + k + 1)
                        dve.wait_ge(s_cast3[k], 2 * i + u + CAST3_CREDIT)
                        V.tensor_tensor(tq[k][:, :], banks(4 * u, 2), cos[:, :], ALU.mult)
                        V.tensor_tensor(tr[k][:, :], banks(4 * u + 2, 2), sin[:, :], ALU.mult
                                        ).then_inc(s_rope[u], 1)
                assert chain.n == A_CHAIN, chain.n
            chain.base, chain.n = base + 2 * A_CHAIN, 0

            for k in range(2):
                dve.wait_ge(s_stored[k], 16 * 3 * NB + STORED_CREDIT)
            for u in range(2):
                dve.wait_ge(s_vc[u], 2 + VC_CREDIT)
            for g in range(HG):
                last = V.memset(ks[g][:, :, :].rearrange("p h t -> p (h t)").bitcast(F32), 0.0)
            chain.link(last)
            for g in range(HG):
                last = V.memset(ks[g][96:99, :, :], 1.0)
            last.then_inc(s_clear, 1)

            def reduce_unit(n, par, idx):
                t, k0, nk, heads, chunk = MAXU[idx]
                dve.wait_ge(s_ms, NMU * n + idx + 1)
                m = len(heads)
                dst = mx[par][:, heads[0]:heads[0] + m, t] if chunk == 0 else \
                    mxb[par][:, heads[0]:heads[0] + m, t - 4]
                V.tensor_reduce(dst, ps[:, 6 + idx % 2, 0:m * nk].rearrange("p (h k) -> p h k", h=m),
                                AX_X, ALU.max).then_inc(s_mr, 1)

            def combine(n, par):
                dve.wait_ge(s_mr, NMU * (n + 1) + MR_CREDIT)
                V.tensor_tensor(mx[par][:, :, 4:8], mx[par][:, :, 4:8], mxb[par][:, :, :], ALU.max
                                ).then_inc(s_mg, 1)

            def normalise(n, b, eg, half):
                dve.wait_ge(s_ot, 2 * n + half + 1 + OT_CREDIT)
                o = ps[:, 5, :].rearrange("p (t h d) -> p t h d", t=4, h=4)
                chain.link(V.reciprocal(rden[half][:, :, :], o[:, :, :, HD]))
                dst = o_all[:, b, 4 * half:4 * half + 4, 32 * eg:32 * eg + 32].rearrange(
                    "p t (h d) -> p t h d", d=HD)
                V.tensor_tensor(dst, o[:, :, :, 0:HD], rden[half][:, :, :].unsqueeze(3).broadcast_to([P, 4, 4, HD]),
                                ALU.mult).then_inc(s_on, 1)

            def step(mn, mg, en, eb, eg, pb, first_exp=False):
                if mn is not None:
                    for idx in range(NMU):
                        if idx == 0 and en is not None:
                            dve.wait_ge(s_mt, mn - 1)
                        reduce_unit(mn, mg % 2, idx)
                        if idx == 8 and en is not None and not first_exp:
                            normalise(en - 1, pb, (eg - 1) % 4, 1)
                        if idx == 32 and en is not None:
                            normalise(en, eb, eg, 0)
                    combine(mn, mg % 2)
                else:
                    normalise(en - 1, pb, (eg - 1) % 4, 1)
                    normalise(en, eb, eg, 0)

            step(0, 0, None, None, None, None)
            step(1, 1, None, None, None, None)
            step(2, 2, 0, 0, 0, None, first_exp=True)
            step(3, 3, 1, 0, 1, 0)
            B_CHAIN = 8
            base = chain.base + chain.n
            with dve.Fori(1, NB) as b:
                chain.base, chain.n = base + B_CHAIN * (b - 1), 0
                for g in range(HG):
                    step(4 * b + g, g, 4 * b + g - 2, b - 1 if g < 2 else b, (g + 2) % 4,
                         b - 1 if g < 3 else b)
                assert chain.n == B_CHAIN, chain.n
            chain.base, chain.n = base + B_CHAIN * (NB - 1), 0
            step(None, None, 4 * NB - 2, NB - 1, 2, NB - 1)
            step(None, None, 4 * NB - 1, NB - 1, 3, NB - 1)
            normalise(4 * NB - 1, NB - 1, 3, 1)

            C_CHAIN = 30
            base = chain.base + chain.n
            with dve.Fori(0, 2) as i:
                chain.base, chain.n = base + C_CHAIN * i, 0

                def moments(u, src):
                    for r in range(CH):
                        last = V.bn_stats(stc[u][:, r, :], src[:, r, :])
                    chain.link(last)
                    merge_halves(mvc[u], stc[u], hvc[u]).then_inc(s_varc[u], 1)

                def normal(u, src, count, free, signal):
                    dve.wait_ge(s_sdc[u], count)
                    dve.wait_ge(s_varc[u], count)
                    chain.link(V.reciprocal(scc[u][:, 1, :], scc[u][:, 0, :]))
                    free()
                    for r in range(CH):
                        last = V.tensor_scalar(zz[u][:, r, :], src[:, r, :], mvc[u][:, r, 0:1],
                                               scc[u][:, 1, r:r + 1], ALU.subtract, ALU.mult)
                    last.then_inc(signal, 1)

                for u in range(2):
                    dve.wait_ge(s_pj[u], i + 1)
                    V.tensor_tensor(x2[u][:, :, :], x1[:, 2 * i + u, :, :],
                                    banks(4 * u + 2, 2).rearrange("p (r d) -> p r d", d=D), ALU.add
                                    ).then_inc(s_x2[u], 1)
                for u in range(2):
                    dve.wait_ge(s_x2[u], i + 1)
                    moments(u, x2[u])
                for u in range(2):
                    normal(u, x2[u], 2 * i + 1, lambda: dve.wait_ge(s_out[u], 16 * i + OUT_CREDIT), s_zz[u])
                for u in range(2):
                    dve.wait_ge(s_lg[u], i + 1)
                    lg = ps[:, 4 * u + 2, 0:CH * NE].rearrange("p (r e) -> p r e", e=NE)
                    pk = pick[u]
                    chain.link(V.tensor_reduce(lmax[u][:, :], lg, AX_X, ALU.max))
                    chain.link(V.tensor_tensor(pk[:, :, :], lg, lmax[u][:, :].unsqueeze(2).broadcast_to([P, CH, NE]),
                                               ALU.is_ge))
                    chain.link(V.tensor_scalar(left[u][:, :], pk[:, :, 0], -1.0, 1.0, ALU.mult, ALU.add))
                    for e in range(1, NE):
                        ins = V.tensor_tensor(pk[:, :, e], pk[:, :, e], left[u][:, :], ALU.mult)
                        if e == NE - 1:
                            ins.then_inc(s_pk[u], 1)
                        else:
                            chain.link(ins)
                            chain.link(V.tensor_tensor(left[u][:, :], left[u][:, :], pk[:, :, e], ALU.subtract))

                def add(c):
                    u, e, ch = c // (2 * NE), c // 2 % NE, c % 2
                    dve.wait_ge(s_yy, CHUNKS * i + c + 1)
                    dve.wait_ge(s_ya, CHUNKS * i + c + YA_CREDIT)
                    if c == 0:
                        for w in range(2):
                            dve.wait_ge(s_acc[w], i + 1)
                            dve.wait_ge(s_pk[w], i + 1)
                    for r in range(4):
                        last = V.scalar_tensor_tensor(
                            out=acc[u][:, 4 * ch + r, :], in0=ps[:, 6 + c % 2, r * P:(r + 1) * P],
                            scalar=pick[u][:, 4 * ch + r, e:e + 1], in1=acc[u][:, 4 * ch + r, :],
                            op0=ALU.mult, op1=ALU.add)
                    last.then_inc(s_ya, 1)

                for c in range(CHUNKS):
                    for f in range(FT):
                        idx = FT * c + f
                        dve.wait_ge(s_sg, UNITS * i + idx + 1)
                        if f == 0 and c >= 2:
                            dve.wait_ge(s_yy, CHUNKS * i + c - 1)
                        V.tensor_tensor(act_v[c % 2][:, f, :], ps[:, 2 * (idx % 3) + 1, :], gate[idx % 3][:, :],
                                        ALU.mult).then_inc(s_av, 1)
                        if f == 2 and c:
                            add(c - 1)
                add(CHUNKS - 1)
                dve.wait_ge(s_ya, CHUNKS * (i + 1) + YA_CREDIT)
                for u in range(2):
                    moments(u, acc[u])
                for u in range(2):
                    normal(u, acc[u], 2 * i + 2, lambda: None, s_res[u])
                assert chain.n == C_CHAIN, chain.n

        @block.gpsimd
        def _(pool):
            G_ = nc.gpsimd
            for u in range(2):
                pool.sem_inc(s_otr[u], OTR_CREDIT)
                pool.sem_inc(s_out[u], OUT_CREDIT)
            G_.memset(ones[:, :], 1.0).then_inc(s_pool, 1)
            G_.memset(v_all[:, :, :, :, :].rearrange("p b t h c -> p (b t h c)"), 1.0).then_inc(s_pool, 1)
            pool.wait_ge(s_weights, 16 * 10)
            for k in range(2):
                w = w_qkv[:, k * D:(k + 1) * D].rearrange("c (h a d) -> c h a d", a=2, d=HD // 2)
                r = w_rot[:, k * D:(k + 1) * D].rearrange("c (h a d) -> c h a d", a=2, d=HD // 2)
                G_.tensor_copy(r[:, :, 0, :], w[:, :, 1, :])
                G_.tensor_copy(r[:, :, 1, :], w[:, :, 0, :])
            pool.wait_ge(s_set_act, 2)
            G_.tensor_copy(decay[:, :, :], ph[:, CH - 1, :].unsqueeze(2).broadcast_to([P, G, P])
                           ).then_inc(s_pool, 1)
            pool.wait_ge(s_pool, 3)
            G_.memset(decay[:, :, 0:1], 0.0).then_inc(s_set_pool, 1)

            with pool.Fori(0, 2) as i:
                for u in range(2):
                    pool.wait_ge(s_x1[u], i + 1)
                    G_.tensor_tensor(hz[u][:, :, :], x1[:, 2 * i + u, :, :],
                                     sc[u][:, 5, :].unsqueeze(2).broadcast_to([P, CH, D]), ALU.mult
                                     ).then_inc(s_hz[u], 1)
                for k in range(2):
                    for u in range(2):
                        m = 2 * i + u
                        pool.wait_ge(s_rope[u], 2 * i + k + 1 + ROPE_CREDIT)
                        G_.tensor_tensor(tq[k][:, :], tq[k][:, :], tr[k][:, :], ALU.add).then_inc(s_sum[k], 1)
                        pool.wait_ge(s_sum[k], m + 1)
                        pool.wait_ge(s_cast1[k], m + 1)
                        G_.tensor_tensor(tr[k][:, :], tq[k][:, :], part[k][0][:, :], ALU.subtract
                                         ).then_inc(s_rest1[k], 1)
                        pool.wait_ge(s_rest1[k], m + 1)
                        pool.wait_ge(s_cast2[k], m + 1)
                        G_.tensor_tensor(part[k][2][:, :], tr[k][:, :], part[k][1][:, :], ALU.subtract
                                         ).then_inc(s_cast3[k], 1)

            for k in range(2):
                pool.wait_ge(s_stored[k], 16 * 3 * NB + STORED_CREDIT)
            for u in range(2):
                pool.wait_ge(s_vc[u], 2 + VC_CREDIT)
            for g in range(HG):
                G_.memset(qs[g][:, :, :].rearrange("p h t -> p (h t)").bitcast(F32), 0.0)
            G_.memset(vs[0][:, :, :, :].rearrange("p t h c -> p (t h c)"), 0.0)
            G_.memset(vs[1][:, :, :, :].rearrange("p t h c -> p (t h c)"), 0.0).then_inc(s_clear, 1)
            pool.wait_ge(s_clear, 2)

            def values(n, b, g):
                pool.wait_ge(s_clear, 2)
                G_.tensor_copy(vs[g % 2][:, :, :, 0:VC], v_all[:, b, :, 4 * g:4 * g + 4, :]
                               ).then_inc(s_vst, 1)

            def max_parts(n, first=False):
                pool.wait_ge(s_mn, n + 1)
                if not first:
                    pool.wait_ge(s_mrow, MROW * n)
                G_.tensor_tensor(m_part[0][:, :], m_neg[:, :], ones[:, :], ALU.mult).then_inc(s_mpc, 1)
                pool.wait_ge(s_mpc, 3 * n + 1)
                G_.tensor_tensor(m_res[:, :], m_neg[:, :], m_part[0][:, :], ALU.subtract).then_inc(s_mpc, 1)
                pool.wait_ge(s_mpc, 3 * n + 2)
                G_.tensor_tensor(m_part[1][:, :], m_res[:, :], ones[:, :], ALU.mult).then_inc(s_mpc, 1)
                pool.wait_ge(s_mpc, 3 * n + 3)
                G_.tensor_tensor(m_part[2][:, :], m_res[:, :], m_part[1][:, :], ALU.subtract).then_inc(s_mp, 1)

            values(0, 0, 0)
            values(1, 0, 1)
            for g in range(HG):
                if g >= 2:
                    pool.wait_ge(s_pv, NEU * (g - 1) + PV_CREDIT)
                    values(g, 0, g)
                max_parts(g, first=(g == 0))
            with pool.Fori(1, NB) as b:
                for g in range(HG):
                    n = 4 * b + g
                    pool.wait_ge(s_pv, NEU * (n - 1) + PV_CREDIT)
                    values(n, b, g)
                    max_parts(n)

            with pool.Fori(0, 2) as i:
                for u in range(2):
                    pool.wait_ge(s_otr[u], i + OTR_CREDIT)
                    pool.wait_ge(s_on, 2 * 4 * NB)
                    G_.tensor_copy(o_in[u][:, :, :], o_all[:, 2 * i + u, :, :]).then_inc(s_oin[u], 1)
                for u in range(2):
                    pool.wait_ge(s_x2[u], i + 1)
                    G_.tensor_tensor(acc[u][:, :, :], x1[:, 2 * i + u, :, :], x2[u][:, :, :], ALU.add
                                     ).then_inc(s_acc[u], 1)


_INS = ["L0_attn_x", "L0_attn_log_A_diag", "L0_attn_B_w", "L0_attn_C_w", "L0_attn_D_vec", "L0_ffn_ln1_w",
        "L0_ffn_ln1_b", "L0_ffn_ln2_w", "L0_ffn_ln2_b", "L0_ffn_conv_w", "L0_ffn_attn_w", "L0_ffn_proj_w",
        "L0_ffn_router_w", "L0_ffn_expert_wv", "L0_ffn_expert_proj"]
_OUTS = [((NB, T, D), "float32")]


def kernel(**inputs):
    import numpy as _np
    import concourse.bacc as _bacc
    from concourse import mybir as _mybir
    from concourse.bass_utils import run_bass_kernel_spmd as _run

    nc = _bacc.Bacc("TRN2", target_bir_lowering=False, num_devices=1)
    arrays, args = {}, []
    for name, a in [("constants", constants())] + [(n, inputs[n]) for n in _INS]:
        a = _np.ascontiguousarray(a)
        arrays[f"in_{name}_dram"] = a
        args.append(nc.dram_tensor(f"in_{name}_dram", a.shape, _mybir.dt.from_np(a.dtype), kind="ExternalInput").ap())
    for i, (shape, dtype) in enumerate(_OUTS):
        dt = _mybir.dt.from_np(_np.dtype(dtype))
        args.append(nc.dram_tensor(f"out_{i}_dram", shape, dt, kind="ExternalOutput").ap())
    layer_kernel(nc, *args)
    r = _run(nc, [arrays], core_ids=[0])
    return r.results[0]["out_0_dram"]
```

```python
from contextlib import ExitStack

import numpy as np
import concourse.bass as bass
from concourse import mybir

F32 = mybir.dt.float32
BF16 = mybir.dt.bfloat16
U32 = mybir.dt.uint32
ALU = mybir.AluOpType
ACT = mybir.ActivationFunctionType
AX_X = mybir.AxisListType.X

P = 128
NB = 4
T = 1024
D = 128
S = 16
CH = 8
G = D * S // P
NH = 16
HD = 8
HG = 4
KT = T // P
NE = 4
DFF = 512
FT = DFF // P
EPS = 1e-5
TILES = NB * KT + NE
REGION = NB * T + P
ROWS = NE * REGION + NE * P
DI = D + 1
WE = 2 * DFF + FT * D
MASKED = -1e30
RATE_MAX = 1e4
SCALE = float(1.0 / np.sqrt(np.float32(HD)))
VC = 9
VW = 32

C_IDENT, C_MASKQ, C_MASKK = 0, P, 2 * P
C_COS, C_SIN = 3 * P, 3 * P + T
C_DS = C_SIN + T
C_DD = C_DS + S
C_PU = C_DD + 8
C_PI = C_PU + 1
C_CM = C_PI + CH
C_ONE = C_CM + CH
C_LOW = C_ONE + P
C_K = C_LOW + P
C_TI = C_K + NB * KT
C_ER = C_TI + TILES
C_P = C_ER + NE
C_ID = C_P + 1
C_IDZ = C_ID + NB * CH
C_ALL = C_IDZ + 2 * NE


def constants():
    c = np.zeros((P, C_ALL), np.float32)
    n = np.arange(P)
    c[:, C_IDENT:C_IDENT + P] = np.eye(P)
    c[:, C_MASKQ:C_MASKQ + P] = np.where(n[None, :] > n[:, None], MASKED, 0.0)
    c[:, C_MASKK:C_MASKK + P] = np.where(n[:, None] > n[None, :], MASKED, 0.0)
    inv = (1.0 / 10000.0 ** (np.arange(0, HD, 2, dtype=np.float32) / HD)).astype(np.float32)
    freq = np.arange(T, dtype=np.float32)[None, :] * inv[:, None]
    d = n % HD
    c[:, C_COS:C_COS + T] = np.cos(freq)[d % (HD // 2)]
    c[:, C_SIN:C_SIN + T] = np.sin(freq)[d % (HD // 2)] * np.where(d < HD // 2, -1, 1)[:, None]
    c[:, C_DS:C_DS + S] = (n % S)[:, None] == np.arange(S)[None, :]
    c[:, C_DD:C_DD + 8] = (n // S)[:, None] == np.arange(8)[None, :]
    j = n // S
    r = np.arange(CH)
    c[:, C_PU] = -(CH - 1 - j)
    c[:, C_PI:C_PI + CH] = -np.maximum(r[None, :] - j[:, None], 0)
    c[:, C_CM:C_CM + CH] = r[None, :] >= j[:, None]
    c[:, C_ONE:C_ONE + P] = 1.0
    c[:, C_LOW:C_LOW + P] = n[:, None] < n[None, :]
    c[:, C_K:C_K + NB * KT] = P * np.arange(NB * KT)
    c[:, C_TI:C_TI + TILES] = np.arange(TILES)
    c[:, C_ER:C_ER + NE] = REGION * np.arange(NE) - 1
    c[:, C_P] = n
    c[:, C_ID:C_ID + NB * CH] = (np.arange(NB)[None, :, None] * T + CH * n[:, None, None]
                                 + np.arange(CH)[None, None, :]).reshape(P, NB * CH)
    c[:, C_IDZ:C_IDZ + 2 * NE] = NB * T + n[:, None] + P * np.arange(2 * NE)[None, :]
    return c


class Chain:

    def __init__(self, eng, sem):
        self.eng, self.sem, self.base, self.n = eng, sem, 0, 0

    def done(self, ins):
        ins.then_inc(self.sem, 1)
        self.n += 1

    def sync(self):
        self.eng.wait_ge(self.sem, self.base + self.n)

    def link(self, ins):
        self.done(ins)
        self.sync()


def max_units():
    out = []
    for t in range(KT):
        for chunk in range(2 if t >= 4 else 1):
            n = min(P * (t + 1) - 512 * chunk, 512)
            k = 4 if n == 128 else 2 if n == 256 else 1
            out += [(t, 512 * chunk, n, tuple(range(h, h + k)), chunk) for h in range(0, 4, k)]
    return out


def exp_units():
    out = []
    for half in range(2):
        for j in range(4 * (half + 1)):
            q0 = max(P * j, 512 * half)
            n = 512 * (half + 1) - q0
            k = 4 if n <= 256 else 2
            out += [(half, j, q0, n, tuple(range(h, h + k))) for h in range(0, 4, k)]
    return out


MAXU = max_units()
EXPU = exp_units()


def place(n, heads, i):
    at = heads.index(i)
    per = 4 if n == 128 else 2 if n == 256 else 1
    return at // per, (at % per) * n


def layer_kernel(nc, const, x, log_a, b_w, c_w, d_vec, ln1_w, ln1_b, ln2_w, ln2_b, conv_w,
                 attn_w, proj_w, router_w, expert_wv, expert_proj, out):
    ctx = ExitStack()
    with ctx:
        def sb(name, shape, dt=F32):
            return ctx.enter_context(nc.sbuf_tensor(name, shape, dt))

        def sem(name):
            return ctx.enter_context(nc.semaphore(name))

        cst = sb("cst", [P, C_COS])
        small = sb("small", [P, C_ALL - C_DS])

        def con(at, n):
            return small[:, at - C_DS:at - C_DS + n]

        ident = cst[:, C_IDENT:C_IDENT + P]
        ident_b = sb("ident_b", [P, P], BF16)
        mask_q = sb("mask_q", [P, P], BF16)
        mask_k = sb("mask_k", [P, P], BF16)
        w_qkv = sb("w_qkv", [P, 3 * D])
        w_rot = sb("w_rot", [P, 2 * D])
        w_proj = sb("w_proj", [P, D])
        w_router = sb("w_router", [P, NE])
        vecs = sb("vecs", [P, 8])
        x1 = sb("x1", [P, NB, CH, D])
        v_all = sb("v_all", [P, NB, KT, NH, VC])
        o_all = sb("o_all", [P, NB, KT, D])
        eps_t = sb("eps_t", [P, 1])
        ones = sb("ones", [32, P])
        zero3 = sb("zero3", [3, T], BF16)
        region = nc.sbuf_base + 64 - nc.sbuf_base % 64

        class Region:

            def __init__(self):
                self.at = region

            def __call__(self, name, shape, dt=F32):
                size = int(np.prod(shape[1:])) * (2 if dt == BF16 else 4)
                t = nc.alloc_sbuf_tensor_at(name, shape, dt, offset=self.at)
                self.at += -(-size // 64) * 64
                assert self.at <= nc.sbuf_usable_end, (name, self.at)
                return t

        ra = Region()
        cos = ra("cos", [P, T])
        sin = ra("sin", [P, T])
        w_state = ra("w_state", [P, D, S])
        w_carry = ra("w_carry", [P, G, CH, 8])
        w_chunk = ra("w_chunk", [P, CH, D])
        decay = ra("decay", [P, G, P])
        b_pad = ra("b_pad", [P, 240])
        diag_d = ra("diag_d", [P, P])
        xt = [ra(f"xt{u}", [P, CH, D]) for u in range(2)]
        xT = [ra(f"xT{u}", [P, CH, P]) for u in range(2)]
        bt = [ra(f"bt{u}", [P, P]) for u in range(2)]
        hs = [ra(f"hs{u}", [P, G * P + 16]) for u in range(2)]
        hz = [ra(f"hz{u}", [P, CH, D]) for u in range(2)]
        hT = [ra(f"hT{u}", [P, T + 2]) for u in range(2)]
        hc = [ra(f"hc{u}", [P, T]) for u in range(2)]
        tq = [ra(f"tq{k}", [P, T]) for k in range(2)]
        tr = [ra(f"tr{k}", [P, T]) for k in range(2)]
        part = [[ra(f"part{k}_{j}", [P, T], BF16) for j in range(3)] for k in range(2)]
        st = [ra(f"st{u}", [P, CH, 6]) for u in range(2)]
        mv = [ra(f"mv{u}", [P, CH, 2]) for u in range(2)]
        hv = [ra(f"hv{u}", [P, 4, CH]) for u in range(2)]
        sc = [ra(f"sc{u}", [P, 8, CH]) for u in range(2)]
        lg_d = ra("lg_d", [P, S])
        cw_d = ra("cw_d", [P, S])
        lg_g = ra("lg_g", [G, P])
        cw_g = ra("cw_g", [G, P])
        bw_s = ra("bw_s", [S, P])
        dv = ra("dv", [P, 1])
        a_rep = ra("a_rep", [P, CH, S])
        c_rep = ra("c_rep", [P, CH, S])
        aT = ra("aT", [P, P])
        cT = ra("cT", [P, P])
        aG = ra("aG", [P, G])
        cG = ra("cG", [P, G])
        pu = ra("pu", [P, P])
        pi = ra("pi", [P, CH, D])
        ph = ra("ph", [P, CH, G])
        phc = ra("phc", [P, CH, G])

        rb = Region()
        qs = [rb(f"qs{g}", [P, 4, T], BF16) for g in range(HG)]
        ks = [rb(f"ks{g}", [P, 4, T], BF16) for g in range(HG)]
        vs = [rb(f"vs{g}", [P, KT, 4, VW]) for g in range(2)]
        pT = [rb(f"pT{n}", [P, T]) for n in range(4)]
        oT = [rb(f"oT{n}", [P, 512]) for n in range(2)]
        mx = [rb(f"mx{n}", [P, 4, KT]) for n in range(2)]
        mxb = [rb(f"mxb{n}", [P, 4, 4]) for n in range(2)]
        m_neg = rb("m_neg", [32, P])
        m_res = rb("m_res", [32, P])
        m_part = [rb(f"m_part{j}", [32, P], BF16) for j in range(3)]
        rden = [rb(f"rden{n}", [P, 4, 4]) for n in range(2)]

        w_exp = rb("w_exp", [P, NE, WE])

        rc = Region()
        o_in = [rc(f"o_in{u}", [P, KT, D]) for u in range(2)]
        ocT = [rc(f"ocT{u}", [P, P, CH]) for u in range(2)]
        x2 = [rc(f"x2{u}", [P, CH, D]) for u in range(2)]
        zz = [rc(f"zz{u}", [P, CH, DI]) for u in range(2)]
        h2T = [rc(f"h2T{u}", [P, CH, P]) for u in range(2)]
        stc = [rc(f"stc{u}", [P, CH, 6]) for u in range(2)]
        mvc = [rc(f"mvc{u}", [P, CH, 2]) for u in range(2)]
        hvc = [rc(f"hvc{u}", [P, 4, CH]) for u in range(2)]
        scc = [rc(f"scc{u}", [P, 4, CH]) for u in range(2)]
        lmax = [rc(f"lmax{u}", [P, CH]) for u in range(2)]
        pick = [rc(f"pick{u}", [P, CH, NE]) for u in range(2)]
        left = [rc(f"left{u}", [P, CH]) for u in range(2)]
        rowc = [rc(f"rowc{u}", [P, NE]) for u in range(2)]
        incl = [rc(f"incl{u}", [P, CH, NE]) for u in range(2)]
        offs = [rc(f"offs{u}", [P, NE]) for u in range(2)]
        rank = [rc(f"rank{u}", [P, CH]) for u in range(2)]
        count = rc("count", [P, NE])
        zero8 = rc("zero8", [P, CH])
        dest = rc("dest", [P, NB, CH], U32)
        dest_now = [rc(f"dest_now{u}", [P, CH], U32) for u in range(2)]
        tail = rc("tail", [P, NE], U32)
        zrow = rc("zrow", [P, 2 * NE, DI])
        above = rc("above", [P, NE, NB * KT])
        tiles_e = rc("tiles_e", [P, NE])
        cum_e = rc("cum_e", [P, NE])
        jump_e = rc("jump_e", [P, NE])
        past = rc("past", [P, TILES, NE])
        past_j = rc("past_j", [P, TILES, NE])
        tile_f = rc("tile_f", [P, 2, TILES])
        tile_expert = rc("tile_expert", [P, TILES], U32)
        tile_row = rc("tile_row", [P, TILES], U32)
        h_row = [rc(f"h_row{k}", [P, DI]) for k in range(4)]
        hT_t = [rc(f"hT_t{k}", [P, P]) for k in range(2)]
        gate = [rc(f"gate{k}", [P, DFF]) for k in range(2)]
        act_v = [rc(f"act_v{k}", [P, DFF]) for k in range(2)]
        act_T = [rc(f"act_T{k}", [P, FT, P]) for k in range(2)]
        y_row = [rc(f"y_row{k}", [P, D]) for k in range(4)]
        y_id = [rc(f"y_id{k}", [P, 1], U32) for k in range(4)]
        yg = rc("yg", [P, NB, CH, D])
        assert rc.at <= rb.at - 4 * NE * WE

        ps = ctx.enter_context(nc.psum_tensor("ps", [P, 8, 512], F32))

        def banks(a, n):
            return ps[:, a:a + n, :].rearrange("p a c -> p (a c)")

        q_parts = nc.dram_tensor("q_parts", (NB, NH, 3, HD, T), BF16, kind="Internal").ap()
        k_parts = nc.dram_tensor("k_parts", (NB, NH, 3, HD, T), BF16, kind="Internal").ap()

        h_sorted = nc.dram_tensor("h_sorted", (ROWS, DI), F32, kind="Internal").ap()
        y_rows = nc.dram_tensor("y_rows", (NB * T + 2 * NE * P, D), F32, kind="Internal").ap()

        x_v = x.rearrange("b (p r) d -> b p r d", r=CH)
        out_v = out.rearrange("b (p r) d -> b p r d", r=CH)

        s_params = sem("params_loaded")
        s_weights = sem("weights_loaded")
        s_experts = sem("experts_loaded")
        s_set_act = sem("setup_act")
        s_set_dve = sem("setup_dve")
        s_set_pool = sem("setup_pool")
        s_set_pe = sem("setup_pe")
        s_x = [sem(f"x_loaded{u}") for u in range(2)]
        s_xtr = [sem(f"x_transposed{u}") for u in range(2)]
        s_xTa = [sem(f"xT_copied_act{u}") for u in range(2)]
        s_xTd = [sem(f"xT_copied_dve{u}") for u in range(2)]
        s_bt = [sem(f"inputs_projected{u}") for u in range(2)]
        s_btc = [sem(f"inputs_copied{u}") for u in range(2)]
        s_u = [sem(f"chunk_states_ready{u}") for u in range(2)]
        s_scan = [sem(f"states_scanned{u}") for u in range(2)]
        s_y = [sem(f"mixer_ready{u}") for u in range(2)]
        s_var = [sem(f"variance_ready{u}") for u in range(2)]
        s_sd = [sem(f"deviation_ready{u}") for u in range(2)]
        s_x1 = [sem(f"x1_ready{u}") for u in range(2)]
        s_hz = [sem(f"hz_ready{u}") for u in range(2)]
        s_hzt = [sem(f"hz_transposed{u}") for u in range(2)]
        s_hT = [sem(f"hT_ready{u}") for u in range(2)]
        s_hc = [sem(f"conv_ready{u}") for u in range(2)]
        s_qk = [sem(f"qk_projected{u}") for u in range(2)]
        s_rope = [sem(f"qk_turned{u}") for u in range(2)]
        s_v = [sem(f"v_projected{u}") for u in range(2)]
        s_vc = [sem(f"v_copied{u}") for u in range(2)]
        s_sum = [sem(f"qk_summed{k}") for k in range(2)]
        s_cast1 = [sem(f"part1_ready{k}") for k in range(2)]
        s_rest1 = [sem(f"rest1_ready{k}") for k in range(2)]
        s_cast2 = [sem(f"part2_ready{k}") for k in range(2)]
        s_cast3 = [sem(f"part3_ready{k}") for k in range(2)]
        s_stored = [sem(f"parts_stored{k}") for k in range(2)]
        s_dve = sem("dve_step")
        s_pool = sem("pool_step")
        s_clear = sem("slots_cleared")
        s_stage = [sem(f"slot_staged{g}") for g in range(HG)]
        s_mrow = sem("max_rows_written")
        s_vst = sem("values_staged")
        s_ms = sem("max_scores_ready")
        s_mr = sem("max_reduced")
        s_mg = sem("group_maxima_ready")
        s_mt = sem("maxima_transposed")
        s_mn = sem("maxima_negated")
        s_mpc = sem("max_part_steps")
        s_mp = sem("max_parts_ready")
        s_es = sem("exp_scores_ready")
        s_ex = sem("exp_done")
        s_pv = sem("unit_weighted")
        s_oc = sem("half_copied")
        s_ot = sem("half_transposed")
        s_on = sem("half_normalised")
        s_oin = [sem(f"o_staged{u}") for u in range(2)]
        s_otr = [sem(f"o_transposed{u}") for u in range(2)]
        s_oca = [sem(f"ocT_copied{u}") for u in range(2)]
        s_pj = [sem(f"projected{u}") for u in range(2)]
        s_x2 = [sem(f"x2_ready{u}") for u in range(2)]
        s_acc = [sem(f"acc_started{u}") for u in range(2)]
        s_varc = [sem(f"variance2_ready{u}") for u in range(2)]
        s_sdc = [sem(f"deviation2_ready{u}") for u in range(2)]
        s_zz = [sem(f"zz_ready{u}") for u in range(2)]
        s_zt = [sem(f"zz_transposed{u}") for u in range(2)]
        s_h2 = [sem(f"h2T_ready{u}") for u in range(2)]
        s_lg = [sem(f"logits_ready{u}") for u in range(2)]
        s_pk = [sem(f"experts_picked{u}") for u in range(2)]
        s_rc = [sem(f"rows_counted{u}") for u in range(2)]
        s_rp = [sem(f"ranks_ready{u}") for u in range(2)]
        s_dest = [sem(f"rows_chosen{u}") for u in range(2)]
        s_scat = [sem(f"tokens_scattered{u}") for u in range(2)]
        s_zfree = [sem(f"zz_free{u}") for u in range(2)]
        s_plan = sem("tiles_planned")
        s_tail = sem("tails_cleared")
        s_zrow = sem("zeros_ready")
        s_ysc = sem("expert_out_released")
        s_id = sem("token_numbers_kept")
        s_aT = sem("activations_transposed")
        s_aTc = sem("activations_turned")
        s_zero = sem("spare_rows_cleared")
        s_hrow = [sem(f"tokens_loaded{k}") for k in range(4)]
        s_tT = sem("tokens_transposed")
        s_hTt = sem("tokens_turned")
        s_gv = sem("gate_value_ready")
        s_sg = sem("gate_silu_ready")
        s_av = sem("activations_ready")
        s_yy = sem("expert_out_ready")
        s_yr = sem("expert_out_copied")
        s_yst = [sem(f"expert_out_stored{k}") for k in range(4)]
        s_yg = [sem(f"expert_out_loaded{u}") for u in range(2)]
        s_fin = [sem(f"sum_ready{u}") for u in range(2)]
        s_res = [sem(f"result_ready{u}") for u in range(2)]
        s_out = [sem(f"result_stored{u}") for u in range(2)]

        block = ctx.enter_context(nc.Block())

        VC_CREDIT = ROPE_CREDIT = CAST3_CREDIT = 1
        STORED_CREDIT = 16
        MR_CREDIT, EX_CREDIT, PV_CREDIT, OC_CREDIT, OT_CREDIT = 2, 2, 4, 1, 2
        OTR_CREDIT, OUT_CREDIT, ZFREE_CREDIT, PK_CREDIT, RES_CREDIT = 1, 16, 1, 1, 1
        NMU, NEU = len(MAXU), len(EXPU)
        STAGE = 16 * 13
        MROW = 16 * 3
        HALF0 = sum(1 for e in EXPU if e[0] == 0)

        def tile_turn(k, slot):
            if isinstance(k, int):
                return 16 * (k // 4 + 1)
            return 4 * (k - slot) + 16

        @block.sync
        def _(sp):
            for dst, src in (
                (cst[:, :], const[:, 0:C_COS]), (small[:, :], const[:, C_DS:C_ALL]),
                (lg_d[:, :], log_a), (cw_d[:, :], c_w),
                (lg_g[:, :], log_a.rearrange("(g e) s -> g (e s)", e=8)),
                (cw_g[:, :], c_w.rearrange("(g e) s -> g (e s)", e=8)),
                (bw_s[:, :], b_w), (dv[:, :], d_vec.rearrange("(d o) -> d o", o=1)),
            ):
                sp.dma_start(dst, src).then_inc(s_params, 16)
            for u in range(2):
                sp.dma_start(xt[u][:, :, :], x_v[u]).then_inc(s_x[u], 16)
            for dst, src in (
                (w_qkv[:, :], attn_w), (cos[:, :], const[:, C_COS:C_COS + T]),
                (sin[:, :], const[:, C_SIN:C_SIN + T]),
                (w_proj[:, :], proj_w), (w_router[:, :], router_w),
                (vecs[:, 0:1], ln1_w.rearrange("(d o) -> d o", o=1)),
                (vecs[:, 1:2], ln1_b.rearrange("(d o) -> d o", o=1)),
                (vecs[:, 2:3], ln2_w.rearrange("(d o) -> d o", o=1)),
                (vecs[:, 3:4], ln2_b.rearrange("(d o) -> d o", o=1)),
                (vecs[:, 4:7], conv_w.rearrange("c o k -> c (o k)")),
            ):
                sp.dma_start(dst, src).then_inc(s_weights, 16)
            for u in range(2):
                sp.wait_ge(s_xtr[u], 1)
                sp.dma_start(xt[u][:, :, :], x_v[2 + u]).then_inc(s_x[u], 16)

            with sp.Fori(0, 2) as i:
                for k, dram in ((0, q_parts), (1, k_parts)):
                    for u in range(2):
                        for j, s, credit in ((0, s_cast1, 0), (1, s_cast2, 0), (2, s_cast3, CAST3_CREDIT)):
                            sp.wait_ge(s[k], 2 * i + u + 1 + credit)
                            dst = dram[2 * i + u].rearrange("h j d t -> j h d t")[j]
                            sp.dma_start(dst, part[k][j][:, :]
                                         ).then_inc(s_stored[k], 16)

            for k in range(2):
                sp.wait_ge(s_stored[k], 16 * 3 * NB + STORED_CREDIT)
            sp.wait_ge(s_clear, 2)

            def stage(b, g):
                q_g = q_parts[b].rearrange("h j d t -> (j d) h t")[:, 4 * g:4 * g + 4, :]
                k_g = k_parts[b].rearrange("h j d t -> (j d) h t")[:, 4 * g:4 * g + 4, :]
                for i in range(3):
                    sp.dma_start(qs[g][24 * i:24 * i + 24, :, :], q_g).then_inc(s_stage[g], 16)
                    for j in range(3):
                        at = 24 * i + 8 * j
                        sp.dma_start(ks[g][at:at + 8, :, :], k_g[8 * i:8 * i + 8]).then_inc(s_stage[g], 16)
                sp.dma_start(qs[g][96:99, :, :], zero3[:, :].unsqueeze(1).broadcast_to([3, 4, T])
                             ).then_inc(s_stage[g], 16)

            def max_rows(n, g):
                sp.wait_ge(s_mp, n + 1)
                for j in range(3):
                    sp.dma_start(qs[g][96 + j:97 + j, :, :], m_part[j][:, :]).then_inc(s_mrow, 16)

            for g in range(HG):
                stage(0, g)
                if g == 1:
                    for e in range(NE):
                        sp.dma_start(w_exp[:, e, 0:2 * DFF], expert_wv[e]).then_inc(s_experts, 16)
                        sp.dma_start(w_exp[:, e, 2 * DFF:WE].rearrange("p (f d) -> p f d", d=D),
                                     expert_proj[e].rearrange("(f p) d -> p f d", p=P)
                                     ).then_inc(s_experts, 16)

            for g in range(HG):
                if g >= 1:
                    max_rows(g - 1, g - 1)
                if g >= 2:
                    sp.wait_ge(s_es, NEU * (g - 1))
                    stage(1, g - 2)
            with sp.Fori(1, NB - 1) as b:
                for g in range(HG):
                    max_rows(4 * b + g - 1, (g + 3) % 4)
                    sp.wait_ge(s_es, NEU * (4 * b + g - 1))
                    stage(b + 1 if g >= 2 else b, (g + 2) % 4)
            for g in range(HG):
                n = 4 * (NB - 1) + g
                max_rows(n - 1, (g + 3) % 4)
                if g < 2:
                    sp.wait_ge(s_es, NEU * (n - 1))
                    stage(NB - 1, g + 2)
            max_rows(4 * NB - 1, 3)

            sp.wait_ge(s_zrow, 1)
            sp.dma_start(h_sorted[NE * REGION:ROWS, :].rearrange("(e p) d -> p e d", p=P),
                         zrow[:, NE:2 * NE, :]).then_inc(s_zero, 16)
            sp.wait_ge(s_zero, 16)
            sp.wait_ge(s_plan, 1)
            for u in range(2):
                sp.wait_ge(s_scat[u], 16 * 2 * CH)
            sp.wait_ge(s_tail, 16 * NE)

            def load_tile(k, slot, wait=True):
                if wait:
                    sp.wait_ge(s_tT, k - 3)
                    sp.wait_ge(s_id, k - 3)
                row = sp.value_load(tile_row[0:1, bass.ds(k, 1)], min_val=0, max_val=ROWS - P)
                sp.dma_start(h_row[slot][:, :], h_sorted[bass.ds(row, P), :]).then_inc(s_hrow[slot], 16)

            for k in range(4):
                load_tile(k, k, wait=False)
            with sp.Fori(1, TILES // 4) as m:
                for j in range(4):
                    load_tile(4 * m + j, j)

            for k in range(4):
                sp.wait_ge(s_yst[k], tile_turn(TILES - 4 + k, k))
            for i in range(2):
                for u in range(2):
                    b = 2 * i + u
                    if i > 0:
                        sp.wait_ge(s_yg[u], 16 * i)
                    sp.dma_start(yg[:, b, :, :], y_rows[b * T:(b + 1) * T, :].rearrange("(p r) d -> p r d", r=CH)
                                 ).then_inc(s_yg[u], 16)

            with sp.Fori(0, 2) as i:
                for u in range(2):
                    sp.wait_ge(s_res[u], i + 1 + RES_CREDIT)
                    sp.dma_start(out_v[2 * i + u], zz[u][:, :, 0:D]).then_inc(s_out[u], 16)
            for u in range(2):
                sp.wait_ge(s_out[u], 32 + OUT_CREDIT)

        @block.tensor
        def _(pe):
            mm = nc.tensor.matmul

            def tp(out_, in_, k=P):
                return nc.tensor.transpose(out_, in_, ident[0:k, 0:k])

            pe.sem_inc(s_mr, MR_CREDIT)
            pe.sem_inc(s_ex, EX_CREDIT)
            for u in range(2):
                pe.sem_inc(s_vc[u], VC_CREDIT)
                pe.sem_inc(s_rope[u], ROPE_CREDIT)
            pe.sem_inc(s_oc, OC_CREDIT)
            for u in range(2):
                pe.sem_inc(s_rp[u], PK_CREDIT)

            pe.wait_ge(s_params, 16 * 8)
            tp(ps[:, 0, 0:S], bw_s[:, :], S).then_inc(s_set_pe, 1)
            pe.wait_ge(s_set_dve, 1)
            tp(ps[:, 1, 0:P], a_rep[:, :, :].rearrange("d j s -> d (j s)"))
            tp(ps[:, 1, P:2 * P], c_rep[:, :, :].rearrange("d j s -> d (j s)"))
            tp(ps[:, 2, 0:G], lg_g[:, :], G)
            tp(ps[:, 2, G:2 * G], cw_g[:, :], G).then_inc(s_set_pe, 1)
            pe.wait_ge(s_set_dve, 3)
            pe.wait_ge(s_set_pool, 1)
            pe.wait_ge(s_weights, 16 * 10)

            with pe.Fori(0, 2) as i:
                for u in range(2):
                    pe.wait_ge(s_x[u], 16 * i + 16)
                    pe.wait_ge(s_vc[u], i + VC_CREDIT)
                    for r in range(CH):
                        last = tp(ps[:, 4 * u + r // 4, (r % 4) * P:(r % 4 + 1) * P], xt[u][:, r, :])
                    last.then_inc(s_xtr[u], 1)
                for u in range(2):
                    pe.wait_ge(s_xTa[u], i + 1)
                    pe.wait_ge(s_xTd[u], i + 1)
                    pe.wait_ge(s_rope[u], 2 * i + ROPE_CREDIT)
                    for j in range(CH):
                        last = mm(ps[:, 4 * u + 2, 0:P], b_pad[:, 112 - S * j:240 - S * j], xT[u][:, j, :],
                                  start=(j == 0), stop=(j == CH - 1))
                    last.then_inc(s_bt[u], 1)
                for u in range(2):
                    pe.wait_ge(s_btc[u], i + 1)
                    for g in range(G):
                        last = mm(ps[:, 4 * u + g // 4, (g % 4) * P:(g % 4 + 1) * P],
                                  w_state[:, 8 * g:8 * g + 8, :].rearrange("p d s -> p (d s)"), bt[u][:, :],
                                  start=(g % 4 == 0), stop=True, skip_group_check=True)
                    last.then_inc(s_u[u], 1)
                for u in range(2):
                    pe.wait_ge(s_scan[u], i + 1)
                    for h in range(2):
                        y = ps[:, 4 * u + h, :].rearrange("p (r d) -> p r d", d=D)
                        mm(ps[:, 4 * u + h, :], bt[u][:, :],
                           w_chunk[:, 4 * h:4 * h + 4, :].rearrange("p r d -> p (r d)"),
                           start=True, stop=False, skip_group_check=True)
                        for r in range(4):
                            mm(y[:, r, :], xT[u][:, 4 * h + r, :], diag_d[:, :],
                               start=False, stop=False, skip_group_check=True)
                        for g in range(G):
                            last = mm(y[:, :, 8 * g:8 * g + 8], hs[u][:, g * P:(g + 1) * P],
                                      w_carry[:, g, 4 * h:4 * h + 4, :],
                                      start=False, stop=(g == G - 1), skip_group_check=True)
                    last.then_inc(s_y[u], 1)
                for u in range(2):
                    pe.wait_ge(s_hz[u], i + 1)
                    for r in range(CH):
                        last = tp(ps[:, 4 * u + 2 + r // 4, (r % 4) * P:(r % 4 + 1) * P], hz[u][:, r, :])
                    last.then_inc(s_hzt[u], 1)
                for k in range(2):
                    for u in range(2):
                        if k == 0:
                            pe.wait_ge(s_hc[u], i + 1)
                        else:
                            pe.wait_ge(s_rope[u], 2 * i + 1 + ROPE_CREDIT)
                        for w, at in ((w_qkv, 0), (w_rot, 2)):
                            for h in range(2):
                                last = mm(ps[:, 4 * u + at + h, :], w[:, k * D:(k + 1) * D],
                                          hc[u][:, 512 * h:512 * h + 512], start=True, stop=True)
                        last.then_inc(s_qk[u], 1)
                for u in range(2):
                    pe.wait_ge(s_rope[u], 2 * i + 2 + ROPE_CREDIT)
                    for t in range(KT):
                        last = mm(ps[:, 4 * u + t // 4, (t % 4) * P:(t % 4 + 1) * P],
                                  hc[u][:, t * P:(t + 1) * P], w_qkv[:, 2 * D:3 * D],
                                  start=(t % 4 == 0), stop=True, skip_group_check=True)
                    last.then_inc(s_v[u], 1)

            for u in range(2):
                pe.wait_ge(s_vc[u], 2 + VC_CREDIT)
            MISC, OBANK, MBANK = 5, 4, 6

            def max_unit(n, b, g, idx):
                t, k0, nk, heads, chunk = MAXU[idx]
                bank = MBANK + idx % 2
                if idx == 0:
                    pe.wait_ge(s_stage[g], STAGE * (b + 1))
                pe.wait_ge(s_mr, NMU * n + idx - 1 + MR_CREDIT)
                diag = k0 + nk == P * (t + 1)
                for a, h in enumerate(heads):
                    last = mm(ps[:, bank, a * nk:(a + 1) * nk], qs[g][:, h, t * P:(t + 1) * P],
                              ks[g][:, h, k0:k0 + nk], start=(a == 0),
                              stop=(not diag), skip_group_check=True)
                if diag:
                    m = len(heads)
                    o = ps[:, bank, 0:m * nk].rearrange("p (h k) -> p h k", h=m)[:, :, nk - P:nk]
                    last = mm(o, ident_b[:, :], mask_q[:, :].unsqueeze(1).broadcast_to([P, m, P]),
                              start=False, stop=True, skip_group_check=True)
                last.then_inc(s_ms, 1)

            def exp_unit(n, g, idx):
                half, j, q0, nq, heads = EXPU[idx]
                pair = 2 * (idx % 2)
                if idx == 0:
                    pe.wait_ge(s_mrow, MROW * (n + 1))
                pe.wait_ge(s_ex, NEU * n + idx - 1 + EX_CREDIT)
                diag = q0 == P * j
                for h in heads:
                    bank, col = place(nq, heads, h)
                    first = col == 0
                    last = mm(ps[:, pair + bank, col:col + nq], ks[g][:, h, j * P:(j + 1) * P],
                              qs[g][:, h, q0:q0 + nq], start=first, stop=(not diag), skip_group_check=True)
                if diag:
                    per = 4 if nq == 128 else 2 if nq == 256 else 1
                    for bank in range(len(heads) // per):
                        o = ps[:, pair + bank, 0:per * nq].rearrange("p (h q) -> p h q", h=per)[:, :, 0:P]
                        last = mm(o, ident_b[:, :], mask_k[:, :].unsqueeze(1).broadcast_to([P, per, P]),
                                  start=False, stop=True, skip_group_check=True)
                last.then_inc(s_es, 1)

            def weigh(n, par, idx):
                half, j, q0, nq, heads = EXPU[idx]
                if idx == 0:
                    pe.wait_ge(s_vst, n + 1)
                if j == 0 and heads[0] == 0:
                    pe.wait_ge(s_oc, 2 * n + half + OC_CREDIT)
                pe.wait_ge(s_ex, NEU * n + idx + 1 + EX_CREDIT)
                for a, h in enumerate(heads):
                    last = mm(ps[VW * h:VW * h + VW, OBANK, q0 - 512 * half:512],
                              vs[par][:, j, h, :], pT[idx % 4][:, a * nq:(a + 1) * nq],
                              start=(j == 0), stop=(j == 4 * half + 3), skip_group_check=True)
                last.then_inc(s_pv, 1)

            def turn_max(n, par):
                pe.wait_ge(s_mg, n + 1)
                tp(ps[0:32, MISC, 0:P], mx[par][:, :, :].rearrange("p h t -> p (h t)")).then_inc(s_mt, 1)

            def turn_out(n, half):
                pe.wait_ge(s_oc, 2 * n + half + 1 + OC_CREDIT)
                for t in range(4):
                    last = tp(ps[:, MISC, t * P:(t + 1) * P], oT[half][:, t * P:(t + 1) * P])
                last.then_inc(s_ot, 1)

            def step(mn, mb, mg, en, eg, first_exp=False, last_exp=False):
                done_m = 0

                def maxima(upto):
                    nonlocal done_m
                    while mn is not None and done_m < min(upto, NMU):
                        max_unit(mn, mb, mg, done_m)
                        done_m += 1

                weighed = 0
                for k in range(NEU):
                    if en is None:
                        break
                    exp_unit(en, eg, k)
                    maxima((k + 1) * NMU // NEU)
                    if k == 2 and not first_exp:
                        pe.wait_ge(s_on, 2 * en - 1)
                        turn_out(en - 1, 1)
                    if k == 5:
                        if not first_exp:
                            pe.wait_ge(s_on, 2 * en)
                        if not last_exp:
                            turn_max(en + 1, (eg + 1) % 2)
                    if k == 14:
                        if not last_exp:
                            pe.wait_ge(s_mn, en + 2)
                        turn_out(en, 0)
                    while k - weighed >= 2:
                        weigh(en, eg % 2, weighed)
                        weighed += 1
                if en is None:
                    maxima(4)
                    if mn > 0:
                        turn_max(mn - 1, (mg + 1) % 2)
                    maxima(NMU)
                else:
                    while weighed < NEU:
                        weigh(en, eg % 2, weighed)
                        weighed += 1

            step(0, 0, 0, None, None)
            step(1, 0, 1, None, None)
            step(2, 0, 2, 0, 0, first_exp=True)
            step(3, 0, 3, 1, 1)
            with pe.Fori(1, NB) as b:
                for g in range(HG):
                    step(4 * b + g, b, g, 4 * b + g - 2, (g + 2) % 4)
            step(None, None, None, 4 * NB - 2, 2)
            step(None, None, None, 4 * NB - 1, 3, last_exp=True)
            pe.wait_ge(s_on, 2 * 4 * NB - 1)
            turn_out(4 * NB - 1, 1)

            pe.wait_ge(s_on, 2 * 4 * NB)
            pe.wait_ge(s_experts, 16 * 2 * NE)
            with pe.Fori(0, 2) as i:
                for u in range(2):
                    pe.wait_ge(s_oin[u], i + 1)
                    for t in range(KT):
                        last = tp(ps[:, 4 * u + t // 4, (t % 4) * P:(t % 4 + 1) * P], o_in[u][:, t, :])
                    last.then_inc(s_otr[u], 1)
                for u in range(2):
                    pe.wait_ge(s_oca[u], i + 1)
                    for r in range(CH):
                        last = mm(ps[:, 4 * u + 2 + r // 4, (r % 4) * P:(r % 4 + 1) * P],
                                  ocT[u][:, :, r], w_proj[:, :], start=(r % 4 == 0), stop=True,
                                  skip_group_check=True)
                    last.then_inc(s_pj[u], 1)
                for u in range(2):
                    pe.wait_ge(s_zz[u], i + 1)
                    for r in range(CH):
                        last = tp(ps[:, 4 * u + r // 4, (r % 4) * P:(r % 4 + 1) * P], zz[u][:, r, 0:D])
                    last.then_inc(s_zt[u], 1)
                for u in range(2):
                    pe.wait_ge(s_h2[u], i + 1)
                    for r in range(CH):
                        last = mm(ps[:, 4 * u + 2, r * NE:(r + 1) * NE], h2T[u][:, r, :], w_router[:, :],
                                  start=(r == 0), stop=True, skip_group_check=True)
                    last.then_inc(s_lg[u], 1)
                for u in range(2):
                    pe.wait_ge(s_rc[u], i + 1)
                    mm(ps[:, 4 * u + 3, 0:NE], con(C_LOW, P), rowc[u][:, :], start=True, stop=True,
                       skip_group_check=True)
                    mm(ps[:, 4 * u + 3, NE:2 * NE], con(C_ONE, P), rowc[u][:, :], start=False, stop=True,
                       skip_group_check=True).then_inc(s_rp[u], 1)

            for u in range(2):
                pe.wait_ge(s_dest[u], 2)

            HBANK, YBANK = 6, 7

            def expert(k):
                return pe.value_load(tile_expert[0:1, bass.ds(k, 1)], min_val=0, max_val=NE - 1)

            def turn_tile(k, s4):
                pe.wait_ge(s_hrow[s4], tile_turn(k, s4))
                if not isinstance(k, int) or k > 0:
                    pe.wait_ge(s_hTt, k)
                tp(ps[:, HBANK, 0:P], h_row[s4][:, 0:D]).then_inc(s_tT, 1)

            def up(k, s2, first=False):
                e = expert(k)
                pe.wait_ge(s_hTt, k + 1)
                if not first:
                    pe.wait_ge(s_av, k - 1)
                for v in range(2):
                    mm(ps[:, 2 * s2 + v, :], hT_t[s2][:, :], w_exp[:, e, v * DFF:(v + 1) * DFF],
                       start=True, stop=True).then_inc(s_gv, 1)

            def turn_activations(k, s2, first=False):
                pe.wait_ge(s_av, k + 1)
                if not first:
                    pe.wait_ge(s_aTc, k - 1)
                for f in range(FT):
                    last = tp(ps[:, 4 + s2, f * P:(f + 1) * P], act_v[s2][:, f * P:(f + 1) * P])
                last.then_inc(s_aT, 1)

            def down(k, s2, first=False):
                e = expert(k)
                pe.wait_ge(s_aTc, k + 1)
                if not first:
                    pe.wait_ge(s_yr, k)
                for f in range(FT):
                    at = 2 * DFF + f * D
                    last = mm(ps[:, YBANK, 0:D], act_T[s2][:, f, :], w_exp[:, e, at:at + D],
                              start=(f == 0), stop=(f == FT - 1))
                last.then_inc(s_yy, 1)

            def work(k, j, start=4):
                up(k, j % 2, first=(start < 2))
                if start > 0:
                    turn_activations(k - 1, (j + 1) % 2, first=(start < 3))
                turn_tile(k + 1, (j + 1) % 4)
                if start > 1:
                    down(k - 2, j % 2, first=(start < 3))

            turn_tile(0, 0)
            for k in range(4):
                work(k, k, k)
            with pe.Fori(1, TILES // 4 - 1) as m:
                for j in range(4):
                    work(4 * m + j, j)
            for j in range(3):
                work(TILES - 4 + j, j)
            up(TILES - 1, 1)
            turn_activations(TILES - 2, 0)
            down(TILES - 3, 1)
            turn_activations(TILES - 1, 1)
            down(TILES - 2, 0)
            down(TILES - 1, 1)

        @block.scalar
        def _(act):
            A = nc.scalar.activation
            for k in range(2):
                act.sem_inc(s_stored[k], STORED_CREDIT)
            act.sem_inc(s_pv, PV_CREDIT)
            act.sem_inc(s_ot, OT_CREDIT)

            act.wait_ge(s_params, 16 * 8)
            A(lg_d[:, :], lg_d[:, :], ACT.Exp)
            A(lg_g[:, :], lg_g[:, :], ACT.Exp).then_inc(s_set_act, 1)
            act.wait_ge(s_set_dve, 2)
            A(pu[:, :], aT[:, :], ACT.Exp, scale=small[:, C_PU - C_DS:C_PU - C_DS + 1])
            for r in range(CH):
                at = C_PI - C_DS + r
                A(pi[:, r, :], aT[:, :], ACT.Exp, scale=small[:, at:at + 1])
                last = A(ph[:, r, :], aG[:, :], ACT.Exp, scale=-float(r + 1))
            last.then_inc(s_set_act, 1)

            act.wait_ge(s_weights, 16 * 10)
            act.wait_ge(s_set_dve, 3)
            with act.Fori(0, 2) as i:
                for u in range(2):
                    act.wait_ge(s_xtr[u], i + 1)
                    A(xT[u][:, 0:4, :], ps[:, 4 * u, :].rearrange("p (r c) -> p r c", c=P),
                      ACT.Copy).then_inc(s_xTa[u], 1)
                for m in range(2):
                    for u in range(2):
                        act.wait_ge(s_var[u], 2 * i + m + 1)
                        src = mv[u][:, :, 1] if m == 0 else sc[u][:, 3, :]
                        A(sc[u][:, 4 * m, :], src, ACT.Sqrt, bias=eps_t[:, 0:1]).then_inc(s_sd[u], 1)
                for u in range(2):
                    act.wait_ge(s_hzt[u], i + 1)
                    slots = hT[u][:, 2:T + 2].rearrange("c (p r) -> c r p", r=CH)
                    for h in range(2):
                        last = A(slots[:, 4 * h:4 * h + 4, :],
                                 ps[:, 4 * u + 2 + h, :].rearrange("c (r p) -> c r p", p=P),
                                 ACT.Identity, scale=vecs[:, 0:1], bias=vecs[:, 1:2])
                    last.then_inc(s_hT[u], 1)
                for k in range(2):
                    for u in range(2):
                        m = 2 * i + u
                        act.wait_ge(s_sum[k], m + 1)
                        act.wait_ge(s_stored[k], 48 * m + STORED_CREDIT)
                        A(part[k][0][:, :], tq[k][:, :], ACT.Copy).then_inc(s_cast1[k], 1)
                        act.wait_ge(s_rest1[k], m + 1)
                        A(part[k][1][:, :], tr[k][:, :], ACT.Copy).then_inc(s_cast2[k], 1)
                for u in range(2):
                    act.wait_ge(s_v[u], i + 1)
                    for h in range(2):
                        last = A(v_all[:, 2 * i + u, 4 * h:4 * h + 4, :, 0:HD],
                                 ps[:, 4 * u + h, :].rearrange("p (t h d) -> p t h d", t=4, d=HD), ACT.Copy)
                    last.then_inc(s_vc[u], 1)

            def negate_max(n, first=False):
                act.wait_ge(s_mt, n + 1)
                if not first:
                    act.wait_ge(s_mp, n)
                A(m_neg[:, :], ps[0:32, 5, 0:P], ACT.Copy, scale=-1.0).then_inc(s_mn, 1)

            def copy_out(n, half):
                units = HALF0 if half == 0 else NEU
                act.wait_ge(s_pv, NEU * n + units + PV_CREDIT)
                act.wait_ge(s_ot, 2 * n + half - 1 + OT_CREDIT)
                A(oT[half][:, :], ps[:, 4, :], ACT.Copy).then_inc(s_oc, 1)

            def exps(n, max_n):
                for k, (half, j, q0, nq, heads) in enumerate(EXPU):
                    act.wait_ge(s_es, NEU * n + k + 1)
                    act.wait_ge(s_pv, NEU * n + k - 3 + PV_CREDIT)
                    pair = 2 * (k % 2)
                    w = nq * len(heads)
                    if nq == 384:
                        src = ps[:, pair:pair + 2, 0:nq]
                        dst = pT[k % 4][:, 0:w].rearrange("p (h q) -> p h q", h=2)
                    else:
                        src = banks(pair, 2)[:, 0:w]
                        dst = pT[k % 4][:, 0:w]
                    A(dst, src, ACT.Exp, scale=SCALE).then_inc(s_ex, 1)
                    if k == HALF0 + 1:
                        copy_out(n, 0)
                    if k == 8 and max_n is not None:
                        negate_max(max_n)
                copy_out(n, 1)

            negate_max(0, first=True)
            exps(0, 1)
            exps(1, 2)
            with act.Fori(1, NB) as b:
                for g in range(HG):
                    exps(4 * b + g - 2, 4 * b + g - 1)
            exps(4 * NB - 2, 4 * NB - 1)
            exps(4 * NB - 1, None)

            with act.Fori(0, 2) as i:
                for u in range(2):
                    act.wait_ge(s_otr[u], i + 1 + OTR_CREDIT)
                    A(ocT[u][:, :, :].rearrange("c p r -> c (p r)"), banks(4 * u, 2), ACT.Copy
                      ).then_inc(s_oca[u], 1)
                for u in range(2):
                    act.wait_ge(s_varc[u], i + 1)
                    A(scc[u][:, 0, :], mvc[u][:, :, 1], ACT.Sqrt, bias=eps_t[:, 0:1]).then_inc(s_sdc[u], 1)
                for u in range(2):
                    act.wait_ge(s_zt[u], i + 1)
                    A(h2T[u][:, :, :].rearrange("c r p -> c (r p)"), banks(4 * u, 2), ACT.Identity,
                      scale=vecs[:, 2:3], bias=vecs[:, 3:4]).then_inc(s_h2[u], 1)

            def turned(k, s2, first=False):
                act.wait_ge(s_tT, k + 1)
                if not first:
                    act.wait_ge(s_gv, 2 * (k - 1))
                A(hT_t[s2][:, :], ps[:, 6, 0:P], ACT.Identity, scale=vecs[:, 2:3], bias=vecs[:, 3:4]
                  ).then_inc(s_hTt, 1)

            def silu(k, s2, first=False):
                act.wait_ge(s_gv, 2 * k + 1)
                if not first:
                    act.wait_ge(s_av, k - 1)
                A(gate[s2][:, :], ps[:, 2 * s2, :], ACT.Silu).then_inc(s_sg, 1)

            def activations_turned(k, s2, first=False):
                act.wait_ge(s_aT, k + 1)
                if not first:
                    act.wait_ge(s_yy, k - 1)
                A(act_T[s2][:, :, :].rearrange("p f t -> p (f t)"), ps[:, 4 + s2, :], ACT.Copy
                  ).then_inc(s_aTc, 1)

            def work(k, j, start=4):
                silu(k, j % 2, first=(start < 2))
                if start > 0:
                    activations_turned(k - 1, (j + 1) % 2, first=(start < 3))
                turned(k + 1, (j + 1) % 2, first=(start < 1))

            turned(0, 0, first=True)
            for k in range(4):
                work(k, k, k)
            with act.Fori(1, TILES // 4 - 1) as m:
                for j in range(4):
                    work(4 * m + j, j)
            for j in range(3):
                work(TILES - 4 + j, j)
            silu(TILES - 1, 1)
            activations_turned(TILES - 2, 0)
            activations_turned(TILES - 1, 1)

            with act.Fori(0, 2) as i:
                for u in range(2):
                    act.wait_ge(s_varc[u], 2 + i + 1)
                    A(scc[u][:, 0, :], mvc[u][:, :, 1], ACT.Sqrt, bias=eps_t[:, 0:1]).then_inc(s_sdc[u], 1)

        @block.vector
        def _(dve):
            V = nc.vector
            chain = Chain(dve, s_dve)
            for k in range(2):
                dve.sem_inc(s_cast3[k], CAST3_CREDIT)

            def merge_halves(to, stats, tmp):
                m0, m1, v0, v1 = (stats[:, :, c] for c in (1, 4, 2, 5))
                V.tensor_tensor(tmp[:, 0, :], m0, m1, ALU.add)
                V.tensor_tensor(tmp[:, 1, :], m0, m1, ALU.subtract)
                chain.link(V.tensor_tensor(tmp[:, 2, :], v0, v1, ALU.add))
                V.tensor_scalar(to[:, :, 0], tmp[:, 0, :], 0.5, None, ALU.mult)
                chain.link(V.scalar_tensor_tensor(out=tmp[:, 3, :], in0=tmp[:, 1, :], scalar=0.25,
                                                  in1=tmp[:, 1, :], op0=ALU.mult, op1=ALU.mult))
                return V.scalar_tensor_tensor(out=to[:, :, 1], in0=tmp[:, 2, :], scalar=1.0 / D,
                                              in1=tmp[:, 3, :], op0=ALU.mult, op1=ALU.add)

            V.memset(eps_t[:, :], EPS)
            V.memset(b_pad[:, :], 0.0)
            for u in range(2):
                V.memset(hT[u][:, 0:2], 0.0)
            V.memset(zero3[:, :], 0.0)
            dve.wait_ge(s_params, 16 * 8)
            V.tensor_copy(ident_b[:, :], ident)
            V.tensor_copy(mask_q[:, :], cst[:, C_MASKQ:C_MASKQ + P])
            V.tensor_copy(mask_k[:, :], cst[:, C_MASKK:C_MASKK + P])
            V.tensor_scalar(diag_d[:, :], ident, dv[:, 0:1], None, ALU.mult)
            V.tensor_copy(c_rep[:, :, :], cw_d[:, :].unsqueeze(1).broadcast_to([P, CH, S]))
            dve.wait_ge(s_set_act, 1)
            V.tensor_scalar(a_rep[:, :, :], lg_d[:, :].unsqueeze(1).broadcast_to([P, CH, S]),
                            RATE_MAX, None, ALU.min)
            chain.link(V.tensor_scalar(lg_g[:, :], lg_g[:, :], RATE_MAX, None, ALU.min))
            V.tensor_tensor(diag_d[:, :], diag_d[:, :], ident, ALU.add).then_inc(s_set_dve, 1)
            dve.wait_ge(s_set_pe, 2)
            V.tensor_copy(b_pad[:, 112:128], ps[:, 0, 0:S])
            V.tensor_copy(aT[:, :], ps[:, 1, 0:P])
            V.tensor_copy(cT[:, :], ps[:, 1, P:2 * P])
            V.tensor_copy(aG[:, :], ps[:, 2, 0:G])
            V.tensor_copy(cG[:, :], ps[:, 2, G:2 * G]).then_inc(s_set_dve, 1)
            dve.wait_ge(s_set_dve, 2)
            dve.wait_ge(s_set_act, 2)
            V.tensor_tensor(w_state[:, :, :], pu[:, :].unsqueeze(2).broadcast_to([P, D, S]),
                            small[:, 0:S].unsqueeze(1).broadcast_to([P, D, S]), ALU.mult)
            chain.link(V.tensor_tensor(phc[:, :, :], ph[:, :, :],
                                       cG[:, :].unsqueeze(1).broadcast_to([P, CH, G]), ALU.mult))
            for g in range(G):
                V.tensor_tensor(w_carry[:, g, :, :], phc[:, :, g].unsqueeze(2).broadcast_to([P, CH, 8]),
                                small[:, C_DD - C_DS:C_DD - C_DS + 8].unsqueeze(1).broadcast_to([P, CH, 8]),
                                ALU.mult)
            for r in range(CH):
                at = C_CM - C_DS + r
                last = V.scalar_tensor_tensor(out=w_chunk[:, r, :], in0=pi[:, r, :], scalar=small[:, at:at + 1],
                                              in1=cT[:, :], op0=ALU.mult, op1=ALU.mult)
            last.then_inc(s_set_dve, 1)
            dve.wait_ge(s_weights, 16 * 10)

            dve.wait_ge(s_set_pool, 1)
            A_CHAIN = 16
            base = chain.n
            with dve.Fori(0, 2) as i:
                chain.base, chain.n = base + A_CHAIN * i, 0
                for u in range(2):
                    dve.wait_ge(s_xtr[u], i + 1)
                    V.tensor_copy(xT[u][:, 4:8, :], ps[:, 4 * u + 1, :].rearrange("p (r c) -> p r c", c=P)
                                  ).then_inc(s_xTd[u], 1)
                for u in range(2):
                    dve.wait_ge(s_bt[u], i + 1)
                    V.tensor_copy(bt[u][:, :], ps[:, 4 * u + 2, 0:P]).then_inc(s_btc[u], 1)
                for u in range(2):
                    dve.wait_ge(s_u[u], i + 1)
                    chain.link(V.tensor_tensor_scan(hs[u][:, 1:G * P + 1], decay[:, :, :].rearrange("p g c -> p (g c)"),
                                                    banks(4 * u, 4), 0.0, ALU.mult, ALU.add))
                    V.memset(hs[u][:, 0:G * P].rearrange("p (g c) -> p g c", c=P)[:, :, 0:1], 0.0
                             ).then_inc(s_scan[u], 1)
                for u in range(2):
                    dve.wait_ge(s_y[u], i + 1)
                    for r in range(CH):
                        last = V.bn_stats(st[u][:, r, :], ps[:, 4 * u + r // 4, (r % 4) * P:(r % 4 + 1) * P])
                    chain.link(last)
                    merge_halves(mv[u], st[u], hv[u]).then_inc(s_var[u], 1)
                for u in range(2):
                    dve.wait_ge(s_sd[u], 2 * i + 1)
                    dve.wait_ge(s_var[u], 2 * i + 1)
                    chain.link(V.reciprocal(sc[u][:, 1, :], sc[u][:, 0, :]))
                    chain.link(V.tensor_tensor(sc[u][:, 2, :], mv[u][:, :, 1], sc[u][:, 1, :], ALU.mult))
                    V.tensor_tensor(sc[u][:, 3, :], sc[u][:, 2, :], sc[u][:, 1, :], ALU.mult
                                    ).then_inc(s_var[u], 1)
                    for r in range(CH):
                        V.tensor_scalar(x1[:, 2 * i + u, r, :], ps[:, 4 * u + r // 4, (r % 4) * P:(r % 4 + 1) * P],
                                        mv[u][:, r, 0:1], sc[u][:, 1, r:r + 1], ALU.subtract, ALU.mult)
                    dve.wait_ge(s_sd[u], 2 * i + 2)
                    V.reciprocal(sc[u][:, 5, :], sc[u][:, 4, :]).then_inc(s_x1[u], 1)
                for u in range(2):
                    dve.wait_ge(s_hT[u], i + 1)
                    for k in range(3):
                        if k == 0:
                            ins = V.tensor_scalar(hc[u][:, :], hT[u][:, 0:T], vecs[:, 4:5], None, ALU.mult)
                        else:
                            ins = V.scalar_tensor_tensor(out=hc[u][:, :], in0=hT[u][:, k:T + k],
                                                         scalar=vecs[:, 4 + k:5 + k], in1=hc[u][:, :],
                                                         op0=ALU.mult, op1=ALU.add)
                        if k < 2:
                            chain.link(ins)
                        else:
                            ins.then_inc(s_hc[u], 1)
                for k in range(2):
                    for u in range(2):
                        dve.wait_ge(s_qk[u], 2 * i + k + 1)
                        dve.wait_ge(s_cast3[k], 2 * i + u + CAST3_CREDIT)
                        V.tensor_tensor(tq[k][:, :], banks(4 * u, 2), cos[:, :], ALU.mult)
                        V.tensor_tensor(tr[k][:, :], banks(4 * u + 2, 2), sin[:, :], ALU.mult
                                        ).then_inc(s_rope[u], 1)
                assert chain.n == A_CHAIN, chain.n
            chain.base, chain.n = base + 2 * A_CHAIN, 0

            for k in range(2):
                dve.wait_ge(s_stored[k], 16 * 3 * NB + STORED_CREDIT)
            for u in range(2):
                dve.wait_ge(s_vc[u], 2 + VC_CREDIT)
            for g in range(HG):
                last = V.memset(ks[g][:, :, :].rearrange("p h t -> p (h t)").bitcast(F32), 0.0)
            chain.link(last)
            for g in range(HG):
                last = V.memset(ks[g][96:99, :, :], 1.0)
            last.then_inc(s_clear, 1)

            def reduce_unit(n, par, idx):
                t, k0, nk, heads, chunk = MAXU[idx]
                dve.wait_ge(s_ms, NMU * n + idx + 1)
                m = len(heads)
                dst = mx[par][:, heads[0]:heads[0] + m, t] if chunk == 0 else \
                    mxb[par][:, heads[0]:heads[0] + m, t - 4]
                V.tensor_reduce(dst, ps[:, 6 + idx % 2, 0:m * nk].rearrange("p (h k) -> p h k", h=m),
                                AX_X, ALU.max).then_inc(s_mr, 1)

            def combine(n, par):
                dve.wait_ge(s_mr, NMU * (n + 1) + MR_CREDIT)
                V.tensor_tensor(mx[par][:, :, 4:8], mx[par][:, :, 4:8], mxb[par][:, :, :], ALU.max
                                ).then_inc(s_mg, 1)

            def normalise(n, b, eg, half):
                dve.wait_ge(s_ot, 2 * n + half + 1 + OT_CREDIT)
                o = ps[:, 5, :].rearrange("p (t h d) -> p t h d", t=4, h=4)
                chain.link(V.reciprocal(rden[half][:, :, :], o[:, :, :, HD]))
                dst = o_all[:, b, 4 * half:4 * half + 4, 32 * eg:32 * eg + 32].rearrange(
                    "p t (h d) -> p t h d", d=HD)
                V.tensor_tensor(dst, o[:, :, :, 0:HD], rden[half][:, :, :].unsqueeze(3).broadcast_to([P, 4, 4, HD]),
                                ALU.mult).then_inc(s_on, 1)

            def step(mn, mg, en, eb, eg, pb, first_exp=False):
                if mn is not None:
                    for idx in range(NMU):
                        if idx == 0 and en is not None:
                            dve.wait_ge(s_mt, mn - 1)
                        reduce_unit(mn, mg % 2, idx)
                        if idx == 8 and en is not None and not first_exp:
                            normalise(en - 1, pb, (eg - 1) % 4, 1)
                        if idx == 32 and en is not None:
                            normalise(en, eb, eg, 0)
                    combine(mn, mg % 2)
                else:
                    normalise(en - 1, pb, (eg - 1) % 4, 1)
                    normalise(en, eb, eg, 0)

            step(0, 0, None, None, None, None)
            step(1, 1, None, None, None, None)
            step(2, 2, 0, 0, 0, None, first_exp=True)
            step(3, 3, 1, 0, 1, 0)
            B_CHAIN = 8
            base = chain.base + chain.n
            with dve.Fori(1, NB) as b:
                chain.base, chain.n = base + B_CHAIN * (b - 1), 0
                for g in range(HG):
                    step(4 * b + g, g, 4 * b + g - 2, b - 1 if g < 2 else b, (g + 2) % 4,
                         b - 1 if g < 3 else b)
                assert chain.n == B_CHAIN, chain.n
            chain.base, chain.n = base + B_CHAIN * (NB - 1), 0
            step(None, None, 4 * NB - 2, NB - 1, 2, NB - 1)
            step(None, None, 4 * NB - 1, NB - 1, 3, NB - 1)
            normalise(4 * NB - 1, NB - 1, 3, 1)

            def moments(u, src):
                for r in range(CH):
                    last = V.bn_stats(stc[u][:, r, :], src(r))
                chain.link(last)
                merge_halves(mvc[u], stc[u], hvc[u]).then_inc(s_varc[u], 1)

            def normal(u, src, turn, signal):
                dve.wait_ge(s_sdc[u], turn)
                dve.wait_ge(s_varc[u], turn)
                chain.link(V.reciprocal(scc[u][:, 1, :], scc[u][:, 0, :]))
                for r in range(CH):
                    last = V.tensor_scalar(zz[u][:, r, 0:D], src(r), mvc[u][:, r, 0:1],
                                           scc[u][:, 1, r:r + 1], ALU.subtract, ALU.mult)
                last.then_inc(signal, 1)

            V.memset(zero8[:, :], 0.0)
            chain.link(V.memset(zrow[:, :, :], 0.0))
            V.tensor_copy(zrow[:, :, D:DI].bitcast(U32), con(C_IDZ, 2 * NE).unsqueeze(2)).then_inc(s_zrow, 1)
            chain.link(V.memset(count[:, :], 0.0))

            C_CHAIN = 36
            base = chain.base + chain.n
            with dve.Fori(0, 2) as i:
                chain.base, chain.n = base + C_CHAIN * i, 0
                for u in range(2):
                    dve.wait_ge(s_pj[u], i + 1)
                    V.tensor_tensor(x2[u][:, :, :], x1[:, 2 * i + u, :, :],
                                    banks(4 * u + 2, 2).rearrange("p (r d) -> p r d", d=D), ALU.add
                                    ).then_inc(s_x2[u], 1)
                for u in range(2):
                    dve.wait_ge(s_x2[u], i + 1)
                    moments(u, lambda r: x2[u][:, r, :])
                for u in range(2):
                    dve.wait_ge(s_zfree[u], i + ZFREE_CREDIT)
                    V.tensor_copy(zz[u][:, :, D:DI].bitcast(U32), con(C_ID, NB * CH).rearrange(
                        "p (b r o) -> p b r o", r=CH, o=1)[:, 2 * i + u, :, :])
                    normal(u, lambda r: x2[u][:, r, :], i + 1, s_zz[u])
                for u in range(2):
                    dve.wait_ge(s_lg[u], i + 1)
                    lg = ps[:, 4 * u + 2, 0:CH * NE].rearrange("p (r e) -> p r e", e=NE)
                    pk = pick[u]
                    chain.link(V.tensor_reduce(lmax[u][:, :], lg, AX_X, ALU.max))
                    chain.link(V.tensor_tensor(pk[:, :, :], lg, lmax[u][:, :].unsqueeze(2).broadcast_to([P, CH, NE]),
                                               ALU.is_ge))
                    chain.link(V.tensor_scalar(left[u][:, :], pk[:, :, 0], -1.0, 1.0, ALU.mult, ALU.add))
                    for e in range(1, NE):
                        chain.link(V.tensor_tensor(pk[:, :, e], pk[:, :, e], left[u][:, :], ALU.mult))
                        if e < NE - 1:
                            chain.link(V.tensor_tensor(left[u][:, :], left[u][:, :], pk[:, :, e], ALU.subtract))
                    V.tensor_reduce(rowc[u][:, :], pk[:, :, :].rearrange("p r e -> p e r"), AX_X, ALU.add
                                    ).then_inc(s_rc[u], 1)
                    for e in range(NE):
                        last = V.tensor_tensor_scan(incl[u][:, :, e], pk[:, :, e], zero8[:, :], 0.0, ALU.add, ALU.add)
                    chain.link(last)
                for u in range(2):
                    dve.wait_ge(s_rp[u], i + 1 + PK_CREDIT)
                    chain.link(V.tensor_tensor(offs[u][:, :], ps[:, 4 * u + 3, 0:NE], count[:, :], ALU.add))
                    V.tensor_tensor(count[:, :], ps[:, 4 * u + 3, NE:2 * NE], count[:, :], ALU.add)
                    chain.link(V.tensor_tensor(offs[u][:, :], offs[u][:, :], con(C_ER, NE), ALU.add))
                    chain.link(V.tensor_tensor(incl[u][:, :, :], incl[u][:, :, :],
                                               offs[u][:, :].unsqueeze(1).broadcast_to([P, CH, NE]), ALU.add))
                    chain.link(V.tensor_tensor(incl[u][:, :, :], incl[u][:, :, :], pick[u][:, :, :], ALU.mult))
                    chain.link(V.tensor_reduce(rank[u][:, :], incl[u][:, :, :], AX_X, ALU.add))
                    V.tensor_copy(dest[:, 2 * i + u, :], rank[u][:, :])
                    V.tensor_copy(dest_now[u][:, :], rank[u][:, :]).then_inc(s_dest[u], 1)
                assert chain.n == C_CHAIN, chain.n
            chain.base, chain.n = base + 2 * C_CHAIN, 0

            V.tensor_tensor(above[:, :, :], count[:, :].unsqueeze(2).broadcast_to([P, NE, NB * KT]),
                            con(C_K, NB * KT).unsqueeze(1).broadcast_to([P, NE, NB * KT]), ALU.is_gt)
            chain.link(V.tensor_scalar(offs[0][:, :], count[:, :], con(C_P, 1), None, ALU.add))
            V.tensor_reduce(tiles_e[:, :], above[:, :, :], AX_X, ALU.add)
            chain.link(V.tensor_tensor(offs[1][:, :], offs[0][:, :], con(C_ER, NE), ALU.add))
            chain.link(V.tensor_scalar(tail[:, :], offs[1][:, :], 1.0, None, ALU.add))
            chain.link(V.tensor_copy(cum_e[:, :], tiles_e[:, :]))
            for e in range(1, NE):
                chain.link(V.tensor_tensor(cum_e[:, e:e + 1], cum_e[:, e:e + 1], cum_e[:, e - 1:e], ALU.add))
            V.tensor_scalar(jump_e[:, :], tiles_e[:, :], -float(P), float(REGION), ALU.mult, ALU.add)
            chain.link(V.tensor_tensor(past[:, :, :], con(C_TI, TILES).unsqueeze(2).broadcast_to([P, TILES, NE]),
                                       cum_e[:, :].unsqueeze(1).broadcast_to([P, TILES, NE]), ALU.is_ge))
            chain.link(V.tensor_tensor(past_j[:, :, :], past[:, :, :],
                                       jump_e[:, :].unsqueeze(1).broadcast_to([P, TILES, NE]), ALU.mult))
            V.tensor_reduce(tile_f[:, 0, :], past[:, :, :], AX_X, ALU.add)
            chain.link(V.tensor_reduce(tile_f[:, 1, :], past_j[:, :, :], AX_X, ALU.add))
            V.tensor_scalar(tile_expert[:, :], tile_f[:, 0, :], float(NE - 1), None, ALU.min)
            V.scalar_tensor_tensor(out=tile_row[:, :], in0=con(C_TI, TILES), scalar=float(P), in1=tile_f[:, 1, :],
                                   op0=ALU.mult, op1=ALU.add).then_inc(s_plan, 1)

            def weigh_values(k, s2, first=False):
                dve.wait_ge(s_gv, 2 * k + 2)
                dve.wait_ge(s_sg, k + 1)
                if not first:
                    dve.wait_ge(s_aT, k - 1)
                V.tensor_tensor(act_v[s2][:, :], ps[:, 2 * s2 + 1, :], gate[s2][:, :], ALU.mult
                                ).then_inc(s_av, 1)

            def keep_numbers(k, s4, first=False):
                dve.wait_ge(s_hrow[s4], tile_turn(k, s4))
                if not first:
                    dve.wait_ge(s_yst[s4], tile_turn(k, s4) - 16)
                V.tensor_copy(y_id[s4][:, :], h_row[s4][:, D:DI].bitcast(U32)).then_inc(s_id, 1)

            def copy_y(k, s4, first=False):
                dve.wait_ge(s_yy, k + 1)
                if not first:
                    dve.wait_ge(s_yst[s4], tile_turn(k, s4) - 16)
                V.tensor_copy(y_row[s4][:, :], ps[:, 7, 0:D]).then_inc(s_yr, 1)

            for k in range(8):
                weigh_values(k, k % 2, first=(k < 2))
                keep_numbers(k, k % 4, first=(k < 4))
                if k > 1:
                    copy_y(k - 2, (k - 2) % 4, first=(k - 2 < 4))
            with dve.Fori(2, TILES // 4) as m:
                for j in range(4):
                    weigh_values(4 * m + j, j % 2)
                    keep_numbers(4 * m + j, j)
                    copy_y(4 * m + j - 2, (j + 2) % 4)
            copy_y(TILES - 2, 2)
            copy_y(TILES - 1, 3)

            for u in range(2):
                dve.wait_ge(s_acc[u], 2)
            F_CHAIN = 8
            base = chain.base + chain.n
            with dve.Fori(0, 2) as i:
                chain.base, chain.n = base + F_CHAIN * i, 0
                for u in range(2):
                    dve.wait_ge(s_yg[u], 16 * (i + 1))
                    dve.wait_ge(s_res[u], i + RES_CREDIT)
                    V.tensor_tensor(x2[u][:, :, :], yg[:, 2 * i + u, :, :], x1[:, 2 * i + u, :, :], ALU.add
                                    ).then_inc(s_fin[u], 1)
                for u in range(2):
                    dve.wait_ge(s_fin[u], i + 1)
                    moments(u, lambda r: x2[u][:, r, :])
                for u in range(2):
                    dve.wait_ge(s_out[u], 16 * i + OUT_CREDIT)
                    normal(u, lambda r: x2[u][:, r, :], 2 + i + 1, s_res[u])
                assert chain.n == F_CHAIN, chain.n

        @block.gpsimd
        def _(pool):
            G_ = nc.gpsimd
            for u in range(2):
                pool.sem_inc(s_otr[u], OTR_CREDIT)
                pool.sem_inc(s_out[u], OUT_CREDIT)
                pool.sem_inc(s_zfree[u], ZFREE_CREDIT)
                pool.sem_inc(s_res[u], RES_CREDIT)
            G_.memset(ones[:, :], 1.0).then_inc(s_pool, 1)
            G_.memset(v_all[:, :, :, :, :].rearrange("p b t h c -> p (b t h c)"), 1.0).then_inc(s_pool, 1)
            pool.wait_ge(s_weights, 16 * 10)
            for k in range(2):
                w = w_qkv[:, k * D:(k + 1) * D].rearrange("c (h a d) -> c h a d", a=2, d=HD // 2)
                r = w_rot[:, k * D:(k + 1) * D].rearrange("c (h a d) -> c h a d", a=2, d=HD // 2)
                G_.tensor_copy(r[:, :, 0, :], w[:, :, 1, :])
                G_.tensor_copy(r[:, :, 1, :], w[:, :, 0, :])
            pool.wait_ge(s_set_act, 2)
            G_.tensor_copy(decay[:, :, :], ph[:, CH - 1, :].unsqueeze(2).broadcast_to([P, G, P])
                           ).then_inc(s_pool, 1)
            pool.wait_ge(s_pool, 3)
            G_.memset(decay[:, :, 0:1], 0.0).then_inc(s_set_pool, 1)

            with pool.Fori(0, 2) as i:
                for u in range(2):
                    pool.wait_ge(s_x1[u], i + 1)
                    G_.tensor_tensor(hz[u][:, :, :], x1[:, 2 * i + u, :, :],
                                     sc[u][:, 5, :].unsqueeze(2).broadcast_to([P, CH, D]), ALU.mult
                                     ).then_inc(s_hz[u], 1)
                for k in range(2):
                    for u in range(2):
                        m = 2 * i + u
                        pool.wait_ge(s_rope[u], 2 * i + k + 1 + ROPE_CREDIT)
                        G_.tensor_tensor(tq[k][:, :], tq[k][:, :], tr[k][:, :], ALU.add).then_inc(s_sum[k], 1)
                        pool.wait_ge(s_sum[k], m + 1)
                        pool.wait_ge(s_cast1[k], m + 1)
                        G_.tensor_tensor(tr[k][:, :], tq[k][:, :], part[k][0][:, :], ALU.subtract
                                         ).then_inc(s_rest1[k], 1)
                        pool.wait_ge(s_rest1[k], m + 1)
                        pool.wait_ge(s_cast2[k], m + 1)
                        G_.tensor_tensor(part[k][2][:, :], tr[k][:, :], part[k][1][:, :], ALU.subtract
                                         ).then_inc(s_cast3[k], 1)

            for k in range(2):
                pool.wait_ge(s_stored[k], 16 * 3 * NB + STORED_CREDIT)
            for u in range(2):
                pool.wait_ge(s_vc[u], 2 + VC_CREDIT)
            for g in range(HG):
                G_.memset(qs[g][:, :, :].rearrange("p h t -> p (h t)").bitcast(F32), 0.0)
            G_.memset(vs[0][:, :, :, :].rearrange("p t h c -> p (t h c)"), 0.0)
            G_.memset(vs[1][:, :, :, :].rearrange("p t h c -> p (t h c)"), 0.0).then_inc(s_clear, 1)
            pool.wait_ge(s_clear, 2)

            def values(n, b, g):
                pool.wait_ge(s_clear, 2)
                G_.tensor_copy(vs[g % 2][:, :, :, 0:VC], v_all[:, b, :, 4 * g:4 * g + 4, :]
                               ).then_inc(s_vst, 1)

            def max_parts(n, first=False):
                pool.wait_ge(s_mn, n + 1)
                if not first:
                    pool.wait_ge(s_mrow, MROW * n)
                G_.tensor_tensor(m_part[0][:, :], m_neg[:, :], ones[:, :], ALU.mult).then_inc(s_mpc, 1)
                pool.wait_ge(s_mpc, 3 * n + 1)
                G_.tensor_tensor(m_res[:, :], m_neg[:, :], m_part[0][:, :], ALU.subtract).then_inc(s_mpc, 1)
                pool.wait_ge(s_mpc, 3 * n + 2)
                G_.tensor_tensor(m_part[1][:, :], m_res[:, :], ones[:, :], ALU.mult).then_inc(s_mpc, 1)
                pool.wait_ge(s_mpc, 3 * n + 3)
                G_.tensor_tensor(m_part[2][:, :], m_res[:, :], m_part[1][:, :], ALU.subtract).then_inc(s_mp, 1)

            values(0, 0, 0)
            values(1, 0, 1)
            for g in range(HG):
                if g >= 2:
                    pool.wait_ge(s_pv, NEU * (g - 1) + PV_CREDIT)
                    values(g, 0, g)
                max_parts(g, first=(g == 0))
            with pool.Fori(1, NB) as b:
                for g in range(HG):
                    n = 4 * b + g
                    pool.wait_ge(s_pv, NEU * (n - 1) + PV_CREDIT)
                    values(n, b, g)
                    max_parts(n)

            with pool.Fori(0, 2) as i:
                for u in range(2):
                    pool.wait_ge(s_otr[u], i + OTR_CREDIT)
                    pool.wait_ge(s_on, 2 * 4 * NB)
                    G_.tensor_copy(o_in[u][:, :, :], o_all[:, 2 * i + u, :, :]).then_inc(s_oin[u], 1)
                for u in range(2):
                    pool.wait_ge(s_x2[u], i + 1)
                    pool.wait_ge(s_on, 2 * 4 * NB)
                    G_.tensor_tensor(x1[:, 2 * i + u, :, :], x1[:, 2 * i + u, :, :], x2[u][:, :, :], ALU.add
                                     ).then_inc(s_acc[u], 1)
                for u in range(2):
                    pool.wait_ge(s_on, 2 * 4 * NB)
                    pool.wait_ge(s_dest[u], i + 1)
                    for r in range(CH):
                        G_.indirect_dma_start(
                            out=h_sorted, out_offset=bass.IndirectOffsetOnAxis(ap=dest_now[u][:, r:r + 1], axis=0),
                            in_=zz[u][:, r, :], in_offset=None).then_inc(s_scat[u], 16)
                for u in range(2):
                    pool.wait_ge(s_scat[u], 16 * CH * (i + 1))
                    pool.sem_inc(s_zfree[u], 1)
            pool.wait_ge(s_plan, 1)
            for e in range(NE):
                G_.indirect_dma_start(out=h_sorted, out_offset=bass.IndirectOffsetOnAxis(ap=tail[:, e:e + 1], axis=0),
                                      in_=zrow[:, e, :], in_offset=None).then_inc(s_tail, 16)

            def scatter_tile(k, s4):
                pool.wait_ge(s_id, k + 1)
                pool.wait_ge(s_yr, k + 1)
                pool.sem_inc(s_ysc, 1)
                G_.indirect_dma_start(out=y_rows, out_offset=bass.IndirectOffsetOnAxis(ap=y_id[s4][:, 0:1], axis=0),
                                      in_=y_row[s4][:, :], in_offset=None).then_inc(s_yst[s4], 16)

            with pool.Fori(0, TILES // 4) as m:
                for j in range(4):
                    scatter_tile(4 * m + j, j)


_INS = ["L0_attn_x", "L0_attn_log_A_diag", "L0_attn_B_w", "L0_attn_C_w", "L0_attn_D_vec", "L0_ffn_ln1_w",
        "L0_ffn_ln1_b", "L0_ffn_ln2_w", "L0_ffn_ln2_b", "L0_ffn_conv_w", "L0_ffn_attn_w", "L0_ffn_proj_w",
        "L0_ffn_router_w", "L0_ffn_expert_wv", "L0_ffn_expert_proj"]
_OUTS = [((NB, T, D), "float32")]


def kernel(**inputs):
    import numpy as _np
    import concourse.bacc as _bacc
    from concourse import mybir as _mybir
    from concourse.bass_utils import run_bass_kernel_spmd as _run

    nc = _bacc.Bacc("TRN2", target_bir_lowering=False, num_devices=1)
    arrays, args = {}, []
    for name, a in [("constants", constants())] + [(n, inputs[n]) for n in _INS]:
        a = _np.ascontiguousarray(a)
        arrays[f"in_{name}_dram"] = a
        args.append(nc.dram_tensor(f"in_{name}_dram", a.shape, _mybir.dt.from_np(a.dtype), kind="ExternalInput").ap())
    for i, (shape, dtype) in enumerate(_OUTS):
        dt = _mybir.dt.from_np(_np.dtype(dtype))
        args.append(nc.dram_tensor(f"out_{i}_dram", shape, dt, kind="ExternalOutput").ap())
    layer_kernel(nc, *args)
    r = _run(nc, [arrays], core_ids=[0])
    return r.results[0]["out_0_dram"]
```

```python
from contextlib import ExitStack

import numpy as np
import concourse.bass as bass
from concourse import mybir

F32 = mybir.dt.float32
BF16 = mybir.dt.bfloat16
U32 = mybir.dt.uint32
ALU = mybir.AluOpType
ACT = mybir.ActivationFunctionType
AX_X = mybir.AxisListType.X

P = 128
NB = 4
T = 1024
D = 128
S = 16
CH = 8
G = D * S // P
NH = 16
HD = 8
HG = 4
KT = T // P
NE = 4
DFF = 512
FT = DFF // P
EPS = 1e-5
TILES = NB * KT + NE
REGION = NB * T + P
ROWS = NE * REGION + NE * P
DI = D + 1
WE = 2 * DFF + FT * D
MASKED = -1e30
ONE_PAIR = float(np.array([0x3F803F80], np.uint32).view(np.float32)[0])
RATE_MAX = 1e4
SCALE = float(1.0 / np.sqrt(np.float32(HD)))
VC = 9
VW = 32

C_IDENT, C_MASKQ, C_MASKK = 0, P, 2 * P
C_COS, C_SIN = 3 * P, 3 * P + T
C_DS = C_SIN + T
C_DD = C_DS + S
C_PU = C_DD + 8
C_PI = C_PU + 1
C_CM = C_PI + CH
C_ONE = C_CM + CH
C_LOW = C_ONE + P
C_K = C_LOW + P
C_TI = C_K + NB * KT
C_ER = C_TI + TILES
C_P = C_ER + NE
C_ID = C_P + 1
C_IDZ = C_ID + NB * CH
C_ALL = C_IDZ + 2 * NE


def constants():
    c = np.zeros((P, C_ALL), np.float32)
    n = np.arange(P)
    c[:, C_IDENT:C_IDENT + P] = np.eye(P)
    c[:, C_MASKQ:C_MASKQ + P] = np.where(n[None, :] > n[:, None], MASKED, 0.0)
    c[:, C_MASKK:C_MASKK + P] = np.where(n[:, None] > n[None, :], MASKED, 0.0)
    inv = (1.0 / 10000.0 ** (np.arange(0, HD, 2, dtype=np.float32) / HD)).astype(np.float32)
    freq = np.arange(T, dtype=np.float32)[None, :] * inv[:, None]
    d = n // NH
    c[:, C_COS:C_COS + T] = np.cos(freq)[d % (HD // 2)]
    c[:, C_SIN:C_SIN + T] = np.sin(freq)[d % (HD // 2)] * np.where(d < HD // 2, -1, 1)[:, None]
    c[:, C_DS:C_DS + S] = (n % S)[:, None] == np.arange(S)[None, :]
    c[:, C_DD:C_DD + 8] = (n // S)[:, None] == np.arange(8)[None, :]
    j = n // S
    r = np.arange(CH)
    c[:, C_PU] = -(CH - 1 - j)
    c[:, C_PI:C_PI + CH] = -np.maximum(r[None, :] - j[:, None], 0)
    c[:, C_CM:C_CM + CH] = r[None, :] >= j[:, None]
    c[:, C_ONE:C_ONE + P] = 1.0
    c[:, C_LOW:C_LOW + P] = n[:, None] < n[None, :]
    c[:, C_K:C_K + NB * KT] = P * np.arange(NB * KT)
    c[:, C_TI:C_TI + TILES] = np.arange(TILES)
    c[:, C_ER:C_ER + NE] = REGION * np.arange(NE) - 1
    c[:, C_P] = n
    c[:, C_ID:C_ID + NB * CH] = (np.arange(NB)[None, :, None] * T + CH * n[:, None, None]
                                 + np.arange(CH)[None, None, :]).reshape(P, NB * CH)
    c[:, C_IDZ:C_IDZ + 2 * NE] = NB * T + n[:, None] + P * np.arange(2 * NE)[None, :]
    return c


class Chain:

    def __init__(self, eng, sem):
        self.eng, self.sem, self.base, self.n = eng, sem, 0, 0

    def done(self, ins):
        ins.then_inc(self.sem, 1)
        self.n += 1

    def sync(self):
        self.eng.wait_ge(self.sem, self.base + self.n)

    def link(self, ins):
        self.done(ins)
        self.sync()


def max_units():
    out = []
    for t in range(KT):
        for chunk in range(2 if t >= 4 else 1):
            n = min(P * (t + 1) - 512 * chunk, 512)
            k = 4 if n == 128 else 2 if n == 256 else 1
            out += [(t, 512 * chunk, n, tuple(range(h, h + k)), chunk) for h in range(0, 4, k)]
    return out


def exp_units():
    out = []
    for half in range(2):
        for j in range(4 * (half + 1)):
            q0 = max(P * j, 512 * half)
            n = 512 * (half + 1) - q0
            k = 4 if n <= 256 else 2
            out += [(half, j, q0, n, tuple(range(h, h + k))) for h in range(0, 4, k)]
    return out


MAXU = max_units()
EXPU = exp_units()


def place(n, heads, i):
    at = heads.index(i)
    per = 4 if n == 128 else 2 if n == 256 else 1
    return at // per, (at % per) * n


def layer_kernel(nc, const, x, log_a, b_w, c_w, d_vec, ln1_w, ln1_b, ln2_w, ln2_b, conv_w,
                 attn_w, proj_w, router_w, expert_wv, expert_proj, out):
    ctx = ExitStack()
    with ctx:
        def sb(name, shape, dt=F32):
            return ctx.enter_context(nc.sbuf_tensor(name, shape, dt))

        def sem(name):
            return ctx.enter_context(nc.semaphore(name))

        cst = sb("cst", [P, C_COS])
        small = sb("small", [P, C_ALL - C_DS])

        def con(at, n):
            return small[:, at - C_DS:at - C_DS + n]

        ident = cst[:, C_IDENT:C_IDENT + P]
        ident_b = sb("ident_b", [P, P], BF16)
        mask_q = sb("mask_q", [P, P], BF16)
        mask_k = sb("mask_k", [P, P], BF16)
        w_qkv = sb("w_qkv", [P, 3 * D])
        w_qk = sb("w_qk", [P, 2 * D])
        w_rot = sb("w_rot", [P, 2 * D])
        w_proj = sb("w_proj", [P, D])
        w_router = sb("w_router", [P, NE])
        vecs = sb("vecs", [P, 8])
        x1 = sb("x1", [P, NB, CH, D])
        v_all = sb("v_all", [P, NB, KT, NH, VC])
        o_all = sb("o_all", [P, NB, KT, D])
        eps_t = sb("eps_t", [P, 1])
        ones = sb("ones", [32, P])
        zero3 = sb("zero3", [3, T], BF16)
        region = nc.sbuf_base + 64 - nc.sbuf_base % 64

        class Region:

            def __init__(self):
                self.at = region

            def __call__(self, name, shape, dt=F32):
                size = int(np.prod(shape[1:])) * (2 if dt == BF16 else 4)
                t = nc.alloc_sbuf_tensor_at(name, shape, dt, offset=self.at)
                self.at += -(-size // 64) * 64
                assert self.at <= nc.sbuf_usable_end, (name, self.at)
                return t

        ra = Region()
        w_state = ra("w_state", [P, D, S])
        w_carry = ra("w_carry", [P, G, CH, 8])
        w_chunk = ra("w_chunk", [P, G, CH, 8])
        decay = ra("decay", [P, G, P])
        b_pad = ra("b_pad", [P, 240])
        d_one = ra("d_one", [P, D])
        xt = [ra(f"xt{u}", [P, CH, D]) for u in range(2)]
        xT = [ra(f"xT{u}", [P, CH, P]) for u in range(2)]
        bt = [ra(f"bt{u}", [P, P]) for u in range(2)]
        hs = [ra(f"hs{u}", [P, G * P + 16]) for u in range(2)]
        ra.at = max(ra.at, region + 8 * 4 * T * 2)
        hz = [ra(f"hz{u}", [P, CH, D]) for u in range(2)]
        cos = ra("cos", [P, T])
        sin = ra("sin", [P, T])
        hT = [ra(f"hT{u}", [P, T + 2]) for u in range(2)]
        hc = [ra(f"hc{u}", [P, T]) for u in range(2)]
        tq = [ra(f"tq{k}", [P, T]) for k in range(2)]
        tr = [ra(f"tr{k}", [P, T]) for k in range(2)]
        part = [[ra(f"part{k}_{j}", [P, T], BF16) for j in range(3)] for k in range(2)]
        st = [ra(f"st{u}", [P, CH, 6]) for u in range(2)]
        mv = [ra(f"mv{u}", [P, CH, 2]) for u in range(2)]
        hv = [ra(f"hv{u}", [P, 4, CH]) for u in range(2)]
        sc = [ra(f"sc{u}", [P, 8, CH]) for u in range(2)]
        lg_d = ra("lg_d", [P, S])
        cw_d = ra("cw_d", [P, S])
        lg_g = ra("lg_g", [G, P])
        cw_g = ra("cw_g", [G, P])
        bw_s = ra("bw_s", [S, P])
        a_rep = ra("a_rep", [P, CH, S])
        c_rep = ra("c_rep", [P, CH, S])
        aT = ra("aT", [P, P])
        cT = ra("cT", [P, P])
        aG = ra("aG", [P, G])
        cG = ra("cG", [P, G])
        pu = ra("pu", [P, P])
        pi = ra("pi", [P, CH, D])
        ph = ra("ph", [P, CH, G])
        phc = ra("phc", [P, CH, G])

        rb = Region()
        qs, ks = [], []
        for g in range(HG):
            qs.append(rb(f"qs{g}", [P, 4, T], BF16))
            ks.append(rb(f"ks{g}", [P, 4, T], BF16))
        vs = [rb(f"vs{g}", [P, KT, 4, VW]) for g in range(2)]
        pT = [rb(f"pT{n}", [P, T]) for n in range(4)]
        oT = [rb(f"oT{n}", [P, 512]) for n in range(2)]
        mx = [rb(f"mx{n}", [P, 4, KT]) for n in range(2)]
        mxb = [rb(f"mxb{n}", [P, 4, 4]) for n in range(2)]
        m_neg = rb("m_neg", [32, P])
        m_res = rb("m_res", [32, P])
        m_part = [rb(f"m_part{j}", [32, P], BF16) for j in range(3)]
        rden = [rb(f"rden{n}", [P, 4, 4]) for n in range(2)]

        w_exp = rb("w_exp", [P, NE, WE])

        rc = Region()
        turned_c = [rc(f"turned_c{u}", [P, T]) for u in range(2)]
        x2 = [rc(f"x2{u}", [P, CH, D]) for u in range(2)]
        table_c = rc("table_c", [P, 2])
        zz = [rc(f"zz{u}", [P, CH, DI]) for u in range(2)]
        stc = [rc(f"stc{u}", [P, CH, 6]) for u in range(2)]
        mvc = [rc(f"mvc{u}", [P, CH, 2]) for u in range(2)]
        hvc = [rc(f"hvc{u}", [P, 4, CH]) for u in range(2)]
        scc = [rc(f"scc{u}", [P, 2, CH]) for u in range(2)]
        lmax = rc("lmax", [P, CH])
        pick = rc("pick", [P, CH, NE])
        left = rc("left", [P, CH])
        rowc = rc("rowc", [P, NE])
        incl = rc("incl", [P, CH, NE])
        offs = rc("offs", [P, NE])
        last_row = rc("last_row", [P, NE])
        rank = rc("rank", [P, CH])
        count = rc("count", [P, NE])
        zero8 = rc("zero8", [P, CH])
        dest = rc("dest", [P, NB, CH], U32)
        assert rc.at <= region + 4 * 4 * T * 2
        tail = rc("tail", [P, NE], U32)
        zrow = rc("zrow", [P, 2 * NE, DI])
        above = rc("above", [P, NE, NB * KT])
        tiles_e = rc("tiles_e", [P, NE])
        cum_e = rc("cum_e", [P, NE])
        jump_e = rc("jump_e", [P, NE])
        past = rc("past", [P, TILES, NE])
        past_j = rc("past_j", [P, TILES, NE])
        tile_f = rc("tile_f", [P, 2, TILES])
        tile_expert = rc("tile_expert", [P, TILES], U32)
        tile_row = rc("tile_row", [P, TILES], U32)
        h_row = [rc(f"h_row{k}", [P, DI]) for k in range(4)]
        hT_t = [rc(f"hT_t{k}", [P, P]) for k in range(2)]
        gate = [rc(f"gate{k}", [P, DFF]) for k in range(2)]
        act_v = [rc(f"act_v{k}", [P, DFF]) for k in range(2)]
        act_T = [rc(f"act_T{k}", [P, FT, P]) for k in range(2)]
        y_row = [rc(f"y_row{k}", [P, D]) for k in range(4)]
        y_id = [rc(f"y_id{k}", [P, 1], U32) for k in range(4)]
        yg = rc("yg", [P, NB, CH, D])
        assert rc.at <= rb.at - 4 * NE * WE

        ps = ctx.enter_context(nc.psum_tensor("ps", [P, 8, 512], F32))

        def banks(a, n):
            return ps[:, a:a + n, :].rearrange("p a c -> p (a c)")

        q_parts = nc.dram_tensor("q_parts", (NB, 3, HD, NH, T), BF16, kind="Internal").ap()
        k_parts = nc.dram_tensor("k_parts", (NB, 3, HD, NH, T), BF16, kind="Internal").ap()

        h_sorted = nc.dram_tensor("h_sorted", (ROWS, DI), F32, kind="Internal").ap()
        y_rows = nc.dram_tensor("y_rows", (NB * T + 2 * NE * P, D), F32, kind="Internal").ap()

        x_v = x.rearrange("b (p r) d -> b p r d", r=CH)
        out_v = out.rearrange("b (p r) d -> b p r d", r=CH)

        s_params = sem("params_loaded")
        s_weights = sem("weights_loaded")
        s_experts = sem("experts_loaded")
        s_set_act = sem("setup_act")
        s_set_dve = sem("setup_dve")
        s_set_pool = sem("setup_pool")
        s_set_pe = sem("setup_pe")
        s_x = [sem(f"x_loaded{u}") for u in range(2)]
        s_xtr = [sem(f"x_transposed{u}") for u in range(2)]
        s_xTa = [sem(f"xT_copied_act{u}") for u in range(2)]
        s_xTd = [sem(f"xT_copied_dve{u}") for u in range(2)]
        s_bt = [sem(f"inputs_projected{u}") for u in range(2)]
        s_btc = [sem(f"inputs_copied{u}") for u in range(2)]
        s_u = [sem(f"chunk_states_ready{u}") for u in range(2)]
        s_scan = [sem(f"states_scanned{u}") for u in range(2)]
        s_xd = [sem(f"x_weighted{u}") for u in range(2)]
        s_y = [sem(f"mixer_ready{u}") for u in range(2)]
        s_var = [sem(f"variance_ready{u}") for u in range(2)]
        s_sd = [sem(f"deviation_ready{u}") for u in range(2)]
        s_x1 = [sem(f"x1_ready{u}") for u in range(2)]
        s_hz = [sem(f"hz_ready{u}") for u in range(2)]
        s_hzt = [sem(f"hz_transposed{u}") for u in range(2)]
        s_hT = [sem(f"hT_ready{u}") for u in range(2)]
        s_hc = [sem(f"conv_ready{u}") for u in range(2)]
        s_qk = [sem(f"qk_projected{u}") for u in range(2)]
        s_rope = [sem(f"qk_turned{u}") for u in range(2)]
        s_v = [sem(f"v_projected{u}") for u in range(2)]
        s_vc = [sem(f"v_copied{u}") for u in range(2)]
        s_sum = [sem(f"qk_summed{k}") for k in range(2)]
        s_cast1 = [sem(f"part1_ready{k}") for k in range(2)]
        s_rest1 = [sem(f"rest1_ready{k}") for k in range(2)]
        s_cast2 = [sem(f"part2_ready{k}") for k in range(2)]
        s_cast3 = [sem(f"part3_ready{k}") for k in range(2)]
        s_stored = [sem(f"parts_stored{k}") for k in range(2)]
        s_dve = sem("dve_step")
        s_pool = sem("pool_step")
        s_clear = sem("slots_cleared")
        s_qclear = sem("last_query_slots_cleared")
        s_vclear = sem("values_cleared")
        s_stage = [sem(f"slot_staged{g}") for g in range(HG)]
        s_mrow = sem("max_rows_written")
        s_vst = sem("values_staged")
        s_ms = sem("max_scores_ready")
        s_mr = sem("max_reduced")
        s_mg = sem("group_maxima_ready")
        s_mt = sem("maxima_transposed")
        s_mn = sem("maxima_negated")
        s_mpc = sem("max_part_steps")
        s_mp = sem("max_parts_ready")
        s_es = sem("exp_scores_ready")
        s_ex = sem("exp_done")
        s_pv = sem("unit_weighted")
        s_oc = sem("half_copied")
        s_ot = sem("half_transposed")
        s_on = sem("half_normalised")
        s_otr = sem("o_transposed")
        s_oca = sem("o_turned")
        s_pj = sem("projected")
        s_x2 = sem("x2_ready")
        s_acc = sem("x1_x2_summed")
        s_varc = sem("variance2_ready")
        s_sdc = sem("deviation2_ready")
        s_zz = sem("zz_ready")
        s_zt = sem("zz_transposed")
        s_h2 = sem("h2_turned")
        s_lg = sem("logits_ready")
        s_rc = sem("rows_counted")
        s_rp = sem("ranks_ready")
        s_dest = sem("rows_chosen")
        s_varf = [sem(f"variance3_ready{u}") for u in range(2)]
        s_sdf = [sem(f"deviation3_ready{u}") for u in range(2)]
        s_scat = [sem(f"tokens_scattered{u}") for u in range(2)]
        s_plan = sem("tiles_planned")
        s_tail = sem("tails_cleared")
        s_zrow = sem("zeros_ready")
        s_ysc = sem("expert_out_released")
        s_id = sem("token_numbers_kept")
        s_aT = sem("activations_transposed")
        s_aTc = sem("activations_turned")
        s_zero = sem("spare_rows_cleared")
        s_hrow = [sem(f"tokens_loaded{k}") for k in range(4)]
        s_tT = sem("tokens_transposed")
        s_hTt = sem("tokens_turned")
        s_gv = sem("gate_value_ready")
        s_sg = sem("gate_silu_ready")
        s_av = sem("activations_ready")
        s_yy = sem("expert_out_ready")
        s_yr = sem("expert_out_copied")
        s_yst = [sem(f"expert_out_stored{k}") for k in range(4)]
        s_yg = [sem(f"expert_out_loaded{u}") for u in range(2)]
        s_fin = [sem(f"sum_ready{u}") for u in range(2)]
        s_res = [sem(f"result_ready{u}") for u in range(2)]
        s_nb = [sem(f"shift_ready{u}") for u in range(2)]
        s_resa = [sem(f"result_ready_act{u}") for u in range(2)]
        s_out = [sem(f"result_stored{u}") for u in range(2)]

        block = ctx.enter_context(nc.Block())

        VC_CREDIT = ROPE_CREDIT = CAST3_CREDIT = 1
        STORED_CREDIT = 16
        MR_CREDIT, EX_CREDIT, PV_CREDIT, OC_CREDIT, OT_CREDIT = 2, 2, 4, 1, 2
        OUT_CREDIT, RES_CREDIT = 16, 1
        NMU, NEU = len(MAXU), len(EXPU)
        STAGE = 16 * 5
        MROW = 16 * 3
        HALF0 = sum(1 for e in EXPU if e[0] == 0)
        HEAD = 13
        TAILU = NEU - HEAD
        LAST = NEU + TAILU

        AT_O = (0, 5, 15, 30)
        AT_P = (2, 12, 23, 33)
        AT_Z = (7, 18, 29, 38)
        AT_L = (9, 20, 31, 39)
        AT_R = (11, 22, 34, 40)
        AT_END = 41
        BANK_O, BANK_P, BANK_L, BANK_R = (6, 6, 6, 0), (6, 6, 6, 2), (6, 6, 6, 4), (7, 7, 7, 5)

        def tile_turn(k, slot):
            if isinstance(k, int):
                return 16 * (k // 4 + 1)
            return 4 * (k - slot) + 16

        @block.sync
        def _(sp):
            for dst, src in (
                (cst[:, :], const[:, 0:C_COS]), (small[:, :], const[:, C_DS:C_ALL]),
                (lg_d[:, :], log_a), (cw_d[:, :], c_w),
                (lg_g[:, :], log_a.rearrange("(g e) s -> g (e s)", e=8)),
                (cw_g[:, :], c_w.rearrange("(g e) s -> g (e s)", e=8)),
                (bw_s[:, :], b_w), (d_one[:, :], d_vec.rearrange("(o d) -> o d", o=1).broadcast_to([P, D])),
            ):
                sp.dma_start(dst, src).then_inc(s_params, 16)
            for u in range(2):
                sp.dma_start(xt[u][:, :, :], x_v[u]).then_inc(s_x[u], 16)
            for dst, src in (
                (w_qkv[:, :], attn_w), (cos[:, :], const[:, C_COS:C_COS + T]),
                (sin[:, :], const[:, C_SIN:C_SIN + T]),
                (w_proj[:, :], proj_w), (w_router[:, :], router_w),
                (vecs[:, 0:1], ln1_w.rearrange("(d o) -> d o", o=1)),
                (vecs[:, 1:2], ln1_b.rearrange("(d o) -> d o", o=1)),
                (vecs[:, 2:3], ln2_w.rearrange("(d o) -> d o", o=1)),
                (vecs[:, 3:4], ln2_b.rearrange("(d o) -> d o", o=1)),
                (vecs[:, 4:7], conv_w.rearrange("c o k -> c (o k)")),
            ):
                sp.dma_start(dst, src).then_inc(s_weights, 16)
            for u in range(2):
                sp.wait_ge(s_y[u], 1)
                sp.dma_start(xt[u][:, :, :], x_v[2 + u]).then_inc(s_x[u], 16)

            with sp.Fori(0, 2) as i:
                for u in range(2):
                    for k, dram in ((0, q_parts), (1, k_parts)):
                        for j, s, credit in ((0, s_cast1, 0), (1, s_cast2, 0), (2, s_cast3, CAST3_CREDIT)):
                            sp.wait_ge(s[k], 2 * i + u + 1 + credit)
                            dst = dram[2 * i + u].rearrange("j d h t -> j (d h) t")[j]
                            sp.dma_start(dst, part[k][j][:, :]
                                         ).then_inc(s_stored[k], 16)

            for k in range(2):
                sp.wait_ge(s_stored[k], 16 * 3 * (NB - 1) + STORED_CREDIT)
            def stage(b, g):
                q_g = q_parts[b].rearrange("j d h t -> (j d) (h t)")[:, 4 * g * T:4 * (g + 1) * T]
                k_g = k_parts[b].rearrange("j d h t -> (j d) (h t)")[:, 4 * g * T:4 * (g + 1) * T]
                sp.dma_start(qs[g][0:72, :, :].rearrange("p h t -> p (h t)"),
                             q_g.unsqueeze(0).broadcast_to([3, 24, 4 * T])
                             ).then_inc(s_stage[g], 16)
                for i in range(3):
                    sp.dma_start(ks[g][24 * i:24 * i + 24, :, :].rearrange("p h t -> p (h t)"),
                                 k_g[8 * i:8 * i + 8].unsqueeze(0).broadcast_to([3, 8, 4 * T])
                                 ).then_inc(s_stage[g], 16)
                sp.dma_start(qs[g][96:99, :, :], zero3[:, :].unsqueeze(1).broadcast_to([3, 4, T])
                             ).then_inc(s_stage[g], 16)

            def max_rows(n, g):
                sp.wait_ge(s_mp, n + 1)
                for j in range(3):
                    sp.dma_start(qs[g][96 + j:97 + j, :, :], m_part[j][:, :]).then_inc(s_mrow, 16)

            for g in range(HG):
                sp.wait_ge(s_clear, g + 1)
                if g >= 2:
                    sp.wait_ge(s_qclear, g - 1)
                stage(0, g)
                if g == 1:
                    for u in range(2):
                        sp.wait_ge(s_stored[u], 16 * 3 * NB + STORED_CREDIT)
                        sp.wait_ge(s_vc[u], 2 + VC_CREDIT)
                    for e in range(NE):
                        sp.dma_start(w_exp[:, e, 0:2 * DFF], expert_wv[e]).then_inc(s_experts, 16)
                        sp.dma_start(w_exp[:, e, 2 * DFF:WE].rearrange("p (f d) -> p f d", d=D),
                                     expert_proj[e].rearrange("(f p) d -> p f d", p=P)
                                     ).then_inc(s_experts, 16)

            for g in range(HG):
                if g >= 1:
                    max_rows(g - 1, g - 1)
                if g >= 2:
                    sp.wait_ge(s_es, NEU * (g - 1))
                    stage(1, g - 2)
            with sp.Fori(1, NB - 1) as b:
                for g in range(HG):
                    max_rows(4 * b + g - 1, (g + 3) % 4)
                    sp.wait_ge(s_es, NEU * (4 * b + g - 1))
                    stage(b + 1 if g >= 2 else b, (g + 2) % 4)
            for g in range(HG):
                n = 4 * (NB - 1) + g
                max_rows(n - 1, (g + 3) % 4)
                if g < 2:
                    sp.wait_ge(s_es, NEU * (n - 1))
                    stage(NB - 1, g + 2)
            max_rows(4 * NB - 1, 3)

            sp.wait_ge(s_zrow, 1)
            sp.dma_start(h_sorted[NE * REGION:ROWS, :].rearrange("(e p) d -> p e d", p=P),
                         zrow[:, NE:2 * NE, :]).then_inc(s_zero, 16)
            sp.wait_ge(s_plan, 1)
            for e in range(NE):
                row = sp.value_load(tail[0:1, e:e + 1], min_val=0, max_val=ROWS - P)
                sp.dma_start(h_sorted[bass.ds(row, P), :], zrow[:, e, :]).then_inc(s_tail, 16)
            rows = [sp.value_load(tile_row[0:1, k:k + 1], min_val=0, max_val=ROWS - P) for k in range(4)]
            sp.wait_ge(s_zero, 16)
            sp.wait_ge(s_tail, 16 * NE)
            for u in range(2):
                sp.wait_ge(s_scat[u], 16 * 2 * CH)
            for k in range(4):
                sp.dma_start(h_row[k][:, :], h_sorted[bass.ds(rows[k], P), :]).then_inc(s_hrow[k], 16)

            def load_tile(k, slot):
                sp.wait_ge(s_tT, k - 3)
                sp.wait_ge(s_id, k - 3)
                row = sp.value_load(tile_row[0:1, bass.ds(k, 1)], min_val=0, max_val=ROWS - P)
                sp.dma_start(h_row[slot][:, :], h_sorted[bass.ds(row, P), :]).then_inc(s_hrow[slot], 16)

            with sp.Fori(1, TILES // 4) as m:
                for j in range(4):
                    load_tile(4 * m + j, j)

            for k in range(4):
                sp.wait_ge(s_yst[k], tile_turn(TILES - 4 + k, k))
            for i in range(2):
                for u in range(2):
                    b = 2 * i + u
                    if i > 0:
                        sp.wait_ge(s_yg[u], 16 * i)
                    sp.dma_start(yg[:, b, :, :], y_rows[b * T:(b + 1) * T, :].rearrange("(p r) d -> p r d", r=CH)
                                 ).then_inc(s_yg[u], 16)

            with sp.Fori(0, 2) as i:
                for u in range(2):
                    sp.wait_ge(s_res[u], i + 1 + RES_CREDIT)
                    sp.wait_ge(s_resa[u], i + 1 + RES_CREDIT)
                    sp.dma_start(out_v[2 * i + u], zz[u][:, :, 0:D]).then_inc(s_out[u], 16)
            for u in range(2):
                sp.wait_ge(s_out[u], 32 + OUT_CREDIT)

        @block.tensor
        def _(pe):
            mm = nc.tensor.matmul

            def tp(out_, in_, k=P):
                return nc.tensor.transpose(out_, in_, ident[0:k, 0:k])

            pe.sem_inc(s_mr, MR_CREDIT)
            pe.sem_inc(s_ex, EX_CREDIT)
            for u in range(2):
                pe.sem_inc(s_vc[u], VC_CREDIT)
                pe.sem_inc(s_rope[u], ROPE_CREDIT)
            pe.sem_inc(s_oc, OC_CREDIT)

            pe.wait_ge(s_params, 16 * 8)
            tp(ps[:, 0, 0:S], bw_s[:, :], S).then_inc(s_set_pe, 1)
            pe.wait_ge(s_set_dve, 1)
            tp(ps[:, 1, 0:P], a_rep[:, :, :].rearrange("d j s -> d (j s)"))
            tp(ps[:, 1, P:2 * P], c_rep[:, :, :].rearrange("d j s -> d (j s)"))
            tp(ps[:, 2, 0:G], lg_g[:, :], G)
            tp(ps[:, 2, G:2 * G], cw_g[:, :], G).then_inc(s_set_pe, 1)
            pe.wait_ge(s_set_dve, 2)

            with pe.Fori(0, 2) as i:
                for u in range(2):
                    pe.wait_ge(s_x[u], 16 * i + 16)
                    pe.wait_ge(s_vc[u], i + VC_CREDIT)
                    for r in range(CH):
                        last = tp(ps[:, 4 * u + r // 4, (r % 4) * P:(r % 4 + 1) * P], xt[u][:, r, :])
                    last.then_inc(s_xtr[u], 1)
                for u in range(2):
                    pe.wait_ge(s_xTa[u], i + 1)
                    pe.wait_ge(s_xTd[u], i + 1)
                    pe.wait_ge(s_rope[u], 2 * i + ROPE_CREDIT)
                    for j in range(CH):
                        last = mm(ps[:, 4 * u + 2, 0:P], b_pad[:, 112 - S * j:240 - S * j], xT[u][:, j, :],
                                  start=(j == 0), stop=(j == CH - 1))
                    last.then_inc(s_bt[u], 1)
                pe.wait_ge(s_set_dve, 3)
                for u in range(2):
                    pe.wait_ge(s_btc[u], i + 1)
                    for g in range(G):
                        last = mm(ps[:, 4 * u + g // 4, (g % 4) * P:(g % 4 + 1) * P],
                                  w_state[:, 8 * g:8 * g + 8, :].rearrange("p d s -> p (d s)"), bt[u][:, :],
                                  start=(g % 4 == 0), stop=True, skip_group_check=True)
                    last.then_inc(s_u[u], 1)
                for u in range(2):
                    pe.wait_ge(s_scan[u], i + 1)
                    pe.wait_ge(s_xd[u], i + 1)
                    for h in range(2):
                        y = ps[:, 4 * u + h, :]
                        mm(y, bt[u][:, :], w_chunk[:, 8 * h:8 * h + 8, :, :].rearrange("p g r e -> p (g r e)"),
                           start=True, stop=False, skip_group_check=True)
                        mm(y, ident, xt[u][:, :, :].rearrange("p r (g e) -> p g r e", e=8)[:, 8 * h:8 * h + 8, :, :],
                           start=False, stop=False, skip_group_check=True)
                        for g in range(8):
                            last = mm(y[:, 64 * g:64 * g + 64], hs[u][:, (8 * h + g) * P:(8 * h + g + 1) * P],
                                      w_carry[:, 8 * h + g, :, :].rearrange("p r e -> p (r e)"),
                                      start=False, stop=True, skip_group_check=True)
                    last.then_inc(s_y[u], 1)

                def turn_hz(u):
                    pe.wait_ge(s_hz[u], i + 1)
                    for r in range(CH):
                        last = tp(ps[:, 4 * u + 2 + r // 4, (r % 4) * P:(r % 4 + 1) * P], hz[u][:, r, :])
                    last.then_inc(s_hzt[u], 1)

                def project_qk(u, k):
                    if k == 0:
                        pe.wait_ge(s_hc[u], i + 1)
                    else:
                        pe.wait_ge(s_rope[u], 2 * i + 1 + ROPE_CREDIT)
                    for w, at in ((w_qk, 0), (w_rot, 2)):
                        for h in range(2):
                            last = mm(ps[:, 4 * u + at + h, :], w[:, k * D:(k + 1) * D],
                                      hc[u][:, 512 * h:512 * h + 512], start=True, stop=True)
                    last.then_inc(s_qk[u], 1)

                turn_hz(0)
                pe.wait_ge(s_set_pool, 1)
                pe.wait_ge(s_weights, 16 * 10)
                project_qk(0, 0)
                turn_hz(1)
                project_qk(0, 1)
                project_qk(1, 0)
                project_qk(1, 1)
                for u in range(2):
                    pe.wait_ge(s_rope[u], 2 * i + 2 + ROPE_CREDIT)
                    for t in range(KT):
                        last = mm(ps[:, 4 * u + t // 4, (t % 4) * P:(t % 4 + 1) * P],
                                  hc[u][:, t * P:(t + 1) * P], w_qkv[:, 2 * D:3 * D],
                                  start=(t % 4 == 0), stop=True, skip_group_check=True)
                    last.then_inc(s_v[u], 1)

            for u in range(2):
                pe.wait_ge(s_vc[u], 2 + VC_CREDIT)
            MISC, OBANK, MBANK = 5, 4, 6

            def max_unit(n, b, g, idx):
                t, k0, nk, heads, chunk = MAXU[idx]
                bank = MBANK + idx % 2
                if idx == 0:
                    pe.wait_ge(s_stage[g], STAGE * (b + 1))
                pe.wait_ge(s_mr, NMU * n + idx - 1 + MR_CREDIT)
                diag = k0 + nk == P * (t + 1)
                for a, h in enumerate(heads):
                    last = mm(ps[:, bank, a * nk:(a + 1) * nk], qs[g][:, h, t * P:(t + 1) * P],
                              ks[g][:, h, k0:k0 + nk], start=(a == 0),
                              stop=(not diag), skip_group_check=True)
                if diag:
                    m = len(heads)
                    o = ps[:, bank, 0:m * nk].rearrange("p (h k) -> p h k", h=m)[:, :, nk - P:nk]
                    last = mm(o, ident_b[:, :], mask_q[:, :].unsqueeze(1).broadcast_to([P, m, P]),
                              start=False, stop=True, skip_group_check=True)
                last.then_inc(s_ms, 1)

            def exp_unit(n, g, idx):
                half, j, q0, nq, heads = EXPU[idx]
                pair = 2 * (idx % 2)
                if idx == 0:
                    pe.wait_ge(s_mrow, MROW * (n + 1))
                pe.wait_ge(s_ex, NEU * n + idx - 1 + EX_CREDIT)
                diag = q0 == P * j
                for h in heads:
                    bank, col = place(nq, heads, h)
                    first = col == 0
                    last = mm(ps[:, pair + bank, col:col + nq], ks[g][:, h, j * P:(j + 1) * P],
                              qs[g][:, h, q0:q0 + nq], start=first, stop=(not diag), skip_group_check=True)
                if diag:
                    per = 4 if nq == 128 else 2 if nq == 256 else 1
                    for bank in range(len(heads) // per):
                        o = ps[:, pair + bank, 0:per * nq].rearrange("p (h q) -> p h q", h=per)[:, :, 0:P]
                        last = mm(o, ident_b[:, :], mask_k[:, :].unsqueeze(1).broadcast_to([P, per, P]),
                                  start=False, stop=True, skip_group_check=True)
                last.then_inc(s_es, 1)

            def weigh(n, par, idx):
                half, j, q0, nq, heads = EXPU[idx]
                if idx == 0:
                    pe.wait_ge(s_vst, n + 1)
                if j == 0 and heads[0] == 0:
                    pe.wait_ge(s_oc, 2 * n + half + OC_CREDIT)
                pe.wait_ge(s_ex, NEU * n + idx + 1 + EX_CREDIT)
                for a, h in enumerate(heads):
                    last = mm(ps[VW * h:VW * h + VW, OBANK, q0 - 512 * half:512],
                              vs[par][:, j, h, :], pT[idx % 4][:, a * nq:(a + 1) * nq],
                              start=(j == 0), stop=(j == 4 * half + 3), skip_group_check=True)
                last.then_inc(s_pv, 1)

            def turn_max(n, par):
                pe.wait_ge(s_mg, n + 1)
                tp(ps[0:32, MISC, 0:P], mx[par][:, :, :].rearrange("p h t -> p (h t)")).then_inc(s_mt, 1)

            def turn_out(n, half):
                pe.wait_ge(s_oc, 2 * n + half + 1 + OC_CREDIT)
                for t in range(4):
                    last = tp(ps[:, MISC, t * P:(t + 1) * P], oT[half][:, t * P:(t + 1) * P])
                last.then_inc(s_ot, 1)

            def beside(at):
                for b in range(NB):
                    if at == AT_O[b]:
                        turn_o(b)
                    if at == AT_P[b]:
                        project(b)
                    if at == AT_Z[b]:
                        turn_normal(b)
                    if at == AT_L[b]:
                        logits(b)
                    if at == AT_R[b]:
                        count_before(b)

            def turn_o(b):
                pe.wait_ge(s_on, 2 * 4 * (b + 1))
                if b == 0:
                    pe.wait_ge(s_mr, NMU * 4 * NB + MR_CREDIT)
                elif b < NB - 1:
                    pe.wait_ge(s_x2, b)
                for t in range(KT):
                    last = tp(ps[:, BANK_O[b] + t // 4, (t % 4) * P:(t % 4 + 1) * P], o_all[:, b, t, :])
                last.then_inc(s_otr, 1)

            def project(b):
                pe.wait_ge(s_oca, b + 1)
                if 0 < b < NB - 1:
                    pe.wait_ge(s_dest, b)
                oc = turned_c[b % 2][:, :].rearrange("c (p r) -> c p r", r=CH)
                for r in range(CH):
                    last = mm(ps[:, BANK_P[b] + r // 4, (r % 4) * P:(r % 4 + 1) * P], oc[:, :, r], w_proj[:, :],
                              start=(r % 4 == 0), stop=True, skip_group_check=True)
                last.then_inc(s_pj, 1)

            def turn_normal(b):
                pe.wait_ge(s_zz, b + 1)
                if b < NB - 2:
                    pe.wait_ge(s_oca, b + 2)
                for r in range(CH):
                    last = tp(ps[:, BANK_O[b] + r // 4, (r % 4) * P:(r % 4 + 1) * P], zz[b % 2][:, r, 0:D])
                last.then_inc(s_zt, 1)

            def logits(b):
                pe.wait_ge(s_h2, b + 1)
                for r in range(CH):
                    last = mm(ps[:, BANK_L[b], r * NE:(r + 1) * NE], turned_c[b % 2][:, r * P:(r + 1) * P],
                              w_router[:, :], start=(r == 0), stop=True, skip_group_check=True)
                last.then_inc(s_lg, 1)

            def count_before(b):
                pe.wait_ge(s_rc, b + 1)
                mm(ps[:, BANK_R[b], 0:NE], con(C_LOW, P), rowc[:, :], start=True, stop=True, skip_group_check=True)
                mm(ps[:, BANK_R[b], NE:2 * NE], con(C_ONE, P), rowc[:, :], start=False, stop=True,
                   skip_group_check=True).then_inc(s_rp, 1)

            def step(n, mb, g, maxima=True, tail=True, head=True, at=None):
                done_m = 0
                lo, lo_g = n - 2, (g + 2) % 4
                hi, hi_g = n - 1, (g + 3) % 4
                for k in range(TAILU + (HEAD if head else 0)):
                    if k < TAILU and tail:
                        exp_unit(lo, lo_g, HEAD + k)
                    if k >= TAILU:
                        exp_unit(hi, hi_g, k - TAILU)
                    if maxima:
                        max_unit(n, mb, g, done_m)
                        done_m += 1
                    if at is not None:
                        beside(at + k)
                    if k == 1 and head:
                        if tail and not (isinstance(n, int) and n < 3):
                            pe.wait_ge(s_on, 2 * (n - 2))
                        elif tail:
                            pe.wait_ge(s_mn, n - 1)
                        turn_max(hi, (g + 1) % 2)
                    if k == 5 and tail:
                        if head:
                            pe.wait_ge(s_mn, n)
                        else:
                            pe.wait_ge(s_on, 2 * lo)
                        turn_out(lo, 0)
                    if k == 12 and tail:
                        pe.wait_ge(s_on, 2 * lo + 1)
                        turn_out(lo, 1)
                    if k - 2 < TAILU:
                        if tail:
                            weigh(lo, lo_g % 2, HEAD + k - 2)
                    else:
                        weigh(hi, hi_g % 2, k - 2 - TAILU)
                    if maxima and done_m < (k + 1) * NMU // NEU:
                        max_unit(n, mb, g, done_m)
                        done_m += 1

            for done_m in range(NMU):
                max_unit(0, 0, 0, done_m)
            step(1, 0, 1, tail=False)
            step(2, 0, 2)
            step(3, 0, 3)
            with pe.Fori(1, NB) as b:
                for g in range(HG):
                    step(4 * b + g, b, g)
            step(4 * NB, None, 0, maxima=False, at=0)
            step(4 * NB + 1, None, 1, maxima=False, head=False, at=NEU)
            for k in (NEU - 2, NEU - 1):
                weigh(4 * NB - 1, 1, k)
            pe.wait_ge(s_on, 2 * 4 * NB - 1)
            turn_out(4 * NB - 1, 1)

            for at in range(LAST, AT_END):
                beside(at)

            pe.wait_ge(s_experts, 16 * 2 * NE)
            pe.wait_ge(s_on, 2 * 4 * NB)
            pe.wait_ge(s_dest, NB)
            HBANK, YBANK = 6, 7

            def expert(k):
                return pe.value_load(tile_expert[0:1, bass.ds(k, 1)], min_val=0, max_val=NE - 1)

            def turn_tile(k, s4):
                pe.wait_ge(s_hrow[s4], tile_turn(k, s4))
                if not isinstance(k, int) or k > 0:
                    pe.wait_ge(s_hTt, k)
                tp(ps[:, HBANK, 0:P], h_row[s4][:, 0:D]).then_inc(s_tT, 1)

            def up(k, s2, first=False):
                e = expert(k)
                pe.wait_ge(s_hTt, k + 1)
                if not first:
                    pe.wait_ge(s_av, k - 1)
                for v in range(2):
                    mm(ps[:, 2 * s2 + v, :], hT_t[s2][:, :], w_exp[:, e, v * DFF:(v + 1) * DFF],
                       start=True, stop=True).then_inc(s_gv, 1)

            def turn_activations(k, s2, first=False):
                pe.wait_ge(s_av, k + 1)
                if not first:
                    pe.wait_ge(s_aTc, k - 1)
                for f in range(FT):
                    last = tp(ps[:, 4 + s2, f * P:(f + 1) * P], act_v[s2][:, f * P:(f + 1) * P])
                last.then_inc(s_aT, 1)

            def down(k, s2, first=False):
                e = expert(k)
                pe.wait_ge(s_aTc, k + 1)
                if not first:
                    pe.wait_ge(s_yr, k)
                for f in range(FT):
                    at = 2 * DFF + f * D
                    last = mm(ps[:, YBANK, 0:D], act_T[s2][:, f, :], w_exp[:, e, at:at + D],
                              start=(f == 0), stop=(f == FT - 1))
                last.then_inc(s_yy, 1)

            def work(k, j, start=4):
                up(k, j % 2, first=(start < 2))
                turn_tile(k + 1, (j + 1) % 4)
                if start > 0:
                    turn_activations(k - 1, (j + 1) % 2, first=(start < 3))
                if start > 1:
                    down(k - 2, j % 2, first=(start < 3))

            turn_tile(0, 0)
            for k in range(4):
                work(k, k, k)
            with pe.Fori(1, TILES // 4 - 1) as m:
                for j in range(4):
                    work(4 * m + j, j)
            for j in range(3):
                work(TILES - 4 + j, j)
            up(TILES - 1, 1)
            turn_activations(TILES - 2, 0)
            down(TILES - 3, 1)
            turn_activations(TILES - 1, 1)
            down(TILES - 2, 0)
            down(TILES - 1, 1)

        @block.scalar
        def _(act):
            A = nc.scalar.activation
            for u in range(2):
                act.sem_inc(s_stored[u], STORED_CREDIT)
            act.sem_inc(s_pv, PV_CREDIT)
            act.sem_inc(s_ot, OT_CREDIT)

            act.wait_ge(s_params, 16 * 8)
            A(lg_d[:, :], lg_d[:, :], ACT.Exp)
            A(lg_g[:, :], lg_g[:, :], ACT.Exp).then_inc(s_set_act, 1)
            act.wait_ge(s_set_dve, 2)
            A(pu[:, :], aT[:, :], ACT.Exp, scale=small[:, C_PU - C_DS:C_PU - C_DS + 1])
            for r in range(CH):
                at = C_PI - C_DS + r
                A(pi[:, r, :], aT[:, :], ACT.Exp, scale=small[:, at:at + 1])
                last = A(ph[:, r, :], aG[:, :], ACT.Exp, scale=-float(r + 1))
            last.then_inc(s_set_act, 1)

            act.wait_ge(s_weights, 16 * 10)
            act.wait_ge(s_set_dve, 3)
            with act.Fori(0, 2) as i:
                for u in range(2):
                    act.wait_ge(s_xtr[u], i + 1)
                    A(xT[u][:, 0:4, :], ps[:, 4 * u, :].rearrange("p (r c) -> p r c", c=P),
                      ACT.Copy).then_inc(s_xTa[u], 1)
                for u in range(2):
                    for m in range(2):
                        act.wait_ge(s_var[u], 2 * i + m + 1)
                        src = mv[u][:, :, 1] if m == 0 else sc[u][:, 3, :]
                        A(sc[u][:, 4 * m, :], src, ACT.Sqrt, bias=eps_t[:, 0:1]).then_inc(s_sd[u], 1)
                    act.wait_ge(s_hzt[u], i + 1)
                    slots = hT[u][:, 2:T + 2].rearrange("c (p r) -> c r p", r=CH)
                    for h in range(2):
                        last = A(slots[:, 4 * h:4 * h + 4, :],
                                 ps[:, 4 * u + 2 + h, :].rearrange("c (r p) -> c r p", p=P),
                                 ACT.Identity, scale=vecs[:, 0:1], bias=vecs[:, 1:2])
                    last.then_inc(s_hT[u], 1)
                for u in range(2):
                    m = 2 * i + u
                    for k in range(2):
                        act.wait_ge(s_sum[k], m + 1)
                        act.wait_ge(s_stored[k], 48 * m + STORED_CREDIT)
                        A(part[k][0][:, :], tq[k][:, :], ACT.Copy).then_inc(s_cast1[k], 1)
                        act.wait_ge(s_rest1[k], m + 1)
                        A(part[k][1][:, :], tr[k][:, :], ACT.Copy).then_inc(s_cast2[k], 1)
                for u in range(2):
                    act.wait_ge(s_v[u], i + 1)
                    for h in range(2):
                        last = A(v_all[:, 2 * i + u, 4 * h:4 * h + 4, :, 0:HD],
                                 ps[:, 4 * u + h, :].rearrange("p (t h d) -> p t h d", t=4, d=HD), ACT.Copy)
                    last.then_inc(s_vc[u], 1)

            def negate_max(n, first=False):
                act.wait_ge(s_mt, n + 1)
                if not first:
                    act.wait_ge(s_mp, n)
                A(m_neg[:, :], ps[0:32, 5, 0:P], ACT.Copy, scale=-1.0).then_inc(s_mn, 1)

            def copy_out(n, half):
                units = HALF0 if half == 0 else NEU
                act.wait_ge(s_pv, NEU * n + units + PV_CREDIT)
                act.wait_ge(s_ot, 2 * n + half - 1 + OT_CREDIT)
                A(oT[half][:, :], ps[:, 4, :], ACT.Copy).then_inc(s_oc, 1)

            def beside(at):
                for b in range(NB):
                    if at == AT_O[b] + 1:
                        if b == 0:
                            act.wait_ge(s_es, NEU * (4 * NB - 2))
                        act.wait_ge(s_otr, b + 1)
                        if b > 1:
                            act.wait_ge(s_lg, b - 1)
                        A(turned_c[b % 2][:, :], banks(BANK_O[b], 2), ACT.Copy).then_inc(s_oca, 1)
                    if at == AT_P[b] + 4:
                        act.wait_ge(s_varc, b + 1)
                        A(scc[b % 2][:, 0, :], mvc[b % 2][:, :, 1], ACT.Sqrt, bias=eps_t[:, 0:1]).then_inc(s_sdc, 1)
                    if at == AT_Z[b] + 1:
                        act.wait_ge(s_zt, b + 1)
                        A(turned_c[b % 2][:, :], banks(BANK_O[b], 2), ACT.Identity, scale=vecs[:, 2:3],
                          bias=vecs[:, 3:4]).then_inc(s_h2, 1)

            def exp_unit(n, k):
                half, j, q0, nq, heads = EXPU[k]
                act.wait_ge(s_es, NEU * n + k + 1)
                act.wait_ge(s_pv, NEU * n + k - 3 + PV_CREDIT)
                pair = 2 * (k % 2)
                w = nq * len(heads)
                if nq == 384:
                    src = ps[:, pair:pair + 2, 0:nq]
                    dst = pT[k % 4][:, 0:w].rearrange("p (h q) -> p h q", h=2)
                else:
                    src = banks(pair, 2)[:, 0:w]
                    dst = pT[k % 4][:, 0:w]
                A(dst, src, ACT.Exp, scale=SCALE).then_inc(s_ex, 1)

            def step(n, tail=True, head=True, at=None):
                for k in range(TAILU + (HEAD if head else 0)):
                    if k < TAILU and tail:
                        exp_unit(n - 2, HEAD + k)
                    if k >= TAILU:
                        exp_unit(n - 1, k - TAILU)
                    if at is not None:
                        beside(at + k)
                    if k == 2 and head:
                        negate_max(n - 1, first=not tail)
                    if k == TAILU + 1 and tail:
                        copy_out(n - 2, 1)
                    if k == TAILU + HALF0 + 1:
                        copy_out(n - 1, 0)

            step(1, tail=False)
            step(2)
            step(3)
            with act.Fori(1, NB) as b:
                for g in range(HG):
                    step(4 * b + g)
            step(4 * NB, at=0)
            step(4 * NB + 1, head=False, at=NEU)
            copy_out(4 * NB - 1, 1)

            for at in range(LAST, AT_END + 1):
                beside(at)

            def turned(k, s2, first=False):
                act.wait_ge(s_tT, k + 1)
                if not first:
                    act.wait_ge(s_gv, 2 * (k - 1))
                A(hT_t[s2][:, :], ps[:, 6, 0:P], ACT.Identity, scale=vecs[:, 2:3], bias=vecs[:, 3:4]
                  ).then_inc(s_hTt, 1)

            def silu(k, s2, first=False):
                act.wait_ge(s_gv, 2 * k + 1)
                if not first:
                    act.wait_ge(s_av, k - 1)
                A(gate[s2][:, :], ps[:, 2 * s2, :], ACT.Silu).then_inc(s_sg, 1)

            def activations_turned(k, s2, first=False):
                act.wait_ge(s_aT, k + 1)
                if not first:
                    act.wait_ge(s_yy, k - 1)
                A(act_T[s2][:, :, :].rearrange("p f t -> p (f t)"), ps[:, 4 + s2, :], ACT.Copy
                  ).then_inc(s_aTc, 1)

            def work(k, j, start=4):
                silu(k, j % 2, first=(start < 2))
                turned(k + 1, (j + 1) % 2, first=(start < 1))
                if start > 0:
                    activations_turned(k - 1, (j + 1) % 2, first=(start < 3))

            A(table_c[:, 0:1], eps_t[:, 0:1], ACT.Silu)
            turned(0, 0, first=True)
            for k in range(4):
                work(k, k, k)
            with act.Fori(1, TILES // 4 - 1) as m:
                for j in range(4):
                    work(4 * m + j, j)
            for j in range(3):
                work(TILES - 4 + j, j)
            silu(TILES - 1, 1)
            activations_turned(TILES - 2, 0)
            activations_turned(TILES - 1, 1)

            A(table_c[:, 1:2], eps_t[:, 0:1], ACT.Sqrt)
            with act.Fori(0, 2) as i:
                for u in range(2):
                    act.wait_ge(s_varf[u], i + 1)
                    A(scc[u][:, 0, :], mvc[u][:, :, 1], ACT.Sqrt, bias=eps_t[:, 0:1]).then_inc(s_sdf[u], 1)
                    act.wait_ge(s_nb[u], i + 1)
                    act.wait_ge(s_out[u], 16 * i + OUT_CREDIT)
                    for r in range(CH // 2, CH):
                        last = A(zz[u][:, r, 0:D], x2[u][:, r, :], ACT.Identity, scale=scc[u][:, 1, r:r + 1],
                                 bias=hvc[u][:, 0, r:r + 1])
                    last.then_inc(s_resa[u], 1)

        @block.vector
        def _(dve):
            V = nc.vector
            chain = Chain(dve, s_dve)
            for u in range(2):
                dve.sem_inc(s_cast3[u], CAST3_CREDIT)

            def merge_halves(to, stats, tmp):
                m0, m1, v0, v1 = (stats[:, :, c] for c in (1, 4, 2, 5))
                V.tensor_tensor(tmp[:, 0, :], m0, m1, ALU.add)
                V.tensor_tensor(tmp[:, 1, :], m0, m1, ALU.subtract)
                chain.link(V.tensor_tensor(tmp[:, 2, :], v0, v1, ALU.add))
                V.tensor_scalar(to[:, :, 0], tmp[:, 0, :], 0.5, None, ALU.mult)
                chain.link(V.scalar_tensor_tensor(out=tmp[:, 3, :], in0=tmp[:, 1, :], scalar=0.25,
                                                  in1=tmp[:, 1, :], op0=ALU.mult, op1=ALU.mult))
                return V.scalar_tensor_tensor(out=to[:, :, 1], in0=tmp[:, 2, :], scalar=1.0 / D,
                                              in1=tmp[:, 3, :], op0=ALU.mult, op1=ALU.add)

            V.memset(eps_t[:, :], EPS)
            V.memset(b_pad[:, :], 0.0)
            for u in range(2):
                V.memset(hT[u][:, 0:2], 0.0)
            V.memset(zero3[:, :], 0.0)
            dve.wait_ge(s_params, 16 * 8)
            V.tensor_copy(ident_b[:, :], ident)
            V.tensor_copy(mask_q[:, :], cst[:, C_MASKQ:C_MASKQ + P])
            V.tensor_copy(mask_k[:, :], cst[:, C_MASKK:C_MASKK + P])
            V.tensor_scalar(d_one[:, :], d_one[:, :], 1.0, None, ALU.add)
            V.tensor_copy(c_rep[:, :, :], cw_d[:, :].unsqueeze(1).broadcast_to([P, CH, S]))
            dve.wait_ge(s_set_act, 1)
            V.tensor_scalar(a_rep[:, :, :], lg_d[:, :].unsqueeze(1).broadcast_to([P, CH, S]),
                            RATE_MAX, None, ALU.min)
            V.tensor_scalar(lg_g[:, :], lg_g[:, :], RATE_MAX, None, ALU.min).then_inc(s_set_dve, 1)
            dve.wait_ge(s_set_pe, 2)
            V.tensor_copy(b_pad[:, 112:128], ps[:, 0, 0:S])
            V.tensor_copy(aT[:, :], ps[:, 1, 0:P])
            V.tensor_copy(cT[:, :], ps[:, 1, P:2 * P])
            V.tensor_copy(aG[:, :], ps[:, 2, 0:G])
            V.tensor_copy(cG[:, :], ps[:, 2, G:2 * G]).then_inc(s_set_dve, 1)
            dve.wait_ge(s_set_dve, 2)
            dve.wait_ge(s_set_act, 2)
            V.tensor_tensor(w_state[:, :, :], pu[:, :].unsqueeze(2).broadcast_to([P, D, S]),
                            small[:, 0:S].unsqueeze(1).broadcast_to([P, D, S]), ALU.mult)
            chain.link(V.tensor_tensor(phc[:, :, :], ph[:, :, :],
                                       cG[:, :].unsqueeze(1).broadcast_to([P, CH, G]), ALU.mult))
            for g in range(G):
                V.tensor_tensor(w_carry[:, g, :, :], phc[:, :, g].unsqueeze(2).broadcast_to([P, CH, 8]),
                                small[:, C_DD - C_DS:C_DD - C_DS + 8].unsqueeze(1).broadcast_to([P, CH, 8]),
                                ALU.mult)
            for r in range(CH):
                at = C_CM - C_DS + r
                last = V.scalar_tensor_tensor(
                    out=w_chunk[:, :, r, :], in0=pi[:, r, :].rearrange("p (g e) -> p g e", e=8),
                    scalar=small[:, at:at + 1], in1=cT[:, :].rearrange("p (g e) -> p g e", e=8),
                    op0=ALU.mult, op1=ALU.mult)
            last.then_inc(s_set_dve, 1)
            dve.wait_ge(s_weights, 16 * 10)

            A_CHAIN = 16
            base = chain.n
            with dve.Fori(0, 2) as i:
                chain.base, chain.n = base + A_CHAIN * i, 0
                for u in range(2):
                    dve.wait_ge(s_xtr[u], i + 1)
                    V.tensor_copy(xT[u][:, 4:8, :], ps[:, 4 * u + 1, :].rearrange("p (r c) -> p r c", c=P)
                                  ).then_inc(s_xTd[u], 1)
                for u in range(2):
                    dve.wait_ge(s_bt[u], i + 1)
                    V.tensor_copy(bt[u][:, :], ps[:, 4 * u + 2, 0:P]).then_inc(s_btc[u], 1)
                dve.wait_ge(s_set_pool, 1)
                for u in range(2):
                    dve.wait_ge(s_u[u], i + 1)
                    chain.link(V.tensor_tensor_scan(hs[u][:, 1:G * P + 1], decay[:, :, :].rearrange("p g c -> p (g c)"),
                                                    banks(4 * u, 4), 0.0, ALU.mult, ALU.add))
                    V.memset(hs[u][:, 0:G * P].rearrange("p (g c) -> p g c", c=P)[:, :, 0:1], 0.0
                             ).then_inc(s_scan[u], 1)
                def mixed(u):
                    return banks(4 * u, 2).rearrange("p (g r e) -> p r g e", r=CH, e=8)

                def first_moments(u):
                    dve.wait_ge(s_y[u], i + 1)
                    for r in range(CH):
                        last = V.bn_stats(st[u][:, r, :], mixed(u)[:, r, :, :])
                    chain.link(last)
                    merge_halves(mv[u], st[u], hv[u]).then_inc(s_var[u], 1)

                def normalise_mixed(u):
                    dve.wait_ge(s_sd[u], 2 * i + 1)
                    dve.wait_ge(s_var[u], 2 * i + 1)
                    chain.link(V.reciprocal(sc[u][:, 1, :], sc[u][:, 0, :]))
                    chain.link(V.tensor_tensor(sc[u][:, 2, :], mv[u][:, :, 1], sc[u][:, 1, :], ALU.mult))
                    V.tensor_tensor(sc[u][:, 3, :], sc[u][:, 2, :], sc[u][:, 1, :], ALU.mult
                                    ).then_inc(s_var[u], 1)
                    for r in range(CH):
                        V.tensor_scalar(x1[:, 2 * i + u, r, :].rearrange("p (g e) -> p g e", e=8),
                                        mixed(u)[:, r, :, :],
                                        mv[u][:, r, 0:1], sc[u][:, 1, r:r + 1], ALU.subtract, ALU.mult)
                    dve.wait_ge(s_sd[u], 2 * i + 2)
                    V.reciprocal(sc[u][:, 5, :], sc[u][:, 4, :]).then_inc(s_x1[u], 1)

                def convolve(u):
                    dve.wait_ge(s_hT[u], i + 1)
                    for k in range(3):
                        if k == 0:
                            ins = V.tensor_scalar(hc[u][:, :], hT[u][:, 0:T], vecs[:, 4:5], None, ALU.mult)
                        else:
                            ins = V.scalar_tensor_tensor(out=hc[u][:, :], in0=hT[u][:, k:T + k],
                                                         scalar=vecs[:, 4 + k:5 + k], in1=hc[u][:, :],
                                                         op0=ALU.mult, op1=ALU.add)
                        if k < 2:
                            chain.link(ins)
                        else:
                            ins.then_inc(s_hc[u], 1)

                def turn(u, k):
                    dve.wait_ge(s_qk[u], 2 * i + k + 1)
                    dve.wait_ge(s_cast3[k], 2 * i + u + CAST3_CREDIT)
                    V.tensor_tensor(tq[k][:, :], banks(4 * u, 2), cos[:, :], ALU.mult)
                    V.tensor_tensor(tr[k][:, :], banks(4 * u + 2, 2), sin[:, :], ALU.mult
                                    ).then_inc(s_rope[u], 1)
                    dve.wait_ge(s_rope[u], 2 * i + k + 1 + ROPE_CREDIT)
                    V.tensor_tensor(tq[k][:, :], tq[k][:, :], tr[k][:, :], ALU.add).then_inc(s_sum[k], 1)

                first_moments(0)
                normalise_mixed(0)
                first_moments(1)
                convolve(0)
                normalise_mixed(1)
                turn(0, 0)
                convolve(1)
                turn(0, 1)
                turn(1, 0)
                turn(1, 1)
                assert chain.n == A_CHAIN, chain.n
            chain.base, chain.n = base + 2 * A_CHAIN, 0

            for u in range(2):
                dve.wait_ge(s_hzt[u], 2)
            for g in range(HG):
                if g < 2:
                    V.memset(qs[g][:, :, :].rearrange("p h t -> p (h t)").bitcast(F32), 0.0)
                V.memset(ks[g][:, :, :].rearrange("p h t -> p (h t)").bitcast(F32), ONE_PAIR).then_inc(s_clear, 1)

            def reduce_unit(n, par, idx):
                t, k0, nk, heads, chunk = MAXU[idx]
                dve.wait_ge(s_ms, NMU * n + idx + 1)
                m = len(heads)
                dst = mx[par][:, heads[0]:heads[0] + m, t] if chunk == 0 else \
                    mxb[par][:, heads[0]:heads[0] + m, t - 4]
                V.tensor_reduce(dst, ps[:, 6 + idx % 2, 0:m * nk].rearrange("p (h k) -> p h k", h=m),
                                AX_X, ALU.max).then_inc(s_mr, 1)

            def combine(n, par):
                dve.wait_ge(s_mr, NMU * (n + 1) + MR_CREDIT)
                V.tensor_tensor(mx[par][:, :, 4:8], mx[par][:, :, 4:8], mxb[par][:, :, :], ALU.max
                                ).then_inc(s_mg, 1)

            def normalise(n, b, eg, half):
                dve.wait_ge(s_ot, 2 * n + half + 1 + OT_CREDIT)
                o = ps[:, 5, :].rearrange("p (t h d) -> p t h d", t=4, h=4)
                chain.link(V.reciprocal(rden[half][:, :, :], o[:, :, :, HD]))
                dst = o_all[:, b, 4 * half:4 * half + 4, 32 * eg:32 * eg + 32].rearrange(
                    "p t (h d) -> p t h d", d=HD)
                V.tensor_tensor(dst, o[:, :, :, 0:HD], rden[half][:, :, :].unsqueeze(3).broadcast_to([P, 4, 4, HD]),
                                ALU.mult).then_inc(s_on, 1)

            def step(n, g, b, tail=True):
                for idx in range(NMU):
                    if idx == 0 and tail:
                        dve.wait_ge(s_mt, n - 1)
                    reduce_unit(n, g % 2, idx)
                    if idx == 12 and tail:
                        normalise(n - 2, b, (g + 2) % 4, 0)
                    if idx == 25 and tail:
                        normalise(n - 2, b, (g + 2) % 4, 1)
                combine(n, g % 2)

            step(0, 0, None, tail=False)
            step(1, 1, None, tail=False)
            step(2, 2, 0)
            step(3, 3, 0)
            B_CHAIN = 8
            base = chain.base + chain.n
            with dve.Fori(1, NB) as b:
                chain.base, chain.n = base + B_CHAIN * (b - 1), 0
                for g in range(HG):
                    step(4 * b + g, g, b - 1 if g < 2 else b)
                assert chain.n == B_CHAIN, chain.n
            chain.base, chain.n = base + B_CHAIN * (NB - 1), 0

            def moments(u, signal):
                for r in range(CH):
                    last = V.bn_stats(stc[u][:, r, :], x2[u][:, r, :])
                chain.link(last)
                merge_halves(mvc[u], stc[u], hvc[u]).then_inc(signal, 1)

            def normal(u, signal, slots=CH):
                chain.link(V.reciprocal(scc[u][:, 1, :], scc[u][:, 0, :]))
                if slots < CH:
                    V.scalar_tensor_tensor(out=hvc[u][:, 0, :], in0=mvc[u][:, :, 0], scalar=-1.0,
                                           in1=scc[u][:, 1, :], op0=ALU.mult, op1=ALU.mult).then_inc(s_nb[u], 1)
                for r in range(slots):
                    last = V.tensor_scalar(zz[u][:, r, 0:D], x2[u][:, r, :], mvc[u][:, r, 0:1],
                                           scc[u][:, 1, r:r + 1], ALU.subtract, ALU.mult)
                last.then_inc(signal, 1)

            def add_and_normalise(b):
                u = b % 2
                dve.wait_ge(s_pj, b + 1)
                if b == 0:
                    V.memset(zero8[:, :], 0.0)
                    V.memset(count[:, :], 0.0)
                if b > 1:
                    dve.wait_ge(s_acc, b - 1)
                V.tensor_tensor(x2[u][:, :, :], x1[:, b, :, :],
                                banks(BANK_P[b], 2).rearrange("p (r d) -> p r d", d=D), ALU.add).then_inc(s_x2, 1)
                dve.wait_ge(s_x2, b + 1)
                moments(u, s_varc)
                if b > 1:
                    dve.wait_ge(s_scat[u], 16 * CH * (b // 2))
                V.tensor_copy(zz[u][:, :, D:DI].bitcast(U32),
                              con(C_ID + b * CH, CH).unsqueeze(2))
                dve.wait_ge(s_sdc, b + 1)
                dve.wait_ge(s_varc, b + 1)
                normal(u, s_zz)

            def pick_experts(b):
                dve.wait_ge(s_lg, b + 1)
                lg = ps[:, BANK_L[b], 0:CH * NE].rearrange("p (r e) -> p r e", e=NE)
                chain.link(V.tensor_reduce(lmax[:, :], lg, AX_X, ALU.max))
                chain.link(V.tensor_tensor(pick[:, :, :], lg, lmax[:, :].unsqueeze(2).broadcast_to([P, CH, NE]),
                                           ALU.is_ge))
                chain.link(V.tensor_scalar(left[:, :], pick[:, :, 0], -1.0, 1.0, ALU.mult, ALU.add))
                for e in range(1, NE):
                    chain.link(V.tensor_tensor(pick[:, :, e], pick[:, :, e], left[:, :], ALU.mult))
                    if e < NE - 1:
                        chain.link(V.tensor_tensor(left[:, :], left[:, :], pick[:, :, e], ALU.subtract))
                V.tensor_reduce(rowc[:, :], pick[:, :, :].rearrange("p r e -> p e r"), AX_X, ALU.add
                                ).then_inc(s_rc, 1)
                for e in range(NE):
                    last = V.tensor_tensor_scan(incl[:, :, e], pick[:, :, e], zero8[:, :], 0.0, ALU.add, ALU.add)
                chain.link(last)

            def choose_rows(b):
                dve.wait_ge(s_rp, b + 1)
                chain.link(V.tensor_tensor(offs[:, :], ps[:, BANK_R[b], 0:NE], count[:, :], ALU.add))
                V.tensor_tensor(count[:, :], ps[:, BANK_R[b], NE:2 * NE], count[:, :], ALU.add)
                chain.link(V.tensor_tensor(offs[:, :], offs[:, :], con(C_ER, NE), ALU.add))
                chain.link(V.tensor_tensor(incl[:, :, :], incl[:, :, :],
                                           offs[:, :].unsqueeze(1).broadcast_to([P, CH, NE]), ALU.add))
                chain.link(V.tensor_tensor(incl[:, :, :], incl[:, :, :], pick[:, :, :], ALU.mult))
                chain.link(V.tensor_reduce(rank[:, :], incl[:, :, :], AX_X, ALU.add))
                V.tensor_copy(dest[:, b, :], rank[:, :]).then_inc(s_dest, 1)

            for at in range(AT_END):
                if at in (5, 12, NEU + 5, LAST):
                    n = 4 * NB - 2 if at < NEU else 4 * NB - 1
                    normalise(n, NB - 1, n % 4, 0 if at % NEU == 5 else 1)
                for b in range(NB):
                    if at == AT_P[b]:
                        add_and_normalise(b)
                    if at == AT_L[b]:
                        pick_experts(b)
                    if at == AT_R[b]:
                        choose_rows(b)
                if at == AT_R[2]:
                    chain.link(V.memset(zrow[:, :, :], 0.0))
                    V.tensor_copy(zrow[:, :, D:DI].bitcast(U32), con(C_IDZ, 2 * NE).unsqueeze(2)
                                  ).then_inc(s_zrow, 1)

            V.tensor_tensor(above[:, :, :], count[:, :].unsqueeze(2).broadcast_to([P, NE, NB * KT]),
                            con(C_K, NB * KT).unsqueeze(1).broadcast_to([P, NE, NB * KT]), ALU.is_gt)
            chain.link(V.tensor_scalar(offs[:, :], count[:, :], con(C_P, 1), None, ALU.add))
            V.tensor_reduce(tiles_e[:, :], above[:, :, :], AX_X, ALU.add)
            chain.link(V.tensor_tensor(last_row[:, :], offs[:, :], con(C_ER, NE), ALU.add))
            chain.link(V.tensor_scalar(tail[:, :], last_row[:, :], 1.0, None, ALU.add))
            chain.link(V.tensor_copy(cum_e[:, :], tiles_e[:, :]))
            for e in range(1, NE):
                chain.link(V.tensor_tensor(cum_e[:, e:e + 1], cum_e[:, e:e + 1], cum_e[:, e - 1:e], ALU.add))
            V.tensor_scalar(jump_e[:, :], tiles_e[:, :], -float(P), float(REGION), ALU.mult, ALU.add)
            chain.link(V.tensor_tensor(past[:, :, :], con(C_TI, TILES).unsqueeze(2).broadcast_to([P, TILES, NE]),
                                       cum_e[:, :].unsqueeze(1).broadcast_to([P, TILES, NE]), ALU.is_ge))
            chain.link(V.tensor_tensor(past_j[:, :, :], past[:, :, :],
                                       jump_e[:, :].unsqueeze(1).broadcast_to([P, TILES, NE]), ALU.mult))
            V.tensor_reduce(tile_f[:, 0, :], past[:, :, :], AX_X, ALU.add)
            chain.link(V.tensor_reduce(tile_f[:, 1, :], past_j[:, :, :], AX_X, ALU.add))
            V.tensor_scalar(tile_expert[:, :], tile_f[:, 0, :], float(NE - 1), None, ALU.min)
            V.scalar_tensor_tensor(out=tile_row[:, :], in0=con(C_TI, TILES), scalar=float(P), in1=tile_f[:, 1, :],
                                   op0=ALU.mult, op1=ALU.add).then_inc(s_plan, 1)

            def weigh_values(k, s2, first=False):
                dve.wait_ge(s_gv, 2 * k + 2)
                dve.wait_ge(s_sg, k + 1)
                if not first:
                    dve.wait_ge(s_aT, k - 1)
                V.tensor_tensor(act_v[s2][:, :], ps[:, 2 * s2 + 1, :], gate[s2][:, :], ALU.mult
                                ).then_inc(s_av, 1)

            def keep_numbers(k, s4, first=False):
                dve.wait_ge(s_hrow[s4], tile_turn(k, s4))
                if not first:
                    dve.wait_ge(s_yst[s4], tile_turn(k, s4) - 16)
                V.tensor_copy(y_id[s4][:, :], h_row[s4][:, D:DI].bitcast(U32)).then_inc(s_id, 1)

            def copy_y(k, s4, first=False):
                dve.wait_ge(s_yy, k + 1)
                if not first:
                    dve.wait_ge(s_yst[s4], tile_turn(k, s4) - 16)
                V.tensor_copy(y_row[s4][:, :], ps[:, 7, 0:D]).then_inc(s_yr, 1)

            for k in range(8):
                weigh_values(k, k % 2, first=(k < 2))
                keep_numbers(k, k % 4, first=(k < 4))
                if k > 1:
                    copy_y(k - 2, (k - 2) % 4, first=(k - 2 < 4))
            with dve.Fori(2, TILES // 4) as m:
                for j in range(4):
                    weigh_values(4 * m + j, j % 2)
                    keep_numbers(4 * m + j, j)
                    copy_y(4 * m + j - 2, (j + 2) % 4)
            copy_y(TILES - 2, 2)
            copy_y(TILES - 1, 3)

            F_CHAIN = 8
            base = chain.base + chain.n
            with dve.Fori(0, 2) as i:
                chain.base, chain.n = base + F_CHAIN * i, 0
                for u in range(2):
                    dve.wait_ge(s_resa[u], i + RES_CREDIT)
                    dve.wait_ge(s_fin[u], i + 1)
                    moments(u, s_varf[u])
                    dve.wait_ge(s_out[u], 16 * i + OUT_CREDIT)
                    dve.wait_ge(s_sdf[u], i + 1)
                    dve.wait_ge(s_varf[u], i + 1)
                    normal(u, s_res[u], CH // 2)
                assert chain.n == F_CHAIN, chain.n

        @block.gpsimd
        def _(pool):
            G_ = nc.gpsimd
            for u in range(2):
                pool.sem_inc(s_out[u], OUT_CREDIT)
                pool.sem_inc(s_res[u], RES_CREDIT)
                pool.sem_inc(s_resa[u], RES_CREDIT)
            G_.memset(ones[:, :], 1.0).then_inc(s_pool, 1)
            G_.memset(v_all[:, :, :, :, :].rearrange("p b t h c -> p (b t h c)"), 1.0).then_inc(s_pool, 1)
            pool.wait_ge(s_weights, 16 * 10)
            for k in range(2):
                w = w_qkv[:, k * D:(k + 1) * D].rearrange("c (h a d) -> c a d h", a=2, d=HD // 2)
                r = w_rot[:, k * D:(k + 1) * D].rearrange("c (a d h) -> c a d h", a=2, h=NH)
                G_.tensor_copy(r[:, 0, :, :], w[:, 1, :, :])
                G_.tensor_copy(r[:, 1, :, :], w[:, 0, :, :])
                G_.tensor_copy(w_qk[:, k * D:(k + 1) * D].rearrange("c (d h) -> c d h", h=NH),
                               w_qkv[:, k * D:(k + 1) * D].rearrange("c (h d) -> c d h", d=HD))
            pool.wait_ge(s_set_act, 2)
            G_.tensor_copy(decay[:, :, :], ph[:, CH - 1, :].unsqueeze(2).broadcast_to([P, G, P])
                           ).then_inc(s_pool, 1)
            pool.wait_ge(s_pool, 3)
            G_.memset(decay[:, :, 0:1], 0.0).then_inc(s_set_pool, 1)

            with pool.Fori(0, 2) as i:
                for u in range(2):
                    pool.wait_ge(s_xtr[u], i + 1)
                    G_.tensor_tensor(xt[u][:, :, :], xt[u][:, :, :], d_one[:, :].unsqueeze(1).broadcast_to([P, CH, D]),
                                     ALU.mult).then_inc(s_xd[u], 1)
                for u in range(2):
                    pool.wait_ge(s_x1[u], i + 1)
                    G_.tensor_tensor(hz[u][:, :, :], x1[:, 2 * i + u, :, :],
                                     sc[u][:, 5, :].unsqueeze(2).broadcast_to([P, CH, D]), ALU.mult
                                     ).then_inc(s_hz[u], 1)
                for u in range(2):
                    m = 2 * i + u
                    for k in range(2):
                        pool.wait_ge(s_sum[k], m + 1)
                        pool.wait_ge(s_cast1[k], m + 1)
                        G_.tensor_tensor(tr[k][:, :], tq[k][:, :], part[k][0][:, :], ALU.subtract
                                         ).then_inc(s_rest1[k], 1)
                        pool.wait_ge(s_rest1[k], m + 1)
                        pool.wait_ge(s_cast2[k], m + 1)
                        G_.tensor_tensor(part[k][2][:, :], tr[k][:, :], part[k][1][:, :], ALU.subtract
                                         ).then_inc(s_cast3[k], 1)

            for u in range(2):
                pool.wait_ge(s_hzt[u], 2)
            for g in range(2, HG):
                G_.memset(qs[g][:, :, :].rearrange("p h t -> p (h t)").bitcast(F32), 0.0).then_inc(s_qclear, 1)
            for u in range(2):
                pool.wait_ge(s_stored[u], 16 * 3 * NB + STORED_CREDIT)
                pool.wait_ge(s_vc[u], 2 + VC_CREDIT)
            for n in range(2):
                G_.memset(vs[n][:, :, :, :].rearrange("p t h c -> p (t h c)"), 0.0).then_inc(s_vclear, 1)

            def values(n, b, g):
                pool.wait_ge(s_vclear, 2)
                G_.tensor_copy(vs[g % 2][:, :, :, 0:VC], v_all[:, b, :, 4 * g:4 * g + 4, :]
                               ).then_inc(s_vst, 1)

            def max_parts(n, first=False):
                pool.wait_ge(s_mn, n + 1)
                if not first:
                    pool.wait_ge(s_mrow, MROW * n)
                G_.tensor_tensor(m_part[0][:, :], m_neg[:, :], ones[:, :], ALU.mult).then_inc(s_mpc, 1)
                pool.wait_ge(s_mpc, 3 * n + 1)
                G_.tensor_tensor(m_res[:, :], m_neg[:, :], m_part[0][:, :], ALU.subtract).then_inc(s_mpc, 1)
                pool.wait_ge(s_mpc, 3 * n + 2)
                G_.tensor_tensor(m_part[1][:, :], m_res[:, :], ones[:, :], ALU.mult).then_inc(s_mpc, 1)
                pool.wait_ge(s_mpc, 3 * n + 3)
                G_.tensor_tensor(m_part[2][:, :], m_res[:, :], m_part[1][:, :], ALU.subtract).then_inc(s_mp, 1)

            values(0, 0, 0)
            values(1, 0, 1)
            for g in range(HG):
                if g >= 2:
                    pool.wait_ge(s_pv, NEU * (g - 1) + PV_CREDIT)
                    values(g, 0, g)
                max_parts(g, first=(g == 0))
            with pool.Fori(1, NB) as b:
                for g in range(HG):
                    n = 4 * b + g
                    pool.wait_ge(s_pv, NEU * (n - 1) + PV_CREDIT)
                    values(n, b, g)
                    max_parts(n)

            for b in range(NB):
                if b > 0:
                    pool.wait_ge(s_x2, b)
                    G_.tensor_tensor(x1[:, b - 1, :, :], x1[:, b - 1, :, :], x2[(b - 1) % 2][:, :, :], ALU.add
                                     ).then_inc(s_acc, 1)
                pool.wait_ge(s_dest, b + 1)
                pool.wait_ge(s_zz, b + 1)
                for r in range(CH):
                    G_.indirect_dma_start(
                        out=h_sorted, out_offset=bass.IndirectOffsetOnAxis(ap=dest[:, b, r:r + 1], axis=0),
                        in_=zz[b % 2][:, r, :], in_offset=None).then_inc(s_scat[b % 2], 16)
            pool.wait_ge(s_x2, NB)
            G_.tensor_tensor(x1[:, NB - 1, :, :], x1[:, NB - 1, :, :], x2[(NB - 1) % 2][:, :, :], ALU.add
                             ).then_inc(s_acc, 1)

            def scatter_tile(k, s4):
                pool.wait_ge(s_id, k + 1)
                pool.wait_ge(s_yr, k + 1)
                pool.sem_inc(s_ysc, 1)
                G_.indirect_dma_start(out=y_rows, out_offset=bass.IndirectOffsetOnAxis(ap=y_id[s4][:, 0:1], axis=0),
                                      in_=y_row[s4][:, :], in_offset=None).then_inc(s_yst[s4], 16)

            with pool.Fori(0, TILES // 4) as m:
                for j in range(4):
                    scatter_tile(4 * m + j, j)

            pool.wait_ge(s_acc, NB)
            with pool.Fori(0, 2) as i:
                for u in range(2):
                    pool.wait_ge(s_yg[u], 16 * (i + 1))
                    pool.wait_ge(s_res[u], i + RES_CREDIT)
                    pool.wait_ge(s_resa[u], i + RES_CREDIT)
                    G_.tensor_tensor(x2[u][:, :, :], yg[:, 2 * i + u, :, :], x1[:, 2 * i + u, :, :], ALU.add
                                     ).then_inc(s_fin[u], 1)



_INS = ["L0_attn_x", "L0_attn_log_A_diag", "L0_attn_B_w", "L0_attn_C_w", "L0_attn_D_vec", "L0_ffn_ln1_w",
        "L0_ffn_ln1_b", "L0_ffn_ln2_w", "L0_ffn_ln2_b", "L0_ffn_conv_w", "L0_ffn_attn_w", "L0_ffn_proj_w",
        "L0_ffn_router_w", "L0_ffn_expert_wv", "L0_ffn_expert_proj"]
_OUTS = [((NB, T, D), "float32")]


def kernel(**inputs):
    import numpy as _np
    import concourse.bacc as _bacc
    from concourse import mybir as _mybir
    from concourse.bass_utils import run_bass_kernel_spmd as _run

    nc = _bacc.Bacc("TRN2", target_bir_lowering=False, num_devices=1)
    arrays, args = {}, []
    for name, a in [("constants", constants())] + [(n, inputs[n]) for n in _INS]:
        a = _np.ascontiguousarray(a)
        arrays[f"in_{name}_dram"] = a
        args.append(nc.dram_tensor(f"in_{name}_dram", a.shape, _mybir.dt.from_np(a.dtype), kind="ExternalInput").ap())
    for i, (shape, dtype) in enumerate(_OUTS):
        dt = _mybir.dt.from_np(_np.dtype(dtype))
        args.append(nc.dram_tensor(f"out_{i}_dram", shape, dt, kind="ExternalOutput").ap())
    layer_kernel(nc, *args)
    r = _run(nc, [arrays], core_ids=[0])
    return r.results[0]["out_0_dram"]
```
